# Optimizing a Trainium2 kernel written in Bass

```python
import numpy as np
import jax
import jax.numpy as jnp

def _softmax(x, axis=-1):
    return jax.nn.softmax(x, axis=axis)

def _gelu(x):
    return jax.nn.gelu(x, approximate=True)

def _silu(x):
    return jax.nn.silu(x)

def _sigmoid(x):
    return jax.nn.sigmoid(x)

def _layernorm(x, axis=-1, eps=1e-05):
    m = jnp.mean(x, axis=axis, keepdims=True)
    v = jnp.var(x, axis=axis, keepdims=True)
    return (x - m) / jnp.sqrt(v + eps)

def _scatter_add(tgt, idx, src, axis=0):
    return tgt.at[idx].add(src)

def _segment_sum(src, seg, n):
    return jax.ops.segment_sum(src, seg, n)
kernel_name = 'mk_decoder_postln_d2_seqx_r4_7ba8ce'

def setup_inputs(seed: int=0):
    np.random.seed(seed)
    _w = jnp.asarray

    def _rec_inputs():
        import jax
        import jax.numpy as jnp
        _rk = jax.random.key(seed)
        x = -0.0003929 + 0.9999 * jax.random.normal(jax.random.fold_in(_rk, 1), (4, 512, 256), jnp.float32)
        _lenS = 512 - jax.random.randint(jax.random.fold_in(_rk, 7), (4,), 0, max(1, 512 // 4) + 1, jnp.int32)
        _lenS2 = 512 - jax.random.randint(jax.random.fold_in(_rk, 8), (4,), 0, max(1, 512 // 4) + 1, jnp.int32)
        _ctx_1024P = jax.random.normal(jax.random.fold_in(_rk, 11), (4, 16, 256), jnp.float32)
        _ctx_1024c = jax.random.dirichlet(jax.random.fold_in(_rk, 511), 0.3 * jnp.ones((16,), jnp.float32), (4, 512))
        _ctx_1024t = jnp.einsum('bsk,bkd->bsd', _ctx_1024c, _ctx_1024P)
        _ctx_1024t = _ctx_1024t * jax.lax.rsqrt(jnp.mean(jnp.square(_ctx_1024t)) + 1e-12) * 0.953939
        ctx_1024 = 4.13588e-05 + 0.999923 * (_ctx_1024t + 0.3 * jax.random.normal(jax.random.fold_in(_rk, 611), (4, 512, 256), jnp.float32))
        return (x, ctx_1024)
    x, ctx_1024 = _rec_inputs()

    def _L0_attn_setup():
        import jax, jax.numpy as jnp
        import numpy as np
        _A = np.array([[1, 1, 1, 0, 1, 1, 1, 0, 0, 0, 1, 1], [1, 1, 0, 1, 1, 1, 0, 0, 0, 1, 1, 0], [1, 0, 1, 1, 1, 0, 0, 0, 1, 1, 0, 1], [0, 1, 1, 1, 0, 0, 0, 1, 1, 0, 1, 1], [0, 0, 0, 0, 1, 1, 1, 1, 1, 1, 1, 1], [1, 1, 1, 1, 0, 0, 0, 0, 0, 0, 0, 0], [0, 0, 0, 0, 1, 1, 1, 1, 0, 0, 0, 0], [1, 1, 0, 0, 1, 1, 0, 0, 1, 1, 0, 0], [1, 0, 1, 0, 1, 0, 1, 0, 1, 0, 1, 0], [0, 1, 0, 1, 0, 1, 0, 1, 0, 1, 0, 1], [1, 0, 0, 1, 1, 0, 0, 1, 1, 0, 0, 1], [0, 1, 1, 0, 0, 1, 1, 0, 0, 1, 1, 0]], dtype=np.float32)
        _H = jnp.asarray(np.concatenate([_A.T, np.eye(12, dtype=np.float32)], axis=1))

        def _fractal_dimension(x):
            s = x.reshape(-1)
            sn = (s - s.min()) / (s.max() - s.min() + 1e-10)
            counts = []
            for sc in (2, 4, 8, 16, 32):
                blk = sn[:sc * sc]
                counts.append(jnp.maximum(jnp.sum(blk > blk.mean()).astype(jnp.float32), 1.0))
            lx = jnp.log(jnp.array([2.0, 4.0, 8.0, 16.0, 32.0], dtype=jnp.float32))
            ly = jnp.log(jnp.stack(counts))
            n = jnp.float32(5.0)
            num = n * jnp.sum(lx * ly) - jnp.sum(lx) * jnp.sum(ly)
            den = n * jnp.sum(lx * lx) - jnp.sum(lx) ** 2
            return jnp.clip(-num / den, 1.0, 2.0)

        def _wave_filter(D, d):
            k = jnp.fft.fftfreq(d).astype(jnp.float32)
            ka = jnp.abs(k) + 1e-08
            omega = 1.0 + 0.2 * D
            a = 1.0 + 0.5 * D
            b = 0.1 * D
            real = jnp.sin(omega * D + a * ka)
            phase = omega * D - ka + b * ka ** 2
            return real * jnp.exp(1j * phase)

        def _golay_correct(bits):
            syn = (bits @ _H.T > 0.5).astype(jnp.float32)
            w = syn.sum(-1)
            _, idx = jax.lax.top_k(syn, 3)
            take = (jnp.arange(3)[None, :] < jnp.minimum(w, 3.0)[:, None]).astype(jnp.float32)
            pattern = (jax.nn.one_hot(idx, 24, dtype=jnp.float32) * take[..., None]).sum(axis=1)
            do_fix = ((w > 0) & (w <= 3))[:, None]
            return jnp.where(do_fix, jnp.mod(bits + pattern, 2.0), bits)
        key = jax.random.key(seed)
        k1, k2, k3 = jax.random.split(key, 3)
        B, S, E = (8, 512, 256)
        x = jax.random.normal(k1, (B, S, E), dtype=jnp.float32)
        W_el = jax.random.normal(k2, (E, 24), dtype=jnp.float32) * 0.02
        b_el = jnp.zeros((24,), dtype=jnp.float32)
        W_le = jax.random.normal(k3, (24, E), dtype=jnp.float32) * 0.02
        b_le = jnp.zeros((E,), dtype=jnp.float32)
        return {'x': x, 'W_el': W_el, 'b_el': b_el, 'W_le': W_le, 'b_le': b_le}
    _L0_attn_all = _L0_attn_setup()
    _L0_attn_in = {k: v for k, v in _L0_attn_all.items() if k in ('W_el', 'b_el', 'W_le', 'b_le')}
    del _L0_attn_all

    def _L0_xattn_setup():
        import jax, jax.numpy as jnp
        import numpy as np
        H = 256
        B = 8
        L_CHAR = 512
        L_SUB = 256

        def _linear(x, W, b):
            return jnp.einsum('blh,oh->blo', x, W) + b

        def _interp_linear(x, out_len):
            L_in = x.shape[1]
            pos = (jnp.arange(out_len, dtype=x.dtype) + 0.5) * (L_in / out_len) - 0.5
            pos = jnp.clip(pos, 0.0, L_in - 1)
            lo = jnp.floor(pos).astype(jnp.int32)
            hi = jnp.minimum(lo + 1, L_in - 1)
            w = (pos - lo.astype(x.dtype))[None, :, None]
            return x[:, lo] * (1 - w) + x[:, hi] * w
        key = jax.random.key(seed)
        ks = jax.random.split(key, 18)
        s = 0.02
        inp = {'char_emb': jax.random.normal(ks[0], (B, L_CHAR, H), jnp.float32), 'subword_emb': jax.random.normal(ks[1], (B, L_SUB, H), jnp.float32)}
        names = ['Wq_c', 'Wk_s', 'Wv_s', 'Wq_s', 'Wk_c', 'Wv_c']
        for i, n in enumerate(names):
            inp[n] = jax.random.normal(ks[2 + 2 * i], (H, H), jnp.float32) * s
            inp['b' + n[1:]] = jax.random.normal(ks[3 + 2 * i], (H,), jnp.float32) * s
        inp['Wg'] = jax.random.normal(ks[14], (H, 2 * H), jnp.float32) * s
        inp['bg'] = jax.random.normal(ks[15], (H,), jnp.float32) * s
        return inp
    _L0_xattn_all = _L0_xattn_setup()
    _L0_xattn_in = {k: v for k, v in _L0_xattn_all.items() if k in ('Wq_c', 'bq_c', 'Wk_s', 'bk_s', 'Wv_s', 'bv_s', 'Wq_s', 'bq_s', 'Wk_c', 'bk_c', 'Wv_c', 'bv_c', 'Wg', 'bg')}
    del _L0_xattn_all

    def _L0_ffn_setup():
        import jax, jax.numpy as jnp
        import numpy as np
        S, B, D, E, C, FF = (512, 4, 256, 8, 512, 1024)
        N = S * B
        key = jax.random.key(seed)
        ks = jax.random.split(key, 7)
        return {'hidden_states': jax.random.normal(ks[0], (S, B, D), dtype=jnp.float32), 'combine_weights': jax.random.uniform(ks[1], (N, E), dtype=jnp.float32), 'top_idx': jax.random.randint(ks[2], (C, E), 0, N, dtype=jnp.int64), 'W1': jax.random.normal(ks[3], (E, D, FF), dtype=jnp.float32) * (1.0 / np.sqrt(D)), 'b1': jnp.zeros((E, FF), dtype=jnp.float32), 'W2': jax.random.normal(ks[4], (E, FF, D), dtype=jnp.float32) * (1.0 / np.sqrt(FF)), 'b2': jnp.zeros((E, D), dtype=jnp.float32)}
    _L0_ffn_all = _L0_ffn_setup()
    _L0_ffn_in = {k: v for k, v in _L0_ffn_all.items() if k in ('combine_weights', 'top_idx', 'W1', 'b1', 'W2', 'b2')}
    del _L0_ffn_all

    def _L1_attn_setup():
        import jax, jax.numpy as jnp
        import numpy as np
        B, S, D, H = (4, 512, 256, 16)

        def _apply_rope(x):
            b, s, d = x.shape
            half = d // 2
            freq = jnp.exp(jnp.arange(0, d, 2, dtype=jnp.float32) * (-np.log(10000.0) / d))
            ang = jnp.arange(s, dtype=jnp.float32)[:, None] * freq[None, :]
            cos, sin = (jnp.cos(ang), jnp.sin(ang))
            x1, x2 = (x[..., :half], x[..., half:])
            return jnp.concatenate([x1 * cos - x2 * sin, x1 * sin + x2 * cos], axis=-1)
        key = jax.random.key(seed)
        ks = jax.random.split(key, 9)
        scale = 0.02
        x = jax.random.normal(ks[0], (B, S, D), dtype=jnp.float32)
        Wq = jax.random.normal(ks[1], (D, D), dtype=jnp.float32) * scale
        bq = jax.random.normal(ks[2], (D,), dtype=jnp.float32) * scale
        Wk = jax.random.normal(ks[3], (D, D), dtype=jnp.float32) * scale
        bk = jax.random.normal(ks[4], (D,), dtype=jnp.float32) * scale
        Wv = jax.random.normal(ks[5], (D, D), dtype=jnp.float32) * scale
        bv = jax.random.normal(ks[6], (D,), dtype=jnp.float32) * scale
        Wo = jax.random.normal(ks[7], (D, D), dtype=jnp.float32) * scale
        bo = jax.random.normal(ks[8], (D,), dtype=jnp.float32) * scale
        return {'x': x, 'Wq': Wq, 'bq': bq, 'Wk': Wk, 'bk': bk, 'Wv': Wv, 'bv': bv, 'Wo': Wo, 'bo': bo}
    _L1_attn_all = _L1_attn_setup()
    _L1_attn_in = {k: v for k, v in _L1_attn_all.items() if k in ('Wq', 'bq', 'Wk', 'bk', 'Wv', 'bv', 'Wo', 'bo')}
    del _L1_attn_all

    def _L1_xattn_setup():
        import jax, jax.numpy as jnp
        import numpy as np
        B, N, D_MODEL, H, DH = (2, 512, 256, 16, 64)
        SCALE = DH ** (-0.5)
        key = jax.random.key(seed)
        ks = jax.random.split(key, 6)

        def lin(k, fan_in, shape):
            return jax.random.normal(k, shape, dtype=jnp.float32) / np.sqrt(fan_in)
        return {'x': jax.random.normal(ks[0], (B, N, D_MODEL), dtype=jnp.float32), 'context': jax.random.normal(ks[1], (B, N, D_MODEL), dtype=jnp.float32), 'Wq': lin(ks[2], D_MODEL, (D_MODEL, H * DH)), 'Wk': lin(ks[3], D_MODEL, (D_MODEL, H * DH)), 'Wv': lin(ks[4], D_MODEL, (D_MODEL, H * DH)), 'Wo': lin(ks[5], H * DH, (H * DH, D_MODEL)), 'bo': jnp.zeros((D_MODEL,), dtype=jnp.float32)}
    _L1_xattn_all = _L1_xattn_setup()
    _L1_xattn_in = {k: v for k, v in _L1_xattn_all.items() if k in ('Wq', 'Wk', 'Wv', 'Wo', 'bo')}
    del _L1_xattn_all

    def _L1_ffn_setup():
        import jax, jax.numpy as jnp
        import numpy as np
        TOP_K = 8
        NUM_EXPERTS = 32
        CAPACITY = 256
        key = jax.random.key(seed)
        k1, k2, k3, k4 = jax.random.split(key, 4)
        B, S, H, E, F = (2, 256, 256, NUM_EXPERTS, 192)
        return {'hidden_states': jax.random.normal(k1, (B, S, H), dtype=jnp.float32), 'gate_weight': jax.random.normal(k2, (E, H), dtype=jnp.float32) * 0.02, 'gate_up_proj': jax.random.normal(k3, (E, 2 * F, H), dtype=jnp.float32) * 0.02, 'down_proj': jax.random.normal(k4, (E, H, F), dtype=jnp.float32) * 0.02}
    _L1_ffn_all = _L1_ffn_setup()
    _L1_ffn_in = {k: v for k, v in _L1_ffn_all.items() if k in ('gate_weight', 'gate_up_proj', 'down_proj')}
    del _L1_ffn_all
    return {'x': x, 'ctx_1024': ctx_1024, 'L0_attn_W_el': _L0_attn_in['W_el'], 'L0_attn_b_el': _L0_attn_in['b_el'], 'L0_attn_W_le': _L0_attn_in['W_le'], 'L0_attn_b_le': _L0_attn_in['b_le'], 'L0_xattn_Wq_c': _L0_xattn_in['Wq_c'], 'L0_xattn_bq_c': _L0_xattn_in['bq_c'], 'L0_xattn_Wk_s': _L0_xattn_in['Wk_s'], 'L0_xattn_bk_s': _L0_xattn_in['bk_s'], 'L0_xattn_Wv_s': _L0_xattn_in['Wv_s'], 'L0_xattn_bv_s': _L0_xattn_in['bv_s'], 'L0_xattn_Wq_s': _L0_xattn_in['Wq_s'], 'L0_xattn_bq_s': _L0_xattn_in['bq_s'], 'L0_xattn_Wk_c': _L0_xattn_in['Wk_c'], 'L0_xattn_bk_c': _L0_xattn_in['bk_c'], 'L0_xattn_Wv_c': _L0_xattn_in['Wv_c'], 'L0_xattn_bv_c': _L0_xattn_in['bv_c'], 'L0_xattn_Wg': _L0_xattn_in['Wg'], 'L0_xattn_bg': _L0_xattn_in['bg'], 'L0_ffn_combine_weights': _L0_ffn_in['combine_weights'], 'L0_ffn_top_idx': _L0_ffn_in['top_idx'], 'L0_ffn_W1': _L0_ffn_in['W1'], 'L0_ffn_b1': _L0_ffn_in['b1'], 'L0_ffn_W2': _L0_ffn_in['W2'], 'L0_ffn_b2': _L0_ffn_in['b2'], 'L1_attn_Wq': _L1_attn_in['Wq'], 'L1_attn_bq': _L1_attn_in['bq'], 'L1_attn_Wk': _L1_attn_in['Wk'], 'L1_attn_bk': _L1_attn_in['bk'], 'L1_attn_Wv': _L1_attn_in['Wv'], 'L1_attn_bv': _L1_attn_in['bv'], 'L1_attn_Wo': _L1_attn_in['Wo'], 'L1_attn_bo': _L1_attn_in['bo'], 'L1_xattn_Wq': _L1_xattn_in['Wq'], 'L1_xattn_Wk': _L1_xattn_in['Wk'], 'L1_xattn_Wv': _L1_xattn_in['Wv'], 'L1_xattn_Wo': _L1_xattn_in['Wo'], 'L1_xattn_bo': _L1_xattn_in['bo'], 'L1_ffn_gate_weight': _L1_ffn_in['gate_weight'], 'L1_ffn_gate_up_proj': _L1_ffn_in['gate_up_proj'], 'L1_ffn_down_proj': _L1_ffn_in['down_proj']}

def reference(x, ctx_1024, L0_attn_W_el, L0_attn_b_el, L0_attn_W_le, L0_attn_b_le, L0_xattn_Wq_c, L0_xattn_bq_c, L0_xattn_Wk_s, L0_xattn_bk_s, L0_xattn_Wv_s, L0_xattn_bv_s, L0_xattn_Wq_s, L0_xattn_bq_s, L0_xattn_Wk_c, L0_xattn_bk_c, L0_xattn_Wv_c, L0_xattn_bv_c, L0_xattn_Wg, L0_xattn_bg, L0_ffn_combine_weights, L0_ffn_top_idx, L0_ffn_W1, L0_ffn_b1, L0_ffn_W2, L0_ffn_b2, L1_attn_Wq, L1_attn_bq, L1_attn_Wk, L1_attn_bk, L1_attn_Wv, L1_attn_bv, L1_attn_Wo, L1_attn_bo, L1_xattn_Wq, L1_xattn_Wk, L1_xattn_Wv, L1_xattn_Wo, L1_xattn_bo, L1_ffn_gate_weight, L1_ffn_gate_up_proj, L1_ffn_down_proj):
    import jax
    import jax.numpy as jnp

    def _L0_attn_ref(x, W_el, b_el, W_le, b_le):
        import jax, jax.numpy as jnp
        import numpy as np
        _A = np.array([[1, 1, 1, 0, 1, 1, 1, 0, 0, 0, 1, 1], [1, 1, 0, 1, 1, 1, 0, 0, 0, 1, 1, 0], [1, 0, 1, 1, 1, 0, 0, 0, 1, 1, 0, 1], [0, 1, 1, 1, 0, 0, 0, 1, 1, 0, 1, 1], [0, 0, 0, 0, 1, 1, 1, 1, 1, 1, 1, 1], [1, 1, 1, 1, 0, 0, 0, 0, 0, 0, 0, 0], [0, 0, 0, 0, 1, 1, 1, 1, 0, 0, 0, 0], [1, 1, 0, 0, 1, 1, 0, 0, 1, 1, 0, 0], [1, 0, 1, 0, 1, 0, 1, 0, 1, 0, 1, 0], [0, 1, 0, 1, 0, 1, 0, 1, 0, 1, 0, 1], [1, 0, 0, 1, 1, 0, 0, 1, 1, 0, 0, 1], [0, 1, 1, 0, 0, 1, 1, 0, 0, 1, 1, 0]], dtype=np.float32)
        _H = jnp.asarray(np.concatenate([_A.T, np.eye(12, dtype=np.float32)], axis=1))

        def _fractal_dimension(x):
            s = x.reshape(-1)
            sn = (s - s.min()) / (s.max() - s.min() + 1e-10)
            counts = []
            for sc in (2, 4, 8, 16, 32):
                blk = sn[:sc * sc]
                counts.append(jnp.maximum(jnp.sum(blk > blk.mean()).astype(jnp.float32), 1.0))
            lx = jnp.log(jnp.array([2.0, 4.0, 8.0, 16.0, 32.0], dtype=jnp.float32))
            ly = jnp.log(jnp.stack(counts))
            n = jnp.float32(5.0)
            num = n * jnp.sum(lx * ly) - jnp.sum(lx) * jnp.sum(ly)
            den = n * jnp.sum(lx * lx) - jnp.sum(lx) ** 2
            return jnp.clip(-num / den, 1.0, 2.0)

        def _wave_filter(D, d):
            k = jnp.fft.fftfreq(d).astype(jnp.float32)
            ka = jnp.abs(k) + 1e-08
            omega = 1.0 + 0.2 * D
            a = 1.0 + 0.5 * D
            b = 0.1 * D
            real = jnp.sin(omega * D + a * ka)
            phase = omega * D - ka + b * ka ** 2
            return real * jnp.exp(1j * phase)

        def _golay_correct(bits):
            syn = (bits @ _H.T > 0.5).astype(jnp.float32)
            w = syn.sum(-1)
            _, idx = jax.lax.top_k(syn, 3)
            take = (jnp.arange(3)[None, :] < jnp.minimum(w, 3.0)[:, None]).astype(jnp.float32)
            pattern = (jax.nn.one_hot(idx, 24, dtype=jnp.float32) * take[..., None]).sum(axis=1)
            do_fix = ((w > 0) & (w <= 3))[:, None]
            return jnp.where(do_fix, jnp.mod(bits + pattern, 2.0), bits)
        B, S, E = x.shape
        D = _fractal_dimension(x)
        filt = _wave_filter(D, E)
        x1 = jnp.fft.ifft(jnp.fft.fft(x, axis=-1) * filt, axis=-1).real.astype(x.dtype)
        lat = x1 @ W_el + b_el
        bits = (jax.nn.sigmoid(lat) > 0.5).astype(jnp.float32).reshape(B * S, 24)
        corrected = _golay_correct(bits).reshape(B, S, 24)
        return x1 + corrected @ W_le + b_le

    def _L0_xattn_ref(char_emb, subword_emb, Wq_c, bq_c, Wk_s, bk_s, Wv_s, bv_s, Wq_s, bq_s, Wk_c, bk_c, Wv_c, bv_c, Wg, bg):
        import jax, jax.numpy as jnp
        import numpy as np
        H = 256
        B = 8
        L_CHAR = 512
        L_SUB = 256

        def _linear(x, W, b):
            return jnp.einsum('blh,oh->blo', x, W) + b

        def _interp_linear(x, out_len):
            L_in = x.shape[1]
            pos = (jnp.arange(out_len, dtype=x.dtype) + 0.5) * (L_in / out_len) - 0.5
            pos = jnp.clip(pos, 0.0, L_in - 1)
            lo = jnp.floor(pos).astype(jnp.int32)
            hi = jnp.minimum(lo + 1, L_in - 1)
            w = (pos - lo.astype(x.dtype))[None, :, None]
            return x[:, lo] * (1 - w) + x[:, hi] * w
        h = char_emb.shape[-1]
        scale = 1.0 / jnp.sqrt(jnp.asarray(h, char_emb.dtype))
        Q_char = _linear(char_emb, Wq_c, bq_c)
        K_sub = _linear(subword_emb, Wk_s, bk_s)
        V_sub = _linear(subword_emb, Wv_s, bv_s)
        scores = jnp.einsum('bqh,bkh->bqk', Q_char, K_sub) * scale
        char2sub = jnp.einsum('bqk,bkh->bqh', jax.nn.softmax(scores, axis=-1), V_sub)
        Q_sub = _linear(subword_emb, Wq_s, bq_s)
        K_char = _linear(char_emb, Wk_c, bk_c)
        V_char = _linear(char_emb, Wv_c, bv_c)
        scores2 = jnp.einsum('bqh,bkh->bqk', Q_sub, K_char) * scale
        sub2char = jnp.einsum('bqk,bkh->bqh', jax.nn.softmax(scores2, axis=-1), V_char)
        L_char = char_emb.shape[1]
        if sub2char.shape[1] != L_char:
            sub2char = _interp_linear(sub2char, L_char)
        gate_in = jnp.concatenate([char2sub, sub2char], axis=-1)
        gate = jax.nn.sigmoid(jnp.einsum('blh,oh->blo', gate_in, Wg) + bg)
        return gate * char2sub + (1 - gate) * sub2char

    def _L0_ffn_ref(hidden_states, combine_weights, top_idx, W1, b1, W2, b2):
        import jax, jax.numpy as jnp
        import numpy as np
        S, B, D, E, C, FF = (512, 4, 256, 8, 512, 1024)
        N = S * B
        s, b, d = hidden_states.shape
        x = hidden_states.reshape(-1, d)
        tok = top_idx.T
        gathered = x[tok]
        h = jax.nn.gelu(jnp.einsum('ecd,edf->ecf', gathered, W1) + b1[:, None, :])
        out_e = jnp.einsum('ecf,efd->ecd', h, W2) + b2[:, None, :]
        e_ids = jnp.arange(tok.shape[0])[:, None]
        w = combine_weights[tok, e_ids]
        weighted = (out_e * w[..., None]).reshape(-1, d)
        out = jnp.zeros_like(x).at[tok.reshape(-1)].add(weighted)
        return out.reshape(s, b, d)

    def _L1_attn_ref(x, Wq, bq, Wk, bk, Wv, bv, Wo, bo):
        import jax, jax.numpy as jnp
        import numpy as np
        B, S, D, H = (4, 512, 256, 16)

        def _apply_rope(x):
            b, s, d = x.shape
            half = d // 2
            freq = jnp.exp(jnp.arange(0, d, 2, dtype=jnp.float32) * (-np.log(10000.0) / d))
            ang = jnp.arange(s, dtype=jnp.float32)[:, None] * freq[None, :]
            cos, sin = (jnp.cos(ang), jnp.sin(ang))
            x1, x2 = (x[..., :half], x[..., half:])
            return jnp.concatenate([x1 * cos - x2 * sin, x1 * sin + x2 * cos], axis=-1)
        b, s, d = x.shape
        h = H
        hd = d // h
        rx = _apply_rope(x)

        def proj(W, bias):
            y = rx @ W.T + bias
            return y.reshape(b, s, h, hd).transpose(0, 2, 1, 3)
        q, k, v = (proj(Wq, bq), proj(Wk, bk), proj(Wv, bv))
        scores = jnp.einsum('bhqd,bhkd->bhqk', q, k) / np.sqrt(hd)
        attn = jax.nn.softmax(scores, axis=-1)
        attended = jnp.einsum('bhqk,bhkd->bhqd', attn, v)
        attended = attended.transpose(0, 2, 1, 3).reshape(b, s, d)
        return attended @ Wo.T + bo

    def _L1_xattn_ref(x, context, Wq, Wk, Wv, Wo, bo):
        import jax, jax.numpy as jnp
        import numpy as np
        B, N, D_MODEL, H, DH = (2, 512, 256, 16, 64)
        SCALE = DH ** (-0.5)
        b, n, _ = x.shape
        m = context.shape[1]
        q = (x @ Wq).reshape(b, n, H, DH)
        k = (context @ Wk * SCALE).reshape(b, m, H, DH)
        v = (context @ Wv).reshape(b, m, H, DH)
        scores = jnp.einsum('bihd,bjhd->bhij', q, k)
        attn = jax.nn.softmax(scores, axis=-1)
        out = jnp.einsum('bhij,bjhd->bihd', attn, v)
        out = out.reshape(b, n, H * DH)
        return out @ Wo + bo

    def _L1_ffn_ref(hidden_states, gate_weight, gate_up_proj, down_proj):
        import jax, jax.numpy as jnp
        import numpy as np
        TOP_K = 8
        NUM_EXPERTS = 32
        CAPACITY = 256
        B, S, H = hidden_states.shape
        E = gate_weight.shape[0]
        N = B * S
        x = hidden_states.reshape(N, H)
        logits = x @ gate_weight.T
        probs = jax.nn.softmax(logits.astype(jnp.float32), axis=-1)
        topw, topi = jax.lax.top_k(probs, TOP_K)
        topw = topw / topw.sum(-1, keepdims=True)
        topw = topw.astype(x.dtype)
        flat_e = topi.reshape(-1)
        flat_w = topw.reshape(-1)
        flat_x = jnp.repeat(x, TOP_K, axis=0)
        oh = jax.nn.one_hot(flat_e, E, dtype=jnp.int32)
        pos = (jnp.cumsum(oh, axis=0) * oh).sum(-1) - 1
        buf = jnp.zeros((E, CAPACITY, H), x.dtype).at[flat_e, pos].set(flat_x, mode='drop')
        gu = jnp.einsum('ech,efh->ecf', buf, gate_up_proj)
        gate, up = jnp.split(gu, 2, axis=-1)
        h = jax.nn.silu(gate) * up
        eo = jnp.einsum('ecf,ehf->ech', h, down_proj)
        tok_out = eo.at[flat_e, pos].get(mode='fill', fill_value=0)
        out = (tok_out * flat_w[:, None]).reshape(N, TOP_K, H).sum(1)
        return out.reshape(B, S, H)
    x = _layernorm(x + _L0_attn_ref(x, L0_attn_W_el, L0_attn_b_el, L0_attn_W_le, L0_attn_b_le), axis=-1)
    x = _layernorm(x + _L0_xattn_ref(x, ctx_1024, L0_xattn_Wq_c, L0_xattn_bq_c, L0_xattn_Wk_s, L0_xattn_bk_s, L0_xattn_Wv_s, L0_xattn_bv_s, L0_xattn_Wq_s, L0_xattn_bq_s, L0_xattn_Wk_c, L0_xattn_bk_c, L0_xattn_Wv_c, L0_xattn_bv_c, L0_xattn_Wg, L0_xattn_bg), axis=-1)
    x = _layernorm(x + _L0_ffn_ref(x, L0_ffn_combine_weights, L0_ffn_top_idx, L0_ffn_W1, L0_ffn_b1, L0_ffn_W2, L0_ffn_b2), axis=-1)
    x = _layernorm(x + _L1_attn_ref(x, L1_attn_Wq, L1_attn_bq, L1_attn_Wk, L1_attn_bk, L1_attn_Wv, L1_attn_bv, L1_attn_Wo, L1_attn_bo), axis=-1)
    x = _layernorm(x + _L1_xattn_ref(x, ctx_1024, L1_xattn_Wq, L1_xattn_Wk, L1_xattn_Wv, L1_xattn_Wo, L1_xattn_bo), axis=-1)
    x = _layernorm(x + _L1_ffn_ref(x, L1_ffn_gate_weight, L1_ffn_gate_up_proj, L1_ffn_down_proj), axis=-1)
    return x

_drawn_inputs = setup_inputs


def setup_inputs(seed=0):
    import zlib

    import numpy as np

    out = dict(_drawn_inputs(seed))
    spreads = {'L0_attn_b_el': (0.0, 0.379),
     'L0_attn_b_le': (0.0, 0.1),
     'L0_ffn_b1': (0.0, 0.1),
     'L0_ffn_b2': (0.0, 0.1),
     'L1_xattn_bo': (0.0, 0.1)}
    factors = {'L0_xattn_Wq_c': 8.0,
     'L0_xattn_bq_c': 8.0,
     'L0_xattn_Wk_s': 8.0,
     'L0_xattn_bk_s': 8.0,
     'L0_xattn_bv_s': 6.151,
     'L0_xattn_Wq_s': 8.0,
     'L0_xattn_bq_s': 8.0,
     'L0_xattn_Wk_c': 8.0,
     'L0_xattn_bk_c': 8.0,
     'L0_xattn_Wv_c': 5.071,
     'L0_xattn_bv_c': 5.965,
     'L0_xattn_Wg': 8.0,
     'L0_xattn_bg': 8.0,
     'L1_attn_Wq': 8.0,
     'L1_attn_bq': 8.0,
     'L1_attn_Wk': 8.0,
     'L1_attn_bk': 8.0,
     'L1_attn_Wv': 7.114,
     'L1_attn_bv': 8.0,
     'L1_attn_Wo': 5.681,
     'L1_attn_bo': 3.282,
     'L1_ffn_gate_weight': 8.0,
     'L1_ffn_gate_up_proj': 8.0,
     'L1_ffn_down_proj': 8.0}
    for name, (base, spread) in spreads.items():
        noise = np.random.default_rng([zlib.crc32(name.encode()), seed]).standard_normal(out[name].shape)
        drawn = base * np.exp(spread * noise) if base else spread * noise
        out[name] = jnp.asarray(drawn.astype(out[name].dtype))
    for name, factor in factors.items():
        out[name] = (out[name] * factor).astype(out[name].dtype)
    return out
```

```python
from contextlib import ExitStack

import numpy as np
import concourse.bass as bass
from concourse import mybir

f32, bf16, i32 = mybir.dt.float32, mybir.dt.bfloat16, mybir.dt.int32
ACT = mybir.ActivationFunctionType
ALU = mybir.AluOpType
AX = mybir.AxisListType

P = 128
B, S, D = 4, 512, 256
NT = B * S // P
TB = S // P
DC = D // P
EPS = 1e-5
E0, C0, F0 = 8, 512, 1024
FC0, CT0 = F0 // P, C0 // P
H1 = 16
E1, F1, CAP, TOPK = 32, 192, 256, 8
FH = F1 // 2
CT1 = CAP // P
GW = D + E0
FRACTAL = (2, 4, 8, 16, 32)
CREDIT = 1024


class Mark:

    def __init__(self, sem, k, section):
        self.sem, self.k, self.section = sem, k, section


class prev:

    def __init__(self, name):
        self.name = name


class Queue:

    def __init__(self, nc, ctx):
        self.nc, self.ctx = nc, ctx
        self.eng = {"pe": nc.tensor, "dve": nc.vector, "act": nc.scalar, "pool": nc.gpsimd, "sp": nc.sync}
        self.sems, self.base = {}, {}
        self.fence = ctx.enter_context(nc.semaphore("s_fence"))
        for e in ("pe", "dve", "act", "pool"):
            self._sem(e)
        self.section, self.ops, self.count, self.names, self.past = 0, [], {}, {}, {}

    def _sem(self, name, credit=CREDIT):
        if name not in self.sems:
            self.sems[name] = self.ctx.enter_context(self.nc.semaphore("s_" + name))
            self.base[name] = credit
            if credit:
                self.nc.sync.sem_inc(self.sems[name], credit)

    def _add(self, e, sem, by, fn, after, name, plain=False):
        mark = None
        if sem:
            self.count[sem] = self.count.get(sem, 0) + by
            mark = Mark(sem, self.count[sem], self.section)
            if name:
                self.names[name] = mark
        flat = []
        for a in after:
            flat += a if isinstance(a, (list, tuple)) else [a]
        self.ops.append((e, sem, by, fn, [a for a in flat if a is not None], plain))
        return mark

    def op(self, e, fn, *after, name=None, inc=True, plain=False):
        return self._add(e, e if inc else None, 1, fn, after, name, plain)

    def dma(self, e, stream, fn, *after, name=None):
        self._sem(stream, 0 if e == "pool" else CREDIT)
        return self._add(e, stream, 16, fn, after, name, plain=e == "pool")

    def _value(self, mark, n):
        base, per, times = self.past[mark.section]
        return base[mark.sem] + (times - 1) * per.get(mark.sem, 0) + mark.k

    def flush(self, n=None):
        ops, per, base = self.ops, self.count, dict(self.base)
        names, me, eng = self.names, self.section, self.eng
        outer, todo = {}, []
        for e, sem, by, fn, after, plain in ops:
            waits = []
            for a in after:
                lag = 0
                if isinstance(a, prev):
                    if n is None:
                        continue
                    a, lag = names[a.name], 1
                if a.section == me:
                    waits.append((a.sem, a.k - lag * per[a.sem]))
                    assert base[a.sem] + waits[-1][1] > 0, (a.sem, a.k)
                else:
                    outer[e, a.sem] = max(outer.get((e, a.sem), 0), self._value(a, n))
            todo.append((e, sem, by, fn, waits, plain))
        for (e, s), v in outer.items():
            eng[e].wait_ge(self.sems[s], v)

        def emit(i):
            at, seen = {}, {}
            for e, sem, by, fn, waits, plain in todo:
                for s, k in waits:
                    if seen.get((e, s), -1 << 30) >= k:
                        continue
                    seen[e, s] = k
                    if n is None:
                        eng[e].wait_ge(self.sems[s], base[s] + k)
                    else:
                        if (e, s) not in at:
                            at[e, s] = eng[e].snap(i * per[s] + base[s])
                        eng[e].wait_ge(self.sems[s], at[e, s] + k)
                if plain and waits and n is not None:
                    eng[e].sem_inc(self.fence, 1)
                ins = fn(i)
                if sem:
                    ins.then_inc(self.sems[sem], by)

        if n is None:
            emit(None)
        else:
            with self.nc.Fori(0, n) as i:
                emit(i)
        for s, c in per.items():
            self.base[s] += c * (n or 1)
        self.past[me] = (base, per, n or 1)
        self.section += 1
        self.ops, self.count, self.names = [], {}, {}

    def barrier(self):
        self.flush()
        for e in self.eng.values():
            for s, sem in self.sems.items():
                if self.base[s] not in (0, CREDIT):
                    e.wait_ge(sem, self.base[s])


def program(nc, T, out, phases=9, dbg=None):
    ctx = ExitStack()
    with ctx:
        ctx.enter_context(nc.allow_non_contiguous_dma(reason="broadcasts and small tables"))
        build(nc, ctx, T, out, phases)


def build(nc, ctx, T, out, phases):
    q = Queue(nc, ctx)
    V, A, PE, G, SP = nc.vector, nc.scalar, nc.tensor, nc.gpsimd, nc.sync

    used = {}

    def sb(name, shape, dt=f32, where=ctx):
        used[name] = used.get(name, 0) + 1
        if used[name] > 1:
            name += "_use%d" % used[name]
        return where.enter_context(nc.sbuf_tensor(name, shape, dt))[tuple(slice(None) for _ in shape)]

    bank = [ctx.enter_context(nc.psum_tensor(f"bank{k}", [P, 512], f32))[:, :] for k in range(8)]
    rows_d = nc.dram_tensor("rows_scratch", (B * S, GW), f32, kind="Internal").ap()
    acc_d = nc.dram_tensor("acc_scratch", (B * S, D), f32, kind="Internal").ap()
    slot_d = nc.dram_tensor("slot_scratch", (2, E1 * CAP), f32, kind="Internal").ap()

    X = sb("X", [P, NT, D])
    ident = sb("ident", [P, P])
    xs = sb("xs", [P, TB, D])
    xT = sb("xT", [P, DC, S])
    summed = sb("summed", [P, TB, D])
    stats = sb("stats", [P, TB, 6])
    mv = sb("mv", [P, TB, 2])
    veps = sb("veps", [P, TB])
    rstd = sb("rstd", [P, TB])
    mhalf = sb("mhalf", [P, TB])
    load = q.dma("sp", "d_x", lambda i: SP.dma_start(X, T["x"].rearrange("(t p) d -> p t d", p=P)))
    load_id = q.dma("sp", "d_id", lambda i: SP.dma_start(ident, T["ident"]))
    c_half = q.op("pool", lambda i: G.memset(mhalf, -0.5))

    def batch_rows(i):
        return X[:, bass.ds(i * TB, TB), :]

    def take_batch(*after):
        got = q.op("dve", lambda i: V.tensor_copy(xs, batch_rows(i)), *after, prev("summed_all"), prev("xs_read"))
        ready = []
        for c in range(DC):
            for t in range(TB):
                m = q.op("pe", lambda i, c=c, t=t: PE.transpose(bank[c][:, t * P:(t + 1) * P], xs[:, t, c * P:(c + 1) * P], ident),
                         got, prev("xT%d" % c), inc=t == TB - 1, name="xs_read")
            e = ("dve", "act")[c]
            last = q.op(e, (lambda i, c=c: V.tensor_copy(xT[:, c, :], bank[c])) if c == 0 else
                        (lambda i, c=c: A.activation(xT[:, c, :], bank[c], ACT.Copy)),
                        m, prev("xT_read"), name="xT%d" % c)
            ready.append(last)
        return ready

    def norm_tile(t, ps, *after, extra=None):
        a = q.op("dve", lambda i: V.tensor_tensor(summed[:, t, :], ps, xs[:, t, :], ALU.add),
                 *after, prev("normed"), name="summed%d" % t)
        if extra is not None:
            a = q.op("dve", lambda i: V.tensor_tensor(summed[:, t, :], summed[:, t, :], extra, ALU.add), a)
        s = q.op("dve", lambda i: V.bn_stats(stats[:, t, :], summed[:, t, :]), a)
        return a, q.op("dve", lambda i: V.bn_aggr(mv[:, t, :], stats[:, t, :]), s, prev("veps"), name="summed_all", plain=True)

    def norm_batch(m, where):
        v = q.op("pool", lambda i: G.tensor_scalar(veps, mv[:, :, 1], EPS, None, ALU.add), m, name="veps", plain=True)
        r = q.op("pool", lambda i: G.tensor_tensor(rstd, veps, mhalf, ALU.pow), v, c_half)
        for t in range(TB):
            last = q.op("dve", lambda i, t=t: V.tensor_scalar(where(i, t), summed[:, t, :], mv[:, t, 0:1], rstd[:, t:t + 1],
                                                             ALU.subtract, ALU.mult), r, name="normed")
        return last

    def to_X(i, t):
        return X[:, bass.ds(i * TB + t, 1), :].rearrange("p a d -> p (a d)")

    with ExitStack() as ph:
        first = sb("first", [5, 1024], where=ph)
        fmask = sb("fmask", [5, 1024], where=ph)
        work5 = sb("work5", [5, 1024], where=ph)
        fconst = sb("fconst", [5, P + 1], where=ph)
        kcols = sb("kcols", [P, 4], where=ph)
        basis = sb("basis", [P, DC, D], where=ph)
        gbasis = sb("gbasis", [P, DC, D], where=ph)
        Cmat = sb("Cmat", [P, DC, D], where=ph)
        w_el = sb("w_el", [P, DC, 24], where=ph)
        w_le = sb("w_le", [25, D], where=ph)
        b_el = sb("b_el", [24, 1], where=ph)
        golay = sb("golay", [24, 48], where=ph)
        CW = sb("CW", [P, DC, 24], where=ph)
        mm = sb("mm", [P, 2], where=ph)
        mmT = sb("mmT", [2, 1], where=ph)
        mm1 = sb("mm1", [5, 8], where=ph)
        sel = sb("sel", [2, 10], where=ph)
        dcol = sb("dcol", [P, 8], where=ph)
        trig = sb("trig", [P, 8], where=ph)
        bits = sb("bits", [24, S], where=ph)
        syn = sb("syn", [24, S], where=ph)
        fix = sb("fix", [24, S], where=ph)
        corr = sb("corr", [32, S], where=ph)
        small = [(first, bass.AP(T["x"].tensor, 0, [[0, 5], [1, 1024]])), (fmask, T["fmask"]), (fconst, T["fconst"]), (kcols, T["kcols"]),
                 (basis, T["basis"]), (w_el, T["W_el"]), (w_le, T["W_le"]), (b_el, T["b_el"]), (golay, T["golay"]), (sel, T["sel"])]
        for dst, src in small:
            loaded = q.dma("act", "d_small", lambda i, dst=dst, src=src: A.dma_start(dst, src))
        ones = q.op("pool", lambda i: G.memset(corr, 1.0))
        m1 = q.op("dve", lambda i: V.tensor_reduce(mm[:, 0:1], X, AX.XY, ALU.max), load)
        m2 = q.op("dve", lambda i: V.tensor_reduce(mm[:, 1:2], X, AX.XY, ALU.min, negate=True), load)
        m = q.op("pe", lambda i: PE.transpose(bank[0][0:2, 0:P], mm, ident), m1, m2, load_id)
        m = q.op("dve", lambda i: V.tensor_reduce(mmT, bank[0][0:2, 0:P], AX.X, ALU.max), m)
        q.op("pe", lambda i: PE.matmul(bank[1][0:5, 0:1], sel[:, 0:5], mmT, start=True, stop=True), m, loaded, inc=False)
        m = q.op("pe", lambda i: PE.matmul(bank[1][0:5, 1:2], sel[:, 5:10], mmT, start=True, stop=True))
        m = q.op("dve", lambda i: V.tensor_copy(mm1[:, 0:2], bank[1][0:5, 0:2]), m)
        m = q.op("dve", lambda i: V.scalar_tensor_tensor(mm1[:, 2:3], mm1[:, 0:1], 1e-10, mm1[:, 1:2], ALU.add, ALU.add), m)
        m = q.op("dve", lambda i: V.reciprocal(mm1[:, 3:4], mm1[:, 2:3]), m)
        m = q.op("dve", lambda i: V.tensor_scalar(first, first, mm1[:, 1:2], mm1[:, 3:4], ALU.add, ALU.mult), m)
        m = q.op("dve", lambda i: V.scalar_tensor_tensor(work5, first, 1.0, fmask, ALU.mult, ALU.mult, accum_out=mm1[:, 4:5]), m)
        m = q.op("dve", lambda i: V.tensor_tensor(mm1[:, 5:6], mm1[:, 4:5], fconst[:, P:P + 1], ALU.mult), m)
        m = q.op("dve", lambda i: V.scalar_tensor_tensor(work5, first, mm1[:, 5:6], fmask, ALU.is_gt, ALU.mult, accum_out=mm1[:, 6:7]), m)
        m = q.op("dve", lambda i: V.tensor_scalar(mm1[:, 6:7], mm1[:, 6:7], 1.0, None, ALU.max), m)
        m = q.op("act", lambda i: A.activation(mm1[:, 7:8], mm1[:, 6:7], ACT.Ln), m)
        m = q.op("pe", lambda i: PE.matmul(bank[2][:, 0:1], fconst[:, 0:P], mm1[:, 7:8], start=True, stop=True), m)
        m = q.op("dve", lambda i: V.tensor_scalar(dcol[:, 0:1], bank[2][:, 0:1], 1.0, 2.0, ALU.max, ALU.min), m)
        m = q.op("dve", lambda i: V.tensor_scalar(dcol[:, 1:2], dcol[:, 0:1], 0.2, 1.0, ALU.mult, ALU.add), m)
        m = q.op("dve", lambda i: V.tensor_tensor(dcol[:, 2:3], dcol[:, 1:2], dcol[:, 0:1], ALU.mult), m)
        m = q.op("dve", lambda i: V.tensor_scalar(dcol[:, 3:4], dcol[:, 0:1], 0.5, 1.0, ALU.mult, ALU.add), m)
        m = q.op("dve", lambda i: V.tensor_scalar(dcol[:, 4:5], dcol[:, 0:1], 0.1, None, ALU.mult), m)
        m = q.op("dve", lambda i: V.tensor_scalar(trig[:, 0:2], kcols[:, 0:2], dcol[:, 3:4], dcol[:, 2:3], ALU.mult, ALU.add), m)
        m = q.op("dve", lambda i: V.tensor_scalar(trig[:, 2:4], kcols[:, 2:4], dcol[:, 4:5], dcol[:, 2:3], ALU.mult, ALU.add), m)
        m = q.op("dve", lambda i: V.tensor_tensor(trig[:, 2:4], trig[:, 2:4], kcols[:, 0:2], ALU.subtract), m)
        m = q.op("dve", lambda i: V.tensor_scalar(trig[:, 0:2], trig[:, 0:2], -1.0, float(np.pi), ALU.mult, ALU.add), m)
        m = q.op("dve", lambda i: V.tensor_scalar(trig[:, 2:4], trig[:, 2:4], -1.0, float(np.pi / 2), ALU.mult, ALU.add), m)
        m = q.op("act", lambda i: A.activation(trig[:, 4:8], trig[:, 0:4], ACT.Sin), m)
        m = q.op("dve", lambda i: V.tensor_tensor(trig[:, 0:2], trig[:, 4:6], trig[:, 6:8], ALU.mult), m)
        for c in range(DC):
            g = q.op("dve", lambda i, c=c: V.tensor_scalar(gbasis[:, c, :], basis[:, c, :], trig[:, c:c + 1], None, ALU.mult), m)
        for r in range(DC):
            for c in range(DC):
                m = q.op("pe", lambda i, r=r, c=c: PE.matmul(bank[3][:, r * D:(r + 1) * D], basis[:, c, r * P:(r + 1) * P], gbasis[:, c, :],
                                                             start=c == 0, stop=c == DC - 1), g)
        m = q.op("dve", lambda i: V.tensor_copy(Cmat.rearrange("p c d -> p (c d)"), bank[3]), m)
        for r in range(DC):
            for c in range(DC):
                w = q.op("pe", lambda i, r=r, c=c: PE.matmul(bank[4][:, r * 24:(r + 1) * 24], Cmat[:, c, r * P:(r + 1) * P], w_el[:, c, :],
                                                             start=c == 0, stop=c == DC - 1), m)
        m_cw = q.op("dve", lambda i: V.tensor_copy(CW.rearrange("p c d -> p (c d)"), bank[4][:, 0:48]), w)
        q.barrier()

        x_ready = take_batch()
        for c in range(DC):
            m = q.op("pe", lambda i, c=c: PE.matmul(bank[2][0:24, :], CW[:, c, :], xT[:, c, :], start=c == 0, stop=c == DC - 1),
                     x_ready, prev("bits"))
        m = q.op("dve", lambda i: V.tensor_scalar(bits, bank[2][0:24, :], b_el, 0.0, ALU.add, ALU.is_gt), m, name="bits")
        m = q.op("pe", lambda i: PE.matmul(bank[3][0:24, :], golay[:, 0:24], bits, start=True, stop=True), m, prev("syn"), plain=True)
        m = q.op("dve", lambda i: V.tensor_scalar(syn, bank[3][0:24, :], 0.5, None, ALU.is_gt), m, name="syn")
        m = q.op("pe", lambda i: PE.matmul(bank[4][0:24, :], golay[:, 24:48], syn, start=True, stop=True), m, prev("fixed"), plain=True)
        m = q.op("dve", lambda i: V.scalar_tensor_tensor(fix, bank[4][0:24, :], 3.5, syn, ALU.is_le, ALU.mult), m, name="fixed")
        n = q.op("dve", lambda i: V.tensor_scalar(syn, bits, -2.0, 1.0, ALU.mult, ALU.add), m)
        m = q.op("dve", lambda i: V.tensor_tensor(fix, fix, syn, ALU.mult), n)
        m = q.op("dve", lambda i: V.tensor_tensor(corr[0:24, :], bits, fix, ALU.add), m, prev("xT_read"))
        for t in range(TB):
            bk = bank[5 + t // 2][:, (t % 2) * D:(t % 2 + 1) * D]
            for c in range(DC):
                q.op("pe", lambda i, t=t, c=c, bk=bk: PE.matmul(bk, xT[:, c, t * P:(t + 1) * P], Cmat[:, c, :], start=c == 0, stop=False),
                     prev("summed%d" % (t | 1)), inc=False)
            y = q.op("pe", lambda i, t=t, bk=bk: PE.matmul(bk, corr[0:25, t * P:(t + 1) * P], w_le, start=False, stop=True), m, name="xT_read")
            if t % 2:
                for u in (t - 1, t):
                    last = norm_tile(u, bank[5 + t // 2][:, (u % 2) * D:(u % 2 + 1) * D], y)
        norm_batch(last[1], to_X)
        q.flush(B)
        q.barrier()
    if phases <= 1:
        return finish(q, out, X, SP)

    S_BANKS, T_BANKS, O_BANKS, M_BANK = (0, 1, 2), (3, 4), (5, 6), 7
    T_LAG, PV_LAG = 5, 6

    def attend(buf, scores, values, jobs, before=None, after=None):
        steps = TB * jobs
        done = {}
        for s in range(steps + PV_LAG):
            if before and s < steps:
                before(s)
            u = s - T_LAG
            if 0 <= u < steps:
                h, kt = divmod(u, TB)
                tb = T_BANKS[u % 2]
                for t in range(TB):
                    m = q.op("pe", lambda i, t=t, kt=kt, tb=tb, h=h: PE.transpose(bank[tb][:, t * P:(t + 1) * P], buf.P[h % 2][:, t, kt * P:(kt + 1) * P], ident),
                             [done["scaled", h, x] for x in range(TB)], done.get(("copied", u - 2)) or prev("copied%d" % (u % 2)),
                             inc=t == TB - 1)
                done["transposed", h] = m
                if kt == TB - 1:
                    q.names["P_read%d" % (h % 2)] = m
                free = done.get(("pv", u - 3)) or prev("pv_any")
                if u % 2:
                    m = q.op("dve", lambda i, u=u, tb=tb: V.tensor_copy(buf.PT[u % 3], bank[tb]), m, free, name="copied1")
                else:
                    m = q.op("act", lambda i, u=u, tb=tb: A.activation(buf.PT[u % 3], bank[tb], ACT.Copy), m, free, name="copied0")
                done["copied", u] = m
            if s < steps:
                h, j = divmod(s, TB)
                sbk = S_BANKS[s % 3]
                pairs, ready = scores(h, j)
                for n, (lhs, rhs) in enumerate(pairs):
                    m = q.op("pe", lambda i, lhs=lhs, rhs=rhs, n=n, sbk=sbk, k=len(pairs): PE.matmul(bank[sbk], lhs, rhs, start=n == 0, stop=n == k - 1),
                             ready, done.get(("exp", s - 3)) or prev("exp%d" % (s % 3)), inc=n == len(pairs) - 1)
                done["scores", h] = m
                c = s % 8
                m = q.op("dve", lambda i, c=c, sbk=sbk: V.tensor_reduce(buf.nmax[:, c:c + 1], bank[sbk], AX.X, ALU.max, negate=True), m,
                         done.get(("exp", s - 8)) or prev("exp_any"))
                m = q.op("act", lambda i, c=c, sbk=sbk, h=h, j=j: A.activation(buf.P[h % 2][:, j, :], bank[sbk], ACT.Exp, bias=buf.nmax[:, c:c + 1], accum_out=buf.rsum[:, c:c + 1]),
                         m, done.get(("transposed", h - 2)) or prev("P_read%d" % (h % 2)), done.get(("scaled8", s - 8)) or prev("scaled_any"), name="exp%d" % (s % 3))
                q.names["exp_any"] = m
                done["exp", s] = m
                m = q.op("dve", lambda i, c=c: V.reciprocal(buf.rinv[:, c:c + 1], buf.rsum[:, c:c + 1]), m)
                m = q.op("dve", lambda i, c=c, h=h, j=j: V.tensor_scalar(buf.P[h % 2][:, j, :], buf.P[h % 2][:, j, :], buf.rinv[:, c:c + 1], None, ALU.mult), m, name="scaled_any")
                done["scaled", h, j] = done["scaled8", s] = m
            u = s - PV_LAG
            if 0 <= u < steps:
                h, kt = divmod(u, TB)
                triples, ready = values(h, kt)
                for lhs, bk, first, last in triples:
                    m = q.op("pe", lambda i, lhs=lhs, bk=bk, first=first, last=last, u=u: PE.matmul(bank[bk], lhs, buf.PT[u % 3], start=first, stop=last),
                             done["copied", u], ready, name="pv_any")
                done["pv", u] = m
                if kt == TB - 1:
                    done["head", h] = m
                    if after:
                        after(h, m)
        return done

    class Buffers:

        def __init__(self, where):
            self.P = [sb("P%d" % k, [P, TB, S], where=where) for k in range(2)]
            self.PT = [sb("PT%d" % k, [P, S], where=where) for k in range(3)]
            self.nmax = sb("nmax", [P, 8], where=where)
            self.rsum = sb("rsum", [P, 8], where=where)
            self.rinv = sb("rinv", [P, 8], where=where)

    def project(w, src, c, dst, bias, scale, ready, free, name, e="dve"):
        for k in range(DC):
            m = q.op("pe", lambda i, k=k: PE.matmul(bank[M_BANK], w[:, k, c * P:(c + 1) * P], src[:, k, :], start=k == 0, stop=k == DC - 1),
                     ready, prev("M_bank") if "M_bank" not in q.names else q.names["M_bank"], inc=k == DC - 1, name=name + "_in")
        if e == "act":
            m = q.op("act", lambda i: A.activation(dst, bank[M_BANK], ACT.Identity, bias=bias, scale=scale) if bias is not None
                     else A.activation(dst, bank[M_BANK], ACT.Copy, scale=scale), m, free, name=name)
        else:
            m = q.op("dve", lambda i: V.tensor_scalar(dst, bank[M_BANK], bias if bias is not None else 0.0, scale, ALU.add, ALU.mult), m, free, name=name)
        q.names["M_bank"] = m
        return m

    with ExitStack() as ph:
        buf = Buffers(ph)
        W6 = {n: sb("w_" + n, [P, DC, D], where=ph) for n in ("Wq_c", "Wk_s", "Wv_s", "Wq_s", "Wk_c", "Wv_c")}
        Wg = sb("Wg", [P, 2 * DC, D], where=ph)
        bias0 = sb("bias0", [P, 7, DC], where=ph)
        bgh = sb("bgh", [P, DC], where=ph)
        ctxT = sb("ctxT", [P, DC, S], where=ph)
        QK = [[sb("%s%d" % (n, d), [P, DC, S], where=ph) for n in ("QT", "KT")] for d in range(2)]
        VV = [sb("VV%d" % d, [P, TB, D], where=ph) for d in range(2)]
        cT = sb("cT", [P, 2 * DC, S], where=ph)
        gate = sb("gate", [P, DC, S], where=ph)
        mix = sb("mix", [P, DC, S], where=ph)
        for n, t in W6.items():
            w_in = q.dma("act", "d_w0", lambda i, n=n, t=t: A.dma_start(t, T[n]))
        w_in = q.dma("act", "d_w0", lambda i: A.dma_start(Wg, T["Wg"]))
        w_in = q.dma("act", "d_w0", lambda i: A.dma_start(bias0, T["bias0"]))
        halved = q.op("dve", lambda i: V.tensor_scalar(bgh, bias0[:, 6, :], 0.5, None, ALU.mult), w_in)
        q.flush()

        ctx_in = q.dma("sp", "d_ctx", lambda i: SP.dma_start(ctxT, T["ctxT"][bass.ds(i, 1)].rearrange("a p c s -> p (a c) s")), prev("ctx_read"))
        x_ready = take_batch(w_in)
        x_ready.append(w_in)
        SC = D ** -0.5
        ready = {}
        for d, (qs, ks, qm, km, wq, wk, wv) in enumerate([(xT, ctxT, x_ready, ctx_in, "Wq_c", "Wk_s", "Wv_s"),
                                                          (ctxT, xT, ctx_in, x_ready, "Wq_s", "Wk_c", "Wv_c")]):
            for c in range(DC):
                a = project(W6[wq], qs, c, QK[d][0][:, c, :], bias0[:, 3 * d, c:c + 1], SC, qm, prev("scores%d" % d), "Q%d%d" % (d, c), "dve")
                b = project(W6[wk], ks, c, QK[d][1][:, c, :], bias0[:, 3 * d + 1, c:c + 1], 1.0, km, prev("scores%d" % d), "K%d%d" % (d, c), "act")
                ready.setdefault(d, []).extend([a, b])
            vb = O_BANKS[0]
            for pair in range(2):
                for t in (2 * pair, 2 * pair + 1):
                    for k in range(DC):
                        m = q.op("pe", lambda i, t=t, k=k, ks=ks, wv=wv, pair=pair: PE.matmul(bank[O_BANKS[pair]][:, (t % 2) * D:(t % 2 + 1) * D], ks[:, k, t * P:(t + 1) * P], W6[wv][:, k, :],
                                                                         start=k == 0, stop=k == DC - 1), km, ready.get(("V", d - 1, pair)) or prev("O_free%d" % pair),
                                 name="xT_read")
                m = q.op("act" if pair else "dve", (lambda i, d=d, pair=pair: A.activation(VV[d][:, 2 * pair:2 * pair + 2, :].rearrange("p t d -> p (t d)"), bank[O_BANKS[pair]], ACT.Copy)) if pair else
                         (lambda i, d=d, pair=pair: V.tensor_copy(VV[d][:, 2 * pair:2 * pair + 2, :].rearrange("p t d -> p (t d)"), bank[O_BANKS[pair]])),
                         m, prev("pv_any"))
                ready["V", d, pair] = m
        q.names["ctx_read"] = q.names["xT_read"]

        def scores0(h, j):
            Q, K = QK[h]
            return [(Q[:, c, j * P:(j + 1) * P], K[:, c, :]) for c in range(DC)], ready[h]

        def values0(h, kt):
            w = [ready["V", h, 0], ready["V", h, 1], ready["V", 1, 0], ready["V", 1, 1]]
            if h:
                w += ready["out", h - 1]
            return [(VV[h][:, kt, c * P:(c + 1) * P], O_BANKS[c], kt == 0, kt == TB - 1) for c in range(DC)], w

        def after0(h, m):
            for c in range(DC):
                r = q.op("act", lambda i, c=c: A.activation(cT[:, DC * h + c, :], bank[O_BANKS[c]], ACT.Identity, bias=bias0[:, 3 * h + 2, c:c + 1], scale=1.0),
                         m, prev("mixed"), name="O_free%d" % c)
                ready.setdefault(("out", h), []).append(r)

        done = attend(buf, scores0, values0, 2, after=after0)
        q.names["scores0"], q.names["scores1"] = done["scores", 0], done["scores", 1]
        both = ready["out", 0] + ready["out", 1]
        for c in range(DC):
            for k in range(2 * DC):
                m = q.op("pe", lambda i, c=c, k=k: PE.matmul(bank[T_BANKS[c]], Wg[:, k, c * P:(c + 1) * P], cT[:, k, :], start=k == 0, stop=k == 2 * DC - 1),
                         both, done["copied", 4 * 2 - 2 + c])
            m = q.op("act", lambda i, c=c: A.activation(gate[:, c, :], bank[T_BANKS[c]], ACT.Tanh, bias=bgh[:, c:c + 1], scale=0.5), m, prev("mixed"), name="copied%d" % c)
            m = q.op("pool", lambda i, c=c: G.tensor_scalar(gate[:, c, :], gate[:, c, :], 0.5, 0.5, ALU.mult, ALU.add), m, plain=True)
            n = q.op("dve", lambda i, c=c: V.tensor_tensor(mix[:, c, :], cT[:, c, :], cT[:, DC + c, :], ALU.subtract), both, prev("mix_read"))
            n = q.op("dve", lambda i, c=c: V.tensor_tensor(mix[:, c, :], mix[:, c, :], gate[:, c, :], ALU.mult), n, m)
            n = q.op("dve", lambda i, c=c: V.tensor_tensor(mix[:, c, :], mix[:, c, :], cT[:, DC + c, :], ALU.add), n, name="mixed")
            ready["mix", c] = n
        for t in range(TB):
            for c in range(DC):
                m = q.op("pe", lambda i, t=t, c=c: PE.transpose(bank[O_BANKS[t // 2]][:, (t % 2) * D + c * P:(t % 2) * D + (c + 1) * P], mix[:, c, t * P:(t + 1) * P], ident),
                         ready["mix", 0], ready["mix", 1], name="mix_read")
            if t % 2:
                for v in (t - 1, t):
                    last = norm_tile(v, bank[O_BANKS[t // 2]][:, (v % 2) * D:(v % 2 + 1) * D], m)
                q.names["O_free%d" % (t // 2)] = last[0]
        norm_batch(last[1], to_X)
        q.flush(B)
        q.barrier()
    if phases <= 2:
        return finish(q, out, X, SP)

    def norm_from_acc():
        ld = q.dma("sp", "d_acc", lambda i: SP.dma_start(summed, acc_d.rearrange("(t p) d -> p t d", p=P)[:, bass.ds(i * TB, TB), :]), prev("normed"))
        for t in range(TB):
            s_ = q.op("dve", lambda i, t=t: V.bn_stats(stats[:, t, :], summed[:, t, :]), ld)
            m = q.op("dve", lambda i, t=t: V.bn_aggr(mv[:, t, :], stats[:, t, :]), s_, prev("veps"), plain=True)
        norm_batch(m, to_X)
        q.flush(B)
        q.barrier()

    with ExitStack() as ph:
        W1 = [sb("W1_%d" % b, [P, DC, F0], where=ph) for b in range(2)]
        W2 = [sb("W2_%d" % b, [P, FC0, D], where=ph) for b in range(2)]
        b1 = sb("b1", [P, E0 * FC0], where=ph)
        b2 = sb("b2", [P, E0 * D], where=ph)
        idx_all = sb("idx_all", [P, (E0 + 2) * CT0], i32, where=ph)
        tok_col = sb("tok_col", [P, E0 * CT0], where=ph)
        tok_row = sb("tok_row", [P, E0 * C0], i32, where=ph)
        lower = sb("lower", [P, P], where=ph)
        idx = [sb("idx%d" % b, [P, CT0], i32, where=ph) for b in range(2)]
        rows = [sb("rows%d" % b, [P, CT0, GW], where=ph) for b in range(2)]
        wcol = [sb("wcol%d" % b, [P, CT0], where=ph) for b in range(2)]
        GT = [sb("GT%d" % b, [P, DC, C0], where=ph) for b in range(2)]
        hT = [sb("hT%d" % b, [P, FC0, C0], where=ph) for b in range(2)]
        same = [sb("same%d" % b, [P, CT0, P], where=ph) for b in range(2)]
        junk = sb("junk", [P, P], where=ph)
        again = sb("again", [P, 2 * CT0], where=ph)
        sidx = [sb("sidx%d" % b, [P, CT0], i32, where=ph) for b in range(2)]
        wv = [sb("wv%d" % b, [P, D], where=ph) for b in range(2)]
        merged = [sb("merged%d" % b, [P, CT0, D], where=ph) for b in range(2)]
        for dst, src in ((b1, T["b1"]), (b2, bass.AP(T["b2"].tensor, 0, [[0, P], [1, E0 * D]])), (lower, T["lower"])):
            w_in = q.dma("act", "d_w0", lambda i, dst=dst, src=src: A.dma_start(dst, src))
        i_in = q.dma("pool", "d_g0", lambda i: G.dma_start(idx_all[:, 0:E0 * CT0], T["idx"]))
        padded = [i_in, q.op("pool", lambda i: G.memset(idx_all[:, E0 * CT0:], 0))]
        j_in = q.dma("pool", "d_g1", lambda i: G.dma_start(tok_row, bass.AP(T["tok"].tensor, 0, [[0, P], [1, E0 * C0]])))
        acc_in = q.dma("pool", "d_sc0", lambda i: G.dma_start(acc_d.rearrange("(t p) d -> p t d", p=P), X))
        rows_in = [q.dma("pool", "d_sc1", lambda i: G.dma_start(rows_d.rearrange("(t p) d -> p t d", p=P)[:, :, 0:D], X)),
                   q.dma("sp", "d_rows", lambda i: SP.dma_start(rows_d[:, D:GW], T["combine"]))]
        tok_f = q.op("dve", lambda i: V.tensor_copy(tok_col, idx_all[:, 0:E0 * CT0]), i_in)
        q.flush()

        def gather0(i, b, rows_free):
            m = q.op("pool", lambda _, b=b, i=i: G.tensor_copy(idx[b], idx_all[:, i(_, b)]), padded, rows_free, q.names.get("gathered%d" % b))
            for t in range(CT0):
                q.dma("pool", "d_g%d" % b, lambda _, b=b, t=t: G.indirect_dma_start(rows[b][:, t, :], None, rows_d, bass.IndirectOffsetOnAxis(ap=idx[b][:, t:t + 1], axis=0)),
                      m, rows_in, rows_free, name="gathered%d" % b)

        for b in range(2):
            gather0(lambda _, b: slice(b * CT0, (b + 1) * CT0), b, None)
        q.flush()
        for b in range(2):
            for dst, name in ((W1[b], "W1"), (W2[b], "W2")):
                w = q.dma("sp", "d_e%d" % b, lambda i, b=b, dst=dst, name=name: SP.dma_start(dst, T[name][bass.ds(2 * i + b, 1)].rearrange("a p c f -> p (a c) f")), prev("W_read%d" % b))
            g = prev("gathered%d" % b)
            for c in range(DC):
                for t in range(CT0):
                    m = q.op("pe", lambda i, b=b, t=t, c=c: PE.transpose(bank[c][:, t * P:(t + 1) * P], rows[b][:, t, c * P:(c + 1) * P], ident),
                             g, (q.names["GT%d" % c] if b else prev("GT%d" % c)), inc=t == CT0 - 1)
                m_t = m
                if c:
                    m = q.op("act", lambda i, b=b, c=c: A.activation(GT[b][:, c, :], bank[c], ACT.Copy), m, prev("GT_read%d" % b), name="GT1")
                else:
                    m = q.op("dve", lambda i, b=b, c=c: V.tensor_copy(GT[b][:, c, :], bank[c]), m, prev("GT_read%d" % b), name="GT0")
            gt = [q.names["GT0"], q.names["GT1"]]
            wc = q.op("dve", lambda i, b=b: V.tensor_copy(wcol[b], rows[b][:, :, bass.ds(2 * i + b + D, 1)].rearrange("p t a -> p (t a)")), g, prev("wcol_read%d" % b))
            gather0(lambda i, b: bass.ds((2 * i + b + 2) * CT0, CT0), b, [m_t, wc])
            for t in range(CT0):
                a = q.op("dve", lambda i, b=b, t=t: V.tensor_scalar(same[b][:, t, :], tok_row[:, bass.ds((2 * i + b) * C0 + t * P, P)], tok_col[:, bass.ds((2 * i + b) * CT0 + t, 1)], None, ALU.is_equal),
                         tok_f, j_in, prev("same_read%d" % b))
                m = q.op("dve", lambda i, b=b, t=t: V.scalar_tensor_tensor(junk, tok_row[:, bass.ds((2 * i + b) * C0 + t * P, P)], tok_col[:, bass.ds((2 * i + b) * CT0 + t, 1)], lower,
                                                                        ALU.is_equal, ALU.mult, accum_out=again[:, t:t + 1]), w_in, q.names.get("junk") or prev("junk"), name="junk")
            m = q.op("dve", lambda i: V.tensor_scalar(again[:, CT0:2 * CT0], again[:, 0:CT0], 0.0, float(1 << 16), ALU.is_gt, ALU.mult), m)
            found = q.op("dve", lambda i, b=b: V.tensor_tensor(sidx[b], again[:, CT0:2 * CT0], tok_col[:, bass.ds((2 * i + b) * CT0, CT0)], ALU.add), m, prev("stored%d" % b))
            for f in range(FC0):
                bk = 2 + f % 2
                for c in range(DC):
                    m = q.op("pe", lambda i, b=b, f=f, c=c, bk=bk: PE.matmul(bank[bk], W1[b][:, c, f * P:(f + 1) * P], GT[b][:, c, :], start=c == 0, stop=c == DC - 1),
                             w, gt, q.names.get("hid%d" % (f % 2)) or prev("hid%d" % (f % 2)), inc=c == DC - 1, name="GT_read%d" % b)
                m = q.op("act", lambda i, b=b, f=f, bk=bk: A.activation(hT[b][:, f, :], bank[bk], ACT.Gelu_apprx_tanh, bias=b1[:, bass.ds((2 * i + b) * FC0 + f, 1)], scale=1.0),
                         m, w_in, prev("hT_read%d" % b), name="hid%d" % (f % 2))
            for t in range(CT0):
                bk = 4 + t % 2
                for f in range(FC0):
                    m2 = q.op("pe", lambda i, b=b, t=t, f=f, bk=bk: PE.matmul(bank[bk][:, 0:D], hT[b][:, f, t * P:(t + 1) * P], W2[b][:, f, :], start=f == 0, stop=f == FC0 - 1),
                              m if f == FC0 - 1 else q.names["hid%d" % (f % 2)], q.names.get("up%d" % (t % 2)) or prev("up%d" % (t % 2)), inc=f == FC0 - 1, name="hT_read%d" % b)
                q.names["W_read%d" % b] = m2
                a = q.op("dve", lambda i, b=b, t=t, bk=bk: V.tensor_tensor(wv[t % 2], bank[bk][:, 0:D], b2[:, bass.ds((2 * i + b) * D, D)], ALU.add), m2,
                         q.names.get("wv_read%d" % (t % 2)) or prev("wv_read%d" % (t % 2)), name="up%d" % (t % 2))
                a = q.op("dve", lambda i, b=b, t=t: V.tensor_scalar(wv[t % 2], wv[t % 2], wcol[b][:, t:t + 1], None, ALU.mult), a, wc, name="wcol_read%d" % b)
                bm = 6 + t % 2
                m3 = q.op("pe", lambda i, b=b, t=t, bm=bm: PE.matmul(bank[bm][:, 0:D], same[b][:, t, :], wv[t % 2], start=True, stop=True), a,
                          q.names.get("mg%d" % (t % 2)) or prev("mg%d" % (t % 2)), name="wv_read%d" % (t % 2))
                q.names["same_read%d" % b] = m3
                a = q.op("dve", lambda i, b=b, t=t, bm=bm: V.tensor_copy(merged[b][:, t, :], bank[bm][:, 0:D]), m3, prev("stored%d" % b), name="mg%d" % (t % 2))
                q.dma("pool", "d_sc%d" % b, lambda i, b=b, t=t: G.indirect_dma_start(acc_d, bass.IndirectOffsetOnAxis(ap=sidx[b][:, t:t + 1], axis=0), merged[b][:, t, :], None,
                                                                           compute_op=ALU.add, bounds_check=B * S - 1, oob_is_err=False),
                      a, found, acc_in, q.names.get("stored") or prev("stored"), name="stored")
            q.names["stored%d" % b] = q.names["stored"]
        q.flush(E0 // 2)
        q.barrier()
    norm_from_acc()
    if phases <= 3:
        return finish(q, out, X, SP)

    def many_heads(ph, hd, names, rope):
        gh = P // hd
        ng = H1 // gh
        n_out = H1 * hd
        buf = Buffers(ph)
        Wq, Wk, Wv = (sb("W" + n, [P, DC, n_out], where=ph) for n in "qkv")
        Wo = sb("Wo", [P, ng, D], where=ph)
        mask = sb("mask", [P, gh], where=ph)
        bo = sb("bo", [P, D], where=ph)
        bqkv = sb("bqkv", [P, 3, ng], where=ph) if rope else None
        qT = sb("qT", [P, S], where=ph)
        Qm = [sb("Qm%d" % k, [P, gh, S], where=ph) for k in range(2)]
        kT = [sb("kT%d" % k, [P, S], where=ph) for k in range(2)]
        Vm = sb("Vm", [P, TB, H1, P], where=ph)
        attT = sb("attT", [P, ng, S], where=ph)
        for dst, n in ((Wq, names[0]), (Wk, names[1]), (Wv, names[2]), (Wo, names[3]), (mask, "mask%d" % hd)):
            w_in = q.dma("act", "d_w0", lambda i, dst=dst, n=n: A.dma_start(dst, T[n]))
        w_in = q.dma("act", "d_w0", lambda i: A.dma_start(bo, bass.AP(T[names[4]].tensor, 0, [[0, P], [1, D]])))
        if rope:
            w_in = q.dma("act", "d_w0", lambda i: A.dma_start(bqkv, T["bqkv"]))
            cs = sb("cs", [P, 2, S], where=ph)
            turned = sb("turned", [P, DC, S], where=ph)
            part = sb("part", [P, DC, S], where=ph)
            w_in = q.dma("act", "d_w0", lambda i: A.dma_start(cs, T["cs"]))
        else:
            ctxT = sb("ctxT1", [P, DC, S], where=ph)
        zeroed = q.op("pool", lambda i: G.memset(Vm, 0.0))
        q.flush()

        x_ready = take_batch(w_in)
        x_ready.append(w_in)
        if rope:
            for c in range(DC):
                a = q.op("dve", lambda i, c=c: V.tensor_tensor(turned[:, c, :], xT[:, 0, :], cs[:, c, :], ALU.mult), x_ready, prev("src_read"))
                b = q.op("pool", lambda i, c=c: G.tensor_tensor(part[:, c, :], xT[:, 1, :], cs[:, 1 - c, :], ALU.mult), x_ready, prev("turned%d" % c), plain=True, name="xT_read")
                m = q.op("dve", lambda i, c=c: V.tensor_tensor(turned[:, c, :], turned[:, c, :], part[:, c, :], ALU.add if c else ALU.subtract), a, b, name="turned%d" % c)
            x_ready = k_ready = [m, q.names["turned0"]]
            src, ksrc = turned, turned
        else:
            k_ready = q.dma("sp", "d_ctx", lambda i: SP.dma_start(ctxT, T["ctxT"][bass.ds(i, 1)].rearrange("a p c s -> p (a c) s")), prev("K%d_in" % (ng - 1)))
            src, ksrc = xT, ctxT
        free, ready = {}, {}

        def project_q(g):
            m = project(Wq, src, g, qT, bqkv[:, 0, g:g + 1] if rope else None, hd ** -0.5, x_ready, q.names.get("masked") or prev("masked"), "qT", "dve")
            for k in range(gh):
                n = q.op("pool", lambda i, g=g, k=k: G.tensor_scalar(Qm[g % 2][:, k, :], qT, mask[:, k:k + 1], None, ALU.mult), m, w_in,
                         free.get(g - 2) or prev("Q_free%d" % (g % 2)), name="masked", plain=True)
                ready["q", g, k] = n

        def project_k(g):
            ready["k", g] = project(Wk, ksrc, g, kT[g % 2], bqkv[:, 1, g:g + 1] if rope else None, 1.0, k_ready, free.get(g - 2) or prev("Q_free%d" % (g % 2)), "K%d" % g, "act")

        project_q(0)
        project_k(0)
        q.names["src_read"] = q.names["K0_in"]
        N = min(n_out, 512)
        hn = N // hd
        x = 0
        for t in range(TB):
            for n in range(n_out // N):
                for c in range(DC):
                    m = q.op("pe", lambda i, t=t, n=n, c=c, x=x: PE.matmul(bank[O_BANKS[x % 2]][:, 0:N], ksrc[:, c, t * P:(t + 1) * P], Wv[:, c, n * N:(n + 1) * N], start=c == 0, stop=c == DC - 1),
                             k_ready, w_in, ready.get(("V", x - 2)) or prev("O_free%d" % (x % 2)), inc=c == DC - 1)
                head0 = Vm[:, t, n * hn:(n + 1) * hn, :]
                dst = bass.AP(head0.tensor, head0.offset, [head0.ap[0], [gh * P, hn // gh], [P + hd, gh], [1, hd]])
                psv = bank[O_BANKS[x % 2]][:, 0:N].rearrange("p (g h d) -> p g h d", h=gh, d=hd)
                if x % 2:
                    m = q.op("act", lambda i, dst=dst, psv=psv: A.activation(dst, psv, ACT.Copy), m, zeroed, prev("pv_any"))
                else:
                    m = q.op("dve", lambda i, dst=dst, psv=psv: V.tensor_copy(dst, psv), m, zeroed, prev("pv_any"))
                ready["V", x] = m
                x += 1
        v_ready = [ready["V", x - 1], ready["V", x - 2]]
        steps = gh * TB

        def before(s):
            g, r = divmod(s, steps)
            if g + 1 < ng and r == 1:
                project_q(g + 1)
            if g + 1 < ng and r == 4:
                project_k(g + 1)

        def scores1(h, j):
            g, k = divmod(h, gh)
            return [(Qm[g % 2][:, k, j * P:(j + 1) * P], kT[g % 2])], [ready["q", g, k], ready["k", g]]

        def values1(h, kt):
            g, k = divmod(h, gh)
            wait = list(v_ready)
            if (g - 2) in out_of:
                wait.append(out_of[g - 2])
            return [(Vm[:, kt, h, :], O_BANKS[g % 2], k == 0 and kt == 0, k == gh - 1 and kt == TB - 1)], wait

        out_of = {}

        def after1(h, m):
            g, k = divmod(h, gh)
            if k == gh - 1:
                bias = bqkv[:, 2, g:g + 1] if rope else 0.0
                out_of[g] = q.op("dve", lambda i: V.tensor_scalar(attT[:, g, :], bank[O_BANKS[g % 2]], bias, None, ALU.add), m, prev("att_read"), name="O_free%d" % (g % 2))

        def scores_mark(h, j):
            g, k = divmod(h, gh)
            if k == 0 and j == 0 and g:
                free[g - 1] = Mark("pe", q.count["pe"], q.section)
            return scores1(h, j)

        done = attend(buf, scores_mark, values1, H1, before=before, after=after1)
        free[ng - 1] = done["scores", H1 - 1]
        q.names["Q_free0"], q.names["Q_free1"] = (free[ng - 2], free[ng - 1]) if ng % 2 == 0 else (free[ng - 1], free[ng - 2])
        if not rope:
            q.names["xT_read"] = q.names["qT_in"]
        else:
            q.names["src_read"] = q.names["K%d_in" % (ng - 1)]
        for t in range(TB):
            bk = bank[S_BANKS[t // 2]][:, (t % 2) * D:(t % 2 + 1) * D]
            for g in range(ng):
                m = q.op("pe", lambda i, t=t, g=g, bk=bk: PE.matmul(bk, attT[:, g, t * P:(t + 1) * P], Wo[:, g, :], start=g == 0, stop=g == ng - 1),
                         list(out_of.values()), done["exp", 4 * H1 - 1], inc=g == ng - 1, name="att_read")
            if t % 2:
                for v in (t - 1, t):
                    last = norm_tile(v, bank[S_BANKS[t // 2]][:, (v % 2) * D:(v % 2 + 1) * D], m, extra=bo)
                q.names["exp%d" % (t // 2)] = last[0]
        norm_batch(last[1], to_X)
        q.flush(B)
        q.barrier()

    with ExitStack() as ph:
        many_heads(ph, D // H1, ("Wq1", "Wk1", "Wv1", "Wo1", "bo1"), True)
    if phases <= 4:
        return finish(q, out, X, SP)
    with ExitStack() as ph:
        many_heads(ph, 64, ("Wq2", "Wk2", "Wv2", "Wo2", "bo2"), False)
    if phases <= 5:
        return finish(q, out, X, SP)

    with ExitStack() as ph:
        gidx_all = sb("gidx_all", [P, (E1 + 2) * CT1], i32, where=ph)
        sidx_all = sb("sidx_all", [P, E1 * CT1], i32, where=ph)
        slot_w = sb("slot_w", [P, E1 * CT1], where=ph)
        with ExitStack() as route:
            TE = [P, NT, E1]
            gw = sb("gw", [P, DC, E1], where=route)
            L = sb("L", TE, where=route)
            shifted = sb("shifted", TE, where=route)
            left = sb("left", TE, where=route)
            chosen = sb("chosen", TE, where=route)
            weight = sb("weight", TE, where=route)
            top = sb("top", [P, NT, 8], where=route)
            cols = sb("cols", [P, 3, NT], where=route)
            marks16 = sb("marks16", TE, bf16, where=route)
            before16 = sb("before16", TE, bf16, where=route)
            tri = sb("tri", [P, 2, P], bf16, where=route)
            keep = sb("keep", TE, where=route)
            place = sb("place", TE, i32, where=route)
            hi_i = sb("hi_i", TE, i32, where=route)
            lo_i = sb("lo_i", TE, i32, where=route)
            hi = sb("hi", TE, where=route)
            lo = sb("lo", TE, where=route)
            ramp = sb("ramp", [P, 32], where=route)
            token1 = sb("token1", [P, NT], where=route)
            A_ = [sb("A%d" % b, [P, NT, 8, 16], where=route) for b in range(2)]
            B_ = [sb("B%d" % b, [P, NT, 8, 16], where=route) for b in range(2)]
            BV = [sb("BV%d" % b, [P, NT, 2, 128], where=route) for b in range(2)]
            diag = sb("diag", [P, 8], where=route)
            cross = sb("cross", [P, 2, 8, 16], where=route)
            slots = sb("slots", [P, 4, 2, 16], where=route)
            slot_rows = sb("slot_rows", [E1 * CT1, 2, P], where=route)
            slot_n = sb("slot_n", [P, 2, E1 * CT1], where=route)
            for dst, n in ((gw, "gw"), (tri, "tri"), (ramp, "ramp"), (token1, "token1"), (diag, "diag")):
                w_in = q.dma("act", "d_w0", lambda i, dst=dst, n=n: A.dma_start(dst, T[n]))
            acc_in = q.dma("pool", "d_sc0", lambda i: G.dma_start(acc_d.rearrange("(t p) d -> p t d", p=P), X))
            rows_in = q.dma("pool", "d_sc1", lambda i: G.dma_start(rows_d.rearrange("(t p) d -> p t d", p=P)[:, :, 0:D], X))
            q.flush()
            x_ready = take_batch()
            for t in range(TB):
                for c in range(DC):
                    m = q.op("pe", lambda i, t=t, c=c: PE.matmul(bank[2][:, t * E1:(t + 1) * E1], xT[:, c, t * P:(t + 1) * P], gw[:, c, :], start=c == 0, stop=c == DC - 1),
                             x_ready, w_in, prev("logits"), name="xT_read")
            q.op("dve", lambda i: V.tensor_copy(L[:, bass.ds(i * TB, TB), :].rearrange("p t e -> p (t e)"), bank[2][:, 0:TB * E1]), m, name="logits")
            q.names["summed_all"] = q.names["logits"]
            q.flush(B)
            q.barrier()

            def every(ap, n):
                return bass.AP(ap.tensor, ap.offset, [*ap.ap, [0, n]])

            m = q.op("dve", lambda i: V.tensor_reduce(cols[:, 0, :], L, AX.X, ALU.max))
            m = q.op("dve", lambda i: V.tensor_tensor(shifted, L, every(cols[:, 0, :], E1), ALU.subtract), m)
            m_exp = q.op("act", lambda i: A.activation(shifted, shifted, ACT.Exp), m)
            for t in range(NT):
                m = q.op("dve", lambda i, t=t: V.max(top[:, t, :], L[:, t, :]))
            for t in range(NT):
                m2 = q.op("dve", lambda i, t=t: V.match_replace(left[:, t, :], top[:, t, :], L[:, t, :], -3e38), m)
            m = q.op("dve", lambda i: V.tensor_tensor(chosen, left, L, ALU.not_equal), m2)
            c16 = q.op("act", lambda i: A.activation(marks16, chosen, ACT.Copy), m)
            w = q.op("dve", lambda i: V.tensor_tensor(weight, shifted, chosen, ALU.mult), m, m_exp)
            w = q.op("dve", lambda i: V.tensor_reduce(cols[:, 1, :], weight, AX.X, ALU.add), w)
            w = q.op("dve", lambda i: V.reciprocal(cols[:, 2, :], cols[:, 1, :]), w)
            w = q.op("dve", lambda i: V.tensor_tensor(weight, weight, every(cols[:, 2, :], E1), ALU.mult), w)
            r = q.op("pool", lambda i: G.memset(before16[:, 0, :], 0.0))
            for t in range(1, NT):
                r = q.op("pool", lambda i, t=t: G.tensor_tensor(before16[:, t, :], before16[:, t - 1, :], marks16[:, t - 1, :], ALU.add), r, c16)
            for t in range(NT):
                q.op("pe", lambda i, t=t: PE.matmul(bank[0][:, t * E1:(t + 1) * E1], tri[:, 0, :], marks16[:, t, :], start=True, stop=False), c16, w_in, inc=False)
                n = q.op("pe", lambda i, t=t: PE.matmul(bank[0][:, t * E1:(t + 1) * E1], tri[:, 1, :], before16[:, t, :], start=False, stop=True), r)
            upto = bank[0].rearrange("p (t e) -> p t e", e=E1)
            k = q.op("dve", lambda i: V.scalar_tensor_tensor(keep, upto, float(CAP), chosen, ALU.is_le, ALU.mult), n, m)
            n = q.op("dve", lambda i: V.tensor_scalar(place, upto, -1.0, None, ALU.add), n)
            a = q.op("dve", lambda i: V.tensor_scalar(hi_i, place, 4, None, ALU.arith_shift_right), n)
            b = q.op("dve", lambda i: V.tensor_scalar(lo_i, place, 15, None, ALU.bitwise_and), n)
            a = q.op("dve", lambda i: V.tensor_copy(hi, hi_i), a)
            b = q.op("dve", lambda i: V.tensor_copy(lo, lo_i), b)
            a = q.op("dve", lambda i: V.scalar_tensor_tensor(hi, hi, 1.0, keep, ALU.add, ALU.mult), a, k)
            read, free = {}, {}
            for g in range(4):
                e8 = slice(g * 8, g * 8 + 8)
                z = g % 2

                def along(ap):
                    return bass.AP(ap.tensor, ap.offset, [ap.ap[0], [0, NT], [0, 8], [1, 16]])

                def per_tile(ap):
                    return bass.AP(ap.tensor, ap.offset, [*ap.ap, [0, 8], [0, 16]])

                def value(v, z=z):
                    ap = BV[z][:, :, v, :]
                    return ap.rearrange("p t (e j) -> p t e j", j=16)

                qa = q.op("dve", lambda i, e8=e8, z=z: V.tensor_tensor(A_[z], every(hi[:, :, e8], 16), along(ramp[:, 0:16]), ALU.is_equal), a, read.get(g - 2), w_in)
                qb = q.op("dve", lambda i, e8=e8, z=z: V.tensor_tensor(B_[z], every(lo[:, :, e8], 16), along(ramp[:, 16:32]), ALU.is_equal), b, free.get(g - 2), w_in)
                qc = q.op("pool", lambda i, z=z, value=value: G.tensor_tensor(value(0), B_[z], per_tile(token1), ALU.mult), qb, read.get(g - 2))
                qd = q.op("dve", lambda i, e8=e8, z=z, value=value: V.tensor_tensor(value(1), B_[z], every(weight[:, :, e8], 16), ALU.mult), qb, w, read.get(g - 2))
                free[g] = [qc, qd]
                for t in range(NT):
                    n = q.op("pe", lambda i, t=t, z=z: PE.matmul(bank[1 + z][:, 0:256], A_[z][:, t, :, :].rearrange("p e j -> p (e j)"), BV[z][:, t, :, :].rearrange("p v j -> p (v j)"),
                                                               start=t == 0, stop=t == NT - 1), qa, qc, qd, free.get(("bank", z)), inc=t == NT - 1)
                read[g] = n
                ps = bank[1 + z][:, 0:256].rearrange("p (v x) -> p v x", v=2).rearrange("p v (e j) -> p v e j", j=16)
                on = bass.AP(diag.tensor, diag.offset, [diag.ap[0], [0, 2], [1, 8], [0, 16]])
                n = q.op("dve", lambda i, ps=ps, on=on: V.tensor_tensor(cross, ps, on, ALU.mult), n, free.get("cross"))
                free["bank", z] = n
                n = q.op("dve", lambda i, g=g: V.tensor_reduce(slots[:, g, :, :], cross.rearrange("p v e j -> p v j e"), AX.X, ALU.add), n)
                free["cross"] = n
                for v in range(2):
                    d = q.dma("sp", "d_slot", lambda i, g=g, v=v: SP.dma_start(slot_d[v, g * 2048:(g + 1) * 2048].rearrange("(p j) -> p j", j=16), slots[:, g, v, :]), n)
            d = q.dma("sp", "d_slot", lambda i: SP.dma_start(slot_rows, slot_d.rearrange("v (r c) -> r v c", c=P)), d)
            for v in range(2):
                n = q.op("pe", lambda i, v=v: PE.transpose(bank[3][:, v * 64:(v + 1) * 64], slot_rows[:, v, :], ident[0:64, 0:64]), d)
            n = q.op("dve", lambda i: V.tensor_copy(slot_n.rearrange("p v r -> p (v r)"), bank[3][:, 0:128]), n)
            kept = q.op("dve", lambda i: V.tensor_copy(slot_w, slot_n[:, 1, :]), n)
            q.op("dve", lambda i: V.tensor_scalar(gidx_all[:, 0:E1 * CT1], slot_n[:, 0, :], -1.0, 0.0, ALU.add, ALU.max), n)
            m = q.op("dve", lambda i: V.tensor_scalar(slot_n[:, 1, :], slot_n[:, 0, :], 0.5, float(1 << 16), ALU.is_lt, ALU.mult), kept)
            q.op("dve", lambda i: V.scalar_tensor_tensor(sidx_all, slot_n[:, 0, :], -1.0, slot_n[:, 1, :], ALU.add, ALU.add), m)
            q.op("dve", lambda i: V.memset(gidx_all[:, E1 * CT1:], 0))
            q.barrier()

        Wgu = [sb("Wgu%d" % b, [P, DC, 2 * F1], where=ph) for b in range(2)]
        Wdn = [sb("Wdn%d" % b, [FH, 2, D], where=ph) for b in range(2)]
        gidx = [sb("gidx%d" % b, [P, CT1], i32, where=ph) for b in range(2)]
        sidx1 = [sb("sidx1_%d" % b, [P, CT1], i32, where=ph) for b in range(2)]
        rows1 = [sb("rows1_%d" % b, [P, CT1, GW], where=ph) for b in range(2)]
        RT = [sb("RT%d" % b, [P, DC, CAP], where=ph) for b in range(2)]
        act1 = [sb("act1_%d" % b, [FH, 2, CAP], where=ph) for b in range(2)]
        h1 = [sb("h1_%d" % b, [FH, 2, CAP], where=ph) for b in range(2)]
        res = [sb("res%d" % b, [P, CT1, D], where=ph) for b in range(2)]

        def gather1(i, b, rows_free):
            m = q.op("pool", lambda _, b=b, i=i: G.tensor_copy(gidx[b], gidx_all[:, i(_, b)]), rows_free, q.names.get("gathered%d" % b))
            for t in range(CT1):
                q.dma("pool", "d_g%d" % b, lambda _, b=b, t=t: G.indirect_dma_start(rows1[b][:, t, :], None, rows_d, bass.IndirectOffsetOnAxis(ap=gidx[b][:, t:t + 1], axis=0)),
                      m, rows_free, name="gathered%d" % b)

        for b in range(2):
            gather1(lambda _, b: slice(b * CT1, (b + 1) * CT1), b, None)
        q.flush()
        for b in range(2):
            w = q.dma("sp", "d_e%d" % b, lambda i, b=b: SP.dma_start(Wgu[b], T["Wgu"][bass.ds(2 * i + b, 1)].rearrange("a p c f -> p (a c) f")), prev("W_read%d" % b))
            w = q.dma("sp", "d_e%d" % b, lambda i, b=b: SP.dma_start(Wdn[b], T["Wdn"][bass.ds(2 * i + b, 1)].rearrange("a p c f -> p (a c) f")), prev("W_read%d" % b))
        for b in range(2):
            g = prev("gathered%d" % b)
            w = Mark("d_e%d" % b, q.count["d_e%d" % b], q.section)
            for c in range(DC):
                for t in range(CT1):
                    m = q.op("pe", lambda i, b=b, t=t, c=c: PE.transpose(bank[b][:, c * CAP + t * P:c * CAP + (t + 1) * P], rows1[b][:, t, c * P:(c + 1) * P], ident),
                             g, prev("RT%d" % b), inc=t == CT1 - 1, name="rows_read%d" % b)
            gather1(lambda i, b: bass.ds((2 * i + b + 2) * CT1, CT1), b, m)
            rt = q.op("act", lambda i, b=b: A.activation(RT[b].rearrange("p c s -> p (c s)"), bank[b], ACT.Copy), m, prev("RT_read%d" % b), name="RT%d" % b)
            for half in range(2):
                for f in range(2):
                    for c in range(DC):
                        m = q.op("pe", lambda i, b=b, half=half, f=f, c=c: PE.matmul(bank[2 + 2 * b + half][0:FH, f * CAP:(f + 1) * CAP],
                                                                             Wgu[b][:, c, half * F1 + f * FH:half * F1 + (f + 1) * FH], RT[b][:, c, :], start=c == 0, stop=c == DC - 1),
                                 w, rt, prev("act1_%d" % b) if half == 0 else prev("h1_%d" % b), inc=c == DC - 1, name="RT_read%d" % b)
                if half == 0:
                    s_ = q.op("act", lambda i, b=b: A.activation(act1[b].rearrange("p c s -> p (c s)"), bank[2 + 2 * b][0:FH, :], ACT.Silu), m, prev("h1_%d" % b), name="act1_%d" % b)
            h = q.op("dve", lambda i, b=b: V.tensor_tensor(h1[b].rearrange("p c s -> p (c s)"), bank[3 + 2 * b][0:FH, :], act1[b].rearrange("p c s -> p (c s)"), ALU.mult), m, s_, prev("h_read%d" % b), name="h1_%d" % b)
            for t in range(CT1):
                for f in range(2):
                    m = q.op("pe", lambda i, b=b, t=t, f=f: PE.matmul(bank[6 + b][:, t * D:(t + 1) * D], h1[b][:, f, t * P:(t + 1) * P], Wdn[b][:, f, :], start=f == 0, stop=f == 1),
                             h, w, prev("res%d" % b), inc=f == 1, name="h_read%d" % b)
            q.names["W_read%d" % b] = m
            c_ = q.op("pool", lambda i, b=b: G.tensor_copy(sidx1[b], sidx_all[:, bass.ds((2 * i + b) * CT1, CT1)]), prev("stored%d" % b))
            for t in range(CT1):
                r = q.op("dve", lambda i, b=b, t=t: V.tensor_scalar(res[b][:, t, :], bank[6 + b][:, t * D:(t + 1) * D], slot_w[:, bass.ds((2 * i + b) * CT1 + t, 1)], None, ALU.mult),
                         m, prev("stored%d" % b), name="res%d" % b)
            last = q.names["stored0"] if b else prev("stored1")
            for t in range(CT1):
                q.dma("pool", "d_sc%d" % b, lambda i, b=b, t=t: G.indirect_dma_start(acc_d, bass.IndirectOffsetOnAxis(ap=sidx1[b][:, t:t + 1], axis=0), res[b][:, t, :], None,
                                                                            compute_op=ALU.add, bounds_check=B * S - 1, oob_is_err=False),
                      r, c_, last, name="stored%d" % b)
        q.flush(E1 // 2)
        q.barrier()
    norm_from_acc()
    return finish(q, out, X, SP)


def finish(q, out, X, SP):
    q.dma("sp", "d_out", lambda i: SP.dma_start(out.rearrange("(t p) d -> p t d", p=P), X))
    q.barrier()


def constants():
    k = np.abs(np.fft.fftfreq(D)).astype(np.float32) + np.float32(1e-8)
    n = np.arange(D)
    rows, freq = [], []
    for j in range(D // 2 + 1):
        w = np.sqrt((1.0 if j in (0, D // 2) else 2.0) / D)
        rows.append(w * np.cos(2 * np.pi * ((j * n) % D) / D)); freq.append(j)
        if j not in (0, D // 2):
            rows.append(w * np.sin(2 * np.pi * ((j * n) % D) / D)); freq.append(j)
    basis = np.array(rows, np.float32)
    ka = k[np.array(freq)]
    kc = ka.reshape(DC, P).T
    kcols = np.concatenate([kc, kc * kc], 1)
    lx = np.log(np.array(FRACTAL, np.float64))
    den = 5 * np.sum(lx * lx) - np.sum(lx) ** 2
    weights = -(5 * lx - np.sum(lx)) / den
    sizes = np.array([s * s for s in FRACTAL])
    fmask = (np.arange(1024)[None, :] < sizes[:, None]).astype(np.float32)
    fconst = np.concatenate([np.repeat(weights[:, None], P, 1), 1.0 / sizes[:, None]], 1).astype(np.float32)
    A12 = np.array([[1, 1, 1, 0, 1, 1, 1, 0, 0, 0, 1, 1], [1, 1, 0, 1, 1, 1, 0, 0, 0, 1, 1, 0], [1, 0, 1, 1, 1, 0, 0, 0, 1, 1, 0, 1],
                    [0, 1, 1, 1, 0, 0, 0, 1, 1, 0, 1, 1], [0, 0, 0, 0, 1, 1, 1, 1, 1, 1, 1, 1], [1, 1, 1, 1, 0, 0, 0, 0, 0, 0, 0, 0],
                    [0, 0, 0, 0, 1, 1, 1, 1, 0, 0, 0, 0], [1, 1, 0, 0, 1, 1, 0, 0, 1, 1, 0, 0], [1, 0, 1, 0, 1, 0, 1, 0, 1, 0, 1, 0],
                    [0, 1, 0, 1, 0, 1, 0, 1, 0, 1, 0, 1], [1, 0, 0, 1, 1, 0, 0, 1, 1, 0, 0, 1], [0, 1, 1, 0, 0, 1, 1, 0, 0, 1, 1, 0]], np.float32)
    Hm = np.concatenate([A12.T, np.eye(12, dtype=np.float32)], axis=1)
    golay = np.zeros((24, 48), np.float32)
    golay[:, 0:12] = Hm.T
    golay[0:12, 24:48] = 1.0
    sel = np.zeros((2, 10), np.float32)
    sel[0, 0:5] = 1.0
    sel[1, 5:10] = 1.0
    lower = np.tril(np.ones((P, P), np.float32), -1)
    freq = np.exp(np.arange(0, D, 2, dtype=np.float32) * np.float32(-np.log(10000.0) / D))
    ang = (np.arange(S, dtype=np.float32)[:, None] * freq[None, :]).astype(np.float32)
    cs = np.stack([np.cos(ang).T, np.sin(ang).T], 1).astype(np.float32)
    masks = {"mask%d" % hd: (np.arange(P)[:, None] // hd == np.arange(P // hd)[None, :]).astype(np.float32) for hd in (16, 64)}
    tri = np.stack([np.triu(np.ones((P, P))), np.ones((P, P))], 1).astype(mybir.dt.np(bf16))
    ramp = np.concatenate([np.arange(1, 17), np.arange(16)]).astype(np.float32)[None].repeat(P, 0)
    token1 = (np.arange(P)[:, None] + P * np.arange(NT)[None, :] + 1).astype(np.float32)
    diag = (np.arange(P)[:, None] // 16 == np.arange(8)[None, :]).astype(np.float32)
    return {"tri": tri, "ramp": ramp, "token1": token1, "diag": diag, "lower": lower, "cs": cs, **masks, "ident": np.eye(P, dtype=np.float32), "basis": basis.reshape(DC, P, D).transpose(1, 0, 2), "kcols": kcols.astype(np.float32),
            "fmask": fmask, "fconst": fconst, "golay": golay, "sel": sel}


def chunks(w):
    return w.reshape(w.shape[0] // P, P, *w.shape[1:]).swapaxes(0, 1)


def layout(x, **w):
    a = constants()
    a["x"] = x.reshape(B * S, D)
    a["W_el"] = chunks(w["L0_attn_W_el"])
    a["W_le"] = np.concatenate([w["L0_attn_W_le"], w["L0_attn_b_le"][None]], 0)
    a["b_el"] = w["L0_attn_b_el"][:, None]
    g = "L0_xattn_"
    for n in ("Wq_c", "Wk_s", "Wv_s", "Wq_s", "Wk_c", "Wv_c", "Wg"):
        a[n] = chunks(w[g + n].T)
    a["bias0"] = np.stack([w[g + n].reshape(DC, P).T for n in ("bq_c", "bk_s", "bv_s", "bq_s", "bk_c", "bv_c", "bg")], 1)
    a["ctxT"] = w["ctx_1024"].reshape(B, S, DC, P).transpose(0, 3, 2, 1)
    g = "L0_ffn_"
    a["W1"] = w[g + "W1"].reshape(E0, DC, P, F0).transpose(0, 2, 1, 3)
    a["W2"] = w[g + "W2"].reshape(E0, FC0, P, D).transpose(0, 2, 1, 3)
    a["b1"] = w[g + "b1"].reshape(E0 * FC0, P).T
    a["b2"] = w[g + "b2"]
    tok = w[g + "top_idx"].T
    a["tok"] = tok
    a["idx"] = tok.reshape(E0 * CT0, P).T
    a["combine"] = w[g + "combine_weights"]
    g = "L1_attn_"
    for n in ("Wq", "Wk", "Wv", "Wo"):
        a[n + "1"] = chunks(w[g + n].T)
    a["bqkv"] = np.stack([w[g + n].reshape(DC, P).T for n in ("bq", "bk", "bv")], 1)
    a["bo1"] = w[g + "bo"][None]
    g = "L1_xattn_"
    for n in ("Wq", "Wk", "Wv", "Wo"):
        a[n + "2"] = chunks(w[g + n])
    a["bo2"] = w[g + "bo"][None]
    g = "L1_ffn_"
    a["gw"] = chunks(w[g + "gate_weight"].T)
    a["Wgu"] = w[g + "gate_up_proj"].reshape(E1, 2 * F1, DC, P).transpose(0, 3, 2, 1)
    a["Wdn"] = w[g + "down_proj"].reshape(E1, D, 2, FH).transpose(0, 3, 2, 1)
    return {k: np.ascontiguousarray(v) for k, v in a.items()}


def kernel(**inputs):
    from concourse import bacc
    from concourse.bass_utils import run_bass_kernel_spmd

    arrays = layout(**{k: np.asarray(v) for k, v in inputs.items()})
    nc = bacc.Bacc("TRN2", target_bir_lowering=False, num_devices=1)
    T = {k: nc.dram_tensor("in_" + k, v.shape, mybir.dt.from_np(v.dtype), kind="ExternalInput").ap() for k, v in arrays.items()}
    out = nc.dram_tensor("out_0", (B * S, D), f32, kind="ExternalOutput").ap()
    program(nc, T, out)
    r = run_bass_kernel_spmd(nc, [{"in_" + k: v for k, v in arrays.items()}], core_ids=[0])
    return r.results[0]["out_0"].reshape(B, S, D)
```

```python
from contextlib import ExitStack

import numpy as np
import concourse.bass as bass
from concourse import mybir

f32, f32r, bf16, i32 = mybir.dt.float32, mybir.dt.float32r, mybir.dt.bfloat16, mybir.dt.int32
ACT = mybir.ActivationFunctionType
ALU = mybir.AluOpType
AX = mybir.AxisListType

P = 128
B, S, D = 4, 512, 256
NT = B * S // P
TB = S // P
DC = D // P
EPS = 1e-5
E0, C0, F0 = 8, 512, 1024
FC0, CT0 = F0 // P, C0 // P
H1 = 16
E1, F1, CAP, TOPK = 32, 192, 256, 8
FH = F1 // 2
CT1 = CAP // P
GW = D + E0
FRACTAL = (2, 4, 8, 16, 32)
CREDIT = 1024


class Mark:

    def __init__(self, sem, k, section):
        self.sem, self.k, self.section = sem, k, section


class prev:

    def __init__(self, name):
        self.name = name


class Queue:

    def __init__(self, nc, ctx):
        self.nc, self.ctx = nc, ctx
        self.eng = {"pe": nc.tensor, "dve": nc.vector, "act": nc.scalar, "pool": nc.gpsimd, "sp": nc.sync}
        self.sems, self.base = {}, {}
        self.fence = ctx.enter_context(nc.semaphore("s_fence"))
        for e in ("pe", "dve", "act", "pool"):
            self._sem(e)
        self.section, self.ops, self.count, self.names, self.past = 0, [], {}, {}, {}

    def _sem(self, name, credit=CREDIT):
        if name not in self.sems:
            self.sems[name] = self.ctx.enter_context(self.nc.semaphore("s_" + name))
            self.base[name] = credit
            if credit:
                self.nc.sync.sem_inc(self.sems[name], credit)

    def _add(self, e, sem, by, fn, after, name, plain=False):
        mark = None
        if sem:
            self.count[sem] = self.count.get(sem, 0) + by
            mark = Mark(sem, self.count[sem], self.section)
            if name:
                self.names[name] = mark
        flat, rest = [], list(after)
        while rest:
            a = rest.pop(0)
            if isinstance(a, (list, tuple)):
                rest += a
            else:
                flat.append(a)
        self.ops.append((e, sem, by, fn, [a for a in flat if a is not None], plain))
        return mark

    def op(self, e, fn, *after, name=None, inc=True, plain=False):
        return self._add(e, e if inc else None, 1, fn, after, name, plain)

    def dma(self, e, stream, fn, *after, name=None):
        self._sem(stream, 0 if e == "pool" else CREDIT)
        return self._add(e, stream, 16, fn, after, name, plain=e != "act")

    def _value(self, mark, n):
        base, per, times = self.past[mark.section]
        return base[mark.sem] + (times - 1) * per.get(mark.sem, 0) + mark.k

    def flush(self, n=None):
        ops, per, base = self.ops, self.count, dict(self.base)
        names, me, eng = self.names, self.section, self.eng
        outer, todo = {}, []
        for e, sem, by, fn, after, plain in ops:
            waits = []
            for a in after:
                lag = isinstance(a, prev)
                if lag and n is None:
                    continue
                a = names[a.name] if lag else a
                for mark in a if isinstance(a, list) else [a]:
                    if mark.section == me:
                        waits.append((mark.sem, mark.k - lag * per[mark.sem]))
                        assert base[mark.sem] + waits[-1][1] > 0, (mark.sem, mark.k)
                    else:
                        outer[e, mark.sem] = max(outer.get((e, mark.sem), 0), self._value(mark, n))
            todo.append((e, sem, by, fn, waits, plain))
        for (e, s), v in outer.items():
            eng[e].wait_ge(self.sems[s], v)

        def emit(i):
            at, seen = {}, {}
            for e, sem, by, fn, waits, plain in todo:
                need = {}
                for s, k in waits:
                    need[s] = max(k, need.get(s, k))
                for s in need if n is not None else ():
                    if (e, s) not in at:
                        at[e, s] = eng[e].snap(i * per[s] + base[s])
                for s, k in need.items():
                    if seen.get((e, s), -1 << 30) >= k:
                        continue
                    seen[e, s] = k
                    if n is None:
                        eng[e].wait_ge(self.sems[s], base[s] + k)
                    else:
                        eng[e].wait_ge(self.sems[s], at[e, s] + k)
                        if plain:
                            eng[e].sem_inc(self.fence, 1)
                ins = fn(i)
                if sem:
                    ins.then_inc(self.sems[sem], by)

        if n is None:
            emit(None)
        else:
            with self.nc.Fori(0, n) as i:
                emit(i)
        for s, c in per.items():
            self.base[s] += c * (n or 1)
        self.past[me] = (base, per, n or 1)
        self.section += 1
        self.ops, self.count, self.names = [], {}, {}

    def barrier(self):
        self.flush()
        for e in self.eng.values():
            for s, sem in self.sems.items():
                if self.base[s] not in (0, CREDIT):
                    e.wait_ge(sem, self.base[s])


def program(nc, T, out, phases=9, dbg=None):
    ctx = ExitStack()
    with ctx:
        ctx.enter_context(nc.allow_non_contiguous_dma(reason="broadcasts and small tables"))
        build(nc, ctx, T, out, phases)


def build(nc, ctx, T, out, phases):
    q = Queue(nc, ctx)
    V, A, PE, G, SP = nc.vector, nc.scalar, nc.tensor, nc.gpsimd, nc.sync

    used = {}

    def sb(name, shape, dt=f32, where=ctx):
        used[name] = used.get(name, 0) + 1
        if used[name] > 1:
            name += "_use%d" % used[name]
        return where.enter_context(nc.sbuf_tensor(name, shape, dt))[tuple(slice(None) for _ in shape)]

    bank = [ctx.enter_context(nc.psum_tensor(f"bank{k}", [P, 512], f32))[:, :] for k in range(8)]
    rows_d = nc.dram_tensor("rows_scratch", (B * S, GW), f32, kind="Internal").ap()
    acc_d = nc.dram_tensor("acc_scratch", (B * S, D), f32, kind="Internal").ap()
    hop_d = nc.dram_tensor("hop_scratch", (2, 2, DC, P, S), f32, kind="Internal").ap()
    slot_d = nc.dram_tensor("slot_scratch", (2, E1 * CAP), f32, kind="Internal").ap()

    X = sb("X", [P, NT + TB, D])
    ident = sb("ident", [P, P])
    xs = sb("xs", [P, TB, D])
    xT = sb("xT", [P, DC, S])
    summed = sb("summed", [P, TB, D])
    stats = sb("stats", [P, TB, 6])
    mv = sb("mv", [P, TB, 2])
    veps = sb("veps", [P, TB])
    rstd = sb("rstd", [P, TB])
    mhalf = sb("mhalf", [P, TB])
    load = q.dma("sp", "d_x", lambda i: SP.dma_start(X[:, 0:NT, :], T["x"].rearrange("(t p) d -> p t d", p=P)))
    load_id = q.dma("sp", "d_id", lambda i: SP.dma_start(ident, T["ident"]))
    c_half = q.op("pool", lambda i: G.memset(mhalf, -0.5))
    q.op("pool", lambda i: G.memset(X[:, NT:, :], 0.0), c_half)

    def bank_free(k):
        return q.names.get("bank%d" % k) or prev("bank%d" % k)

    def bank_read(k, mark):
        q.names["bank%d" % k] = mark

    def batch_rows(i):
        return X[:, bass.ds(i * TB, TB), :]

    def take_batch(*after, pair=None):
        got = q.op("dve", lambda i: V.tensor_copy(xs, batch_rows(i)), *after, prev("summed_all"), prev("xs_read"))
        ready = []
        for c in range(DC):
            for t in range(TB):
                m = q.op("pe", lambda i, c=c, t=t: PE.transpose(bank[c][:, t * P:(t + 1) * P], xs[:, t, c * P:(c + 1) * P], ident),
                         got, bank_free(c), inc=t == TB - 1, name="xs_read")
            if pair is not None:
                ready.append(split(cut(pair, slice(None), c), bank[c], m, free=[prev("xT_read")], name="xT%d" % c))
                bank_read(c, ready[-1])
                continue
            e = ("dve", "act")[c]
            last = q.op(e, (lambda i, c=c: V.tensor_copy(xT[:, c, :], bank[c])) if c == 0 else
                        (lambda i, c=c: A.activation(xT[:, c, :], bank[c], ACT.Copy)),
                        m, prev("xT_read"), name="xT%d" % c)
            ready.append(last)
            bank_read(c, last)
        return ready

    def norm_tile(t, ps, *after, extra=None, x_of=lambda i, t: xs[:, t, :]):
        a = q.op("dve", lambda i: V.tensor_tensor(summed[:, t, :], ps, x_of(i, t), ALU.add),
                 *after, prev("normed"), name="summed%d" % t)
        if extra is not None:
            a = q.op("dve", lambda i: V.tensor_tensor(summed[:, t, :], summed[:, t, :], extra, ALU.add), a)
        s = q.op("dve", lambda i: V.bn_stats(stats[:, t, :], summed[:, t, :]), a)
        return a, q.op("dve", lambda i: V.bn_aggr(mv[:, t, :], stats[:, t, :]), s, prev("veps"), name="summed_all", plain=True)

    def norm_batch(m, where):
        v = q.op("pool", lambda i: G.tensor_scalar(veps, mv[:, :, 1], EPS, None, ALU.add), m, name="veps", plain=True)
        r = q.op("pool", lambda i: G.tensor_tensor(rstd, veps, mhalf, ALU.pow), v, c_half)
        for t in range(TB):
            last = q.op("dve", lambda i, t=t: V.tensor_scalar(where(i, t), summed[:, t, :], mv[:, t, 0:1], rstd[:, t:t + 1],
                                                             ALU.subtract, ALU.mult), r, name="normed")
        return last

    def to_X(i, t):
        return X[:, bass.ds(i * TB + t, 1), :].rearrange("p a d -> p (a d)")

    with ExitStack() as ph:
        first = sb("first", [5, 1024], where=ph)
        fmask = sb("fmask", [5, 1024], where=ph)
        work5 = sb("work5", [5, 1024], where=ph)
        fconst = sb("fconst", [5, P + 1], where=ph)
        kcols = sb("kcols", [P, 4], where=ph)
        basis = sb("basis", [P, DC, D], where=ph)
        gbasis = sb("gbasis", [P, DC, D], where=ph)
        Cmat = sb("Cmat", [P, DC, D], where=ph)
        w_el = sb("w_el", [P, DC, 24], where=ph)
        w_le = sb("w_le", [25, D], where=ph)
        b_el = sb("b_el", [24, 1], where=ph)
        golay = sb("golay", [24, 48], where=ph)
        CW = sb("CW", [P, DC, 24], where=ph)
        mm = sb("mm", [P, 2], where=ph)
        mmT = sb("mmT", [2, 1], where=ph)
        mm1 = sb("mm1", [5, 8], where=ph)
        sel = sb("sel", [2, 10], where=ph)
        dcol = sb("dcol", [P, 8], where=ph)
        trig = sb("trig", [P, 8], where=ph)
        bits = sb("bits", [24, S], where=ph)
        syn = sb("syn", [24, S], where=ph)
        fix = sb("fix", [24, S], where=ph)
        corr = sb("corr", [32, S], where=ph)
        small = [(first, bass.AP(T["x"].tensor, 0, [[0, 5], [1, 1024]])), (fmask, T["fmask"]), (fconst, T["fconst"]), (kcols, T["kcols"]),
                 (basis, T["basis"]), (w_el, T["W_el"]), (w_le, T["W_le"]), (b_el, T["b_el"]), (golay, T["golay"]), (sel, T["sel"])]
        for dst, src in small:
            loaded = q.dma("act", "d_small", lambda i, dst=dst, src=src: A.dma_start(dst, src))
        ones = q.op("pool", lambda i: G.memset(corr, 1.0))
        m1 = q.op("dve", lambda i: V.tensor_reduce(mm[:, 0:1], X[:, 0:NT, :], AX.XY, ALU.max), load)
        m2 = q.op("dve", lambda i: V.tensor_reduce(mm[:, 1:2], X[:, 0:NT, :], AX.XY, ALU.min, negate=True), load)
        m = q.op("pe", lambda i: PE.transpose(bank[0][0:2, 0:P], mm, ident), m1, m2, load_id)
        m = q.op("dve", lambda i: V.tensor_reduce(mmT, bank[0][0:2, 0:P], AX.X, ALU.max), m)
        q.op("pe", lambda i: PE.matmul(bank[1][0:5, 0:1], sel[:, 0:5], mmT, start=True, stop=True), m, loaded, inc=False)
        m = q.op("pe", lambda i: PE.matmul(bank[1][0:5, 1:2], sel[:, 5:10], mmT, start=True, stop=True))
        m = q.op("dve", lambda i: V.tensor_copy(mm1[:, 0:2], bank[1][0:5, 0:2]), m)
        m = q.op("dve", lambda i: V.scalar_tensor_tensor(mm1[:, 2:3], mm1[:, 0:1], 1e-10, mm1[:, 1:2], ALU.add, ALU.add), m)
        m = q.op("dve", lambda i: V.reciprocal(mm1[:, 3:4], mm1[:, 2:3]), m)
        m = q.op("dve", lambda i: V.tensor_scalar(first, first, mm1[:, 1:2], mm1[:, 3:4], ALU.add, ALU.mult), m)
        m = q.op("dve", lambda i: V.scalar_tensor_tensor(work5, first, 1.0, fmask, ALU.mult, ALU.mult, accum_out=mm1[:, 4:5]), m)
        m = q.op("dve", lambda i: V.tensor_tensor(mm1[:, 5:6], mm1[:, 4:5], fconst[:, P:P + 1], ALU.mult), m)
        m = q.op("dve", lambda i: V.scalar_tensor_tensor(work5, first, mm1[:, 5:6], fmask, ALU.is_gt, ALU.mult, accum_out=mm1[:, 6:7]), m)
        m = q.op("dve", lambda i: V.tensor_scalar(mm1[:, 6:7], mm1[:, 6:7], 1.0, None, ALU.max), m)
        m = q.op("act", lambda i: A.activation(mm1[:, 7:8], mm1[:, 6:7], ACT.Ln), m)
        m = q.op("pe", lambda i: PE.matmul(bank[2][:, 0:1], fconst[:, 0:P], mm1[:, 7:8], start=True, stop=True), m)
        m = q.op("dve", lambda i: V.tensor_scalar(dcol[:, 0:1], bank[2][:, 0:1], 1.0, 2.0, ALU.max, ALU.min), m)
        m = q.op("dve", lambda i: V.tensor_scalar(dcol[:, 1:2], dcol[:, 0:1], 0.2, 1.0, ALU.mult, ALU.add), m)
        m = q.op("dve", lambda i: V.tensor_tensor(dcol[:, 2:3], dcol[:, 1:2], dcol[:, 0:1], ALU.mult), m)
        m = q.op("dve", lambda i: V.tensor_scalar(dcol[:, 3:4], dcol[:, 0:1], 0.5, 1.0, ALU.mult, ALU.add), m)
        m = q.op("dve", lambda i: V.tensor_scalar(dcol[:, 4:5], dcol[:, 0:1], 0.1, None, ALU.mult), m)
        m = q.op("dve", lambda i: V.tensor_scalar(trig[:, 0:2], kcols[:, 0:2], dcol[:, 3:4], dcol[:, 2:3], ALU.mult, ALU.add), m)
        m = q.op("dve", lambda i: V.tensor_scalar(trig[:, 2:4], kcols[:, 2:4], dcol[:, 4:5], dcol[:, 2:3], ALU.mult, ALU.add), m)
        m = q.op("dve", lambda i: V.tensor_tensor(trig[:, 2:4], trig[:, 2:4], kcols[:, 0:2], ALU.subtract), m)
        m = q.op("dve", lambda i: V.tensor_scalar(trig[:, 0:2], trig[:, 0:2], -1.0, float(np.pi), ALU.mult, ALU.add), m)
        m = q.op("dve", lambda i: V.tensor_scalar(trig[:, 2:4], trig[:, 2:4], -1.0, float(np.pi / 2), ALU.mult, ALU.add), m)
        m = q.op("act", lambda i: A.activation(trig[:, 4:8], trig[:, 0:4], ACT.Sin), m)
        m = q.op("dve", lambda i: V.tensor_tensor(trig[:, 0:2], trig[:, 4:6], trig[:, 6:8], ALU.mult), m)
        for c in range(DC):
            g = q.op("dve", lambda i, c=c: V.tensor_scalar(gbasis[:, c, :], basis[:, c, :], trig[:, c:c + 1], None, ALU.mult), m)
        for r in range(DC):
            for c in range(DC):
                m = q.op("pe", lambda i, r=r, c=c: PE.matmul(bank[3][:, r * D:(r + 1) * D], basis[:, c, r * P:(r + 1) * P], gbasis[:, c, :],
                                                             start=c == 0, stop=c == DC - 1), g)
        m = q.op("dve", lambda i: V.tensor_copy(Cmat.rearrange("p c d -> p (c d)"), bank[3]), m)
        for r in range(DC):
            for c in range(DC):
                w = q.op("pe", lambda i, r=r, c=c: PE.matmul(bank[4][:, r * 24:(r + 1) * 24], Cmat[:, c, r * P:(r + 1) * P], w_el[:, c, :],
                                                             start=c == 0, stop=c == DC - 1), m)
        m_cw = q.op("dve", lambda i: V.tensor_copy(CW.rearrange("p c d -> p (c d)"), bank[4][:, 0:48]), w)
        q.barrier()

        x_ready = take_batch()
        for c in range(DC):
            m = q.op("pe", lambda i, c=c: PE.matmul(bank[2][0:24, :], CW[:, c, :], xT[:, c, :], start=c == 0, stop=c == DC - 1),
                     x_ready, bank_free(2))
        m = q.op("dve", lambda i: V.tensor_scalar(bits, bank[2][0:24, :], b_el, 0.0, ALU.add, ALU.is_gt), m, name="bank2")
        m = q.op("pe", lambda i: PE.matmul(bank[3][0:24, :], golay[:, 0:24], bits, start=True, stop=True), m, prev("syn"), plain=True)
        m = q.op("dve", lambda i: V.tensor_scalar(syn, bank[3][0:24, :], 0.5, None, ALU.is_gt), m, name="syn")
        m = q.op("pe", lambda i: PE.matmul(bank[4][0:24, :], golay[:, 24:48], syn, start=True, stop=True), m, prev("fixed"), plain=True)
        m = q.op("dve", lambda i: V.scalar_tensor_tensor(fix, bank[4][0:24, :], 3.5, syn, ALU.is_le, ALU.mult), m, name="fixed")
        n = q.op("dve", lambda i: V.tensor_scalar(syn, bits, -2.0, 1.0, ALU.mult, ALU.add), m)
        m = q.op("dve", lambda i: V.tensor_tensor(fix, fix, syn, ALU.mult), n)
        m = q.op("dve", lambda i: V.tensor_tensor(corr[0:24, :], bits, fix, ALU.add), m, prev("xT_read"))
        for t in range(TB):
            bk = bank[5 + t // 2][:, (t % 2) * D:(t % 2 + 1) * D]
            for c in range(DC):
                q.op("pe", lambda i, t=t, c=c, bk=bk: PE.matmul(bk, xT[:, c, t * P:(t + 1) * P], Cmat[:, c, :], start=c == 0, stop=False),
                     prev("summed%d" % (t | 1)), inc=False)
            y = q.op("pe", lambda i, t=t, bk=bk: PE.matmul(bk, corr[0:25, t * P:(t + 1) * P], w_le, start=False, stop=True), m, name="xT_read")
            if t % 2:
                for u in (t - 1, t):
                    last = norm_tile(u, bank[5 + t // 2][:, (u % 2) * D:(u % 2 + 1) * D], y)
        norm_batch(last[1], to_X)
        q.flush(B)
        q.barrier()
    if phases <= 1:
        return finish(q, out, X, SP)

    def parts(name, shape, where):
        return tuple(sb(name + x, shape, f32r, where=where) for x in ("_hi", "_lo"))

    def f32_of(ap):
        return ap.bitcast(f32)

    def split(pair, src, *after, free=(), e="act", name=None):
        if e == "act":
            a = q.op("act", lambda i: A.activation(pair[0], src, ACT.Copy), *after, *free)
        else:
            a = q.op("dve", lambda i: V.tensor_copy(pair[0], src), *after, *free)
        return q.op("dve", lambda i: V.tensor_tensor(pair[1], src, f32_of(pair[0]), ALU.subtract), a, *after, *free, name=name)

    def terms(lhs, rhs):
        return [(lhs[0], rhs[0]), (lhs[0], rhs[1]), (lhs[1], rhs[0])]

    def product(out, pairs, *after, name=None, first=True, last=True):
        seq = [t for p in pairs for t in terms(*p)]
        for n, (lhs, rhs) in enumerate(seq):
            m = q.op("pe", lambda i, lhs=lhs, rhs=rhs, n=n: PE.matmul(out, lhs, rhs, start=first and n == 0, stop=last and n == len(seq) - 1),
                     *after, inc=n == len(seq) - 1, name=name)
        return m

    def cut(pair, *idx):
        return tuple(p[idx] for p in pair)

    def weights_in(pair, stage, src, free, k=0):
        m = q.dma("sp", "d_stage%d" % k, lambda i: SP.dma_start(stage, src), free)
        return split(pair, stage, m, e="act")

    S_BANKS, T_BANKS, O_BANKS, M_BANK = (0, 1, 2), (3, 4), (5, 6), 7
    T_LAG, PV_LAG = 5, 6

    def attend(buf, scores, values, jobs, before=None, after=None):
        steps = TB * jobs
        done = {}
        for s in range(steps + PV_LAG):
            if before and s < steps:
                before(s)
            u = s - T_LAG
            if 0 <= u < steps:
                h, kt = divmod(u, TB)
                tb = T_BANKS[u % 2]
                for t in range(TB):
                    m = q.op("pe", lambda i, t=t, kt=kt, tb=tb, h=h: PE.transpose(bank[tb][:, t * P:(t + 1) * P], buf.P[h % 2][:, t, kt * P:(kt + 1) * P], ident),
                             [done["scaled", h, x] for x in range(TB)], bank_free(tb),
                             inc=t == TB - 1)
                done["transposed", h] = m
                if kt == TB - 1:
                    q.names["P_read%d" % (h % 2)] = m
                free = done.get(("pv", u - 3)) or prev("pv_any")
                a = q.op("act", lambda i, u=u, tb=tb: A.activation(buf.PT[u % 3][0], bank[tb], ACT.Copy), m, free)
                m = q.op("dve", lambda i, u=u, tb=tb: V.tensor_tensor(buf.PT[u % 3][1], bank[tb], f32_of(buf.PT[u % 3][0]), ALU.subtract), a, name="bank%d" % tb)
                done["copied", u] = m
            if s < steps:
                h, j = divmod(s, TB)
                sbk = S_BANKS[s % 3]
                pairs, ready = scores(h, j)
                for n, (lhs, rhs) in enumerate(pairs):
                    m = q.op("pe", lambda i, lhs=lhs, rhs=rhs, n=n, sbk=sbk, k=len(pairs): PE.matmul(bank[sbk], lhs, rhs, start=n == 0, stop=n == k - 1),
                             ready, bank_free(sbk), inc=n == len(pairs) - 1)
                done["scores", h] = m
                c = s % 8
                m = q.op("dve", lambda i, c=c, sbk=sbk: V.tensor_reduce(buf.nmax[:, c:c + 1], bank[sbk], AX.X, ALU.max, negate=True), m,
                         done.get(("exp", s - 8)) or prev("exp_any"))
                m = q.op("act", lambda i, c=c, sbk=sbk, h=h, j=j: A.activation(buf.P[h % 2][:, j, :], bank[sbk], ACT.Exp, bias=buf.nmax[:, c:c + 1], accum_out=buf.rsum[:, c:c + 1]),
                         m, done.get(("transposed", h - 2)) or prev("P_read%d" % (h % 2)), done.get(("scaled8", s - 8)) or prev("scaled_any"), name="bank%d" % sbk)
                q.names["exp_any"] = m
                done["exp", s] = m
                m = q.op("dve", lambda i, c=c: V.reciprocal(buf.rinv[:, c:c + 1], buf.rsum[:, c:c + 1]), m)
                if buf.share and s % buf.share == 0:
                    m = q.op("pool", lambda i, c=c, h=h, j=j: G.tensor_scalar(buf.P[h % 2][:, j, :], buf.P[h % 2][:, j, :], buf.rinv[:, c:c + 1], None, ALU.mult), m, name="scaled_any", plain=True)
                else:
                    m = q.op("dve", lambda i, c=c, h=h, j=j: V.tensor_scalar(buf.P[h % 2][:, j, :], buf.P[h % 2][:, j, :], buf.rinv[:, c:c + 1], None, ALU.mult), m, name="scaled_any")
                done["scaled", h, j] = done["scaled8", s] = m
            u = s - PV_LAG
            if 0 <= u < steps:
                h, kt = divmod(u, TB)
                triples, ready = values(h, kt)
                for lhs, bk, first, last in triples:
                    m = product(bank[bk], [(lhs, buf.PT[u % 3])], done["copied", u], ready, name="pv_any", first=first, last=last)
                done["pv", u] = m
                if kt == TB - 1:
                    done["head", h] = m
                    if after:
                        after(h, m)
        return done

    class Buffers:

        def __init__(self, where, share=0):
            self.share = share
            self.P = [sb("P%d" % k, [P, TB, S], where=where) for k in range(2)]
            self.PT = [parts("PT%d" % k, [P, S], where) for k in range(3)]
            self.nmax = sb("nmax", [P, 8], where=where)
            self.rsum = sb("rsum", [P, 8], where=where)
            self.rinv = sb("rinv", [P, 8], where=where)

    def project(w, src, c, full, pair, bias, scale, ready, free, name, bk=M_BANK):
        m = product(bank[bk], [(cut(w, slice(None), k, slice(c * P, (c + 1) * P)), cut(src, slice(None), k)) for k in range(DC)],
                    ready, bank_free(bk), name=name + "_in")
        m = q.op("dve", lambda i: V.tensor_scalar(full, bank[bk], bias if bias is not None else 0.0, scale, ALU.add, ALU.mult), m,
                 q.names.get("full_read") or prev("full_read"))
        bank_read(bk, m)
        if pair is None:
            return m
        m = split(pair, full, m, free=[free], name=name)
        q.names["full_read"] = m
        return m

    with ExitStack() as ph:
        buf = Buffers(ph)
        W6 = {n: parts("w_" + n, [P, DC, D], ph) for n in ("Wq_c", "Wk_s", "Wv_s", "Wq_s", "Wk_c", "Wv_c")}
        Wg = parts("Wg", [P, 2 * DC, D], ph)
        stage = [sb("stage%d" % k, [P, 2 * DC, D], where=ph) for k in range(2)]
        xTp = parts("xTp", [P, DC, S], ph)
        ctxp = parts("ctxp", [P, DC, S], ph)
        full = sb("full", [P, S], where=ph)
        bias0 = sb("bias0", [P, 7, DC], where=ph)
        bgh = sb("bgh", [P, DC], where=ph)
        ctxT = sb("ctxT", [P, DC, S], where=ph)
        QK = [[parts("%s%d" % (n, d), [P, DC, S], ph) for n in ("QT", "KT")] for d in range(2)]
        VV = [parts("VV%d" % d, [P, TB, D], ph) for d in range(2)]
        cTp = parts("cTp", [P, 2 * DC, S], ph)
        cT = sb("cT", [P, 2 * DC, S], where=ph)
        gate = sb("gate", [P, DC, S], where=ph)
        mix = sb("mix", [P, DC, S], where=ph)
        w_done = []
        for k, (n, t) in enumerate([*W6.items(), ("Wg", Wg)]):
            w_done.append(weights_in(t, stage[k % 2][:, 0:t[0].shape[1], :], T[n], w_done[k - 2] if k > 1 else None, k % 2))
        w_in = q.dma("act", "d_w0", lambda i: A.dma_start(bias0, T["bias0"]))
        halved = q.op("dve", lambda i: V.tensor_scalar(bgh, bias0[:, 6, :], 0.5, None, ALU.mult), w_in)
        q.flush()

        ctx_in = q.dma("sp", "d_ctx", lambda i: SP.dma_start(ctxT, T["ctxT"][bass.ds(i, 1)].rearrange("a p c s -> p (a c) s")), prev("ctx_read"))
        ctx_in = split((ctxp[0], ctxp[1]), ctxT, ctx_in, free=[prev("xT_read")], name="ctx_read")
        x_ready = take_batch(w_in, pair=xTp)
        x_ready += w_done + [w_in]
        SC = D ** -0.5
        ready = {}
        for d, (qs, ks, qm, km, wq, wk, wv) in enumerate([(xTp, ctxp, x_ready, ctx_in, "Wq_c", "Wk_s", "Wv_s"),
                                                          (ctxp, xTp, ctx_in, x_ready, "Wq_s", "Wk_c", "Wv_c")]):
            for c in range(DC):
                a = project(W6[wq], qs, c, full, cut(QK[d][0], slice(None), c), bias0[:, 3 * d, c:c + 1], SC, [qm, x_ready], prev("scores%d" % d), "Q%d%d" % (d, c))
                b = project(W6[wk], ks, c, full, cut(QK[d][1], slice(None), c), bias0[:, 3 * d + 1, c:c + 1], 1.0, [km, x_ready], prev("scores%d" % d), "K%d%d" % (d, c), bk=T_BANKS[c])
                ready.setdefault(d, []).extend([a, b])
            for pair in range(2):
                for t in (2 * pair, 2 * pair + 1):
                    m = product(bank[O_BANKS[pair]][:, (t % 2) * D:(t % 2 + 1) * D],
                                [(cut(ks, slice(None), k, slice(t * P, (t + 1) * P)), cut(W6[wv], slice(None), k)) for k in range(DC)],
                                km, x_ready, bank_free(O_BANKS[pair]), name="xT_read")
                ready["V", d, pair] = split(tuple(v[:, 2 * pair:2 * pair + 2, :].rearrange("p t d -> p (t d)") for v in VV[d]), bank[O_BANKS[pair]], m, free=[prev("pv_any")])
                bank_read(O_BANKS[pair], ready["V", d, pair])

        def scores0(h, j):
            Q, K = QK[h]
            return [t for c in range(DC) for t in terms(cut(Q, slice(None), c, slice(j * P, (j + 1) * P)), cut(K, slice(None), c))], ready[h]

        def values0(h, kt):
            w = [ready["V", h, 0], ready["V", h, 1], ready["V", 1, 0], ready["V", 1, 1]]
            w += [bank_free(k) for k in O_BANKS] if kt == 0 else []
            return [(cut(VV[h], slice(None), kt, slice(c * P, (c + 1) * P)), O_BANKS[c], kt == 0, kt == TB - 1) for c in range(DC)], w

        def after0(h, m):
            for c in range(DC):
                r = q.op("act", lambda i, c=c: A.activation(cT[:, DC * h + c, :], bank[O_BANKS[c]], ACT.Identity, bias=bias0[:, 3 * h + 2, c:c + 1], scale=1.0),
                         m, prev("mixed"), name="bank%d" % O_BANKS[c])
                ready.setdefault(("out", h), []).append(r)
                ready.setdefault(("outp", h), []).append(split(cut(cTp, slice(None), DC * h + c), cT[:, DC * h + c, :], r, free=[prev("gate_in")]))

        done = attend(buf, scores0, values0, 2, after=after0)
        q.names["scores0"], q.names["scores1"] = done["scores", 0], done["scores", 1]
        both = ready["out", 0] + ready["out", 1]
        for c in range(DC):
            m = product(bank[T_BANKS[c]], [(cut(Wg, slice(None), k, slice(c * P, (c + 1) * P)), cut(cTp, slice(None), k)) for k in range(2 * DC)],
                        ready["outp", 0], ready["outp", 1], bank_free(T_BANKS[c]), name="gate_in")
            m = q.op("act", lambda i, c=c: A.activation(gate[:, c, :], bank[T_BANKS[c]], ACT.Tanh, bias=bgh[:, c:c + 1], scale=0.5), m, prev("mixed"), name="bank%d" % T_BANKS[c])
            m = q.op("pool", lambda i, c=c: G.tensor_scalar(gate[:, c, :], gate[:, c, :], 0.5, 0.5, ALU.mult, ALU.add), m, plain=True)
            n = q.op("dve", lambda i, c=c: V.tensor_tensor(mix[:, c, :], cT[:, c, :], cT[:, DC + c, :], ALU.subtract), both, prev("mix_read"))
            n = q.op("dve", lambda i, c=c: V.tensor_tensor(mix[:, c, :], mix[:, c, :], gate[:, c, :], ALU.mult), n, m)
            n = q.op("dve", lambda i, c=c: V.tensor_tensor(mix[:, c, :], mix[:, c, :], cT[:, DC + c, :], ALU.add), n, name="mixed")
            ready["mix", c] = n
        for t in range(TB):
            for c in range(DC):
                m = q.op("pe", lambda i, t=t, c=c: PE.transpose(bank[O_BANKS[t // 2]][:, (t % 2) * D + c * P:(t % 2) * D + (c + 1) * P], mix[:, c, t * P:(t + 1) * P], ident),
                         ready["mix", 0], ready["mix", 1], bank_free(O_BANKS[t // 2]), name="mix_read")
            if t % 2:
                for v in (t - 1, t):
                    last = norm_tile(v, bank[O_BANKS[t // 2]][:, (v % 2) * D:(v % 2 + 1) * D], m)
                bank_read(O_BANKS[t // 2], last[0])
        norm_batch(last[1], to_X)
        q.flush(B)
        q.barrier()
    if phases <= 2:
        return finish(q, out, X, SP)

    def norm_from_acc():
        ld = q.dma("sp", "d_acc", lambda i: SP.dma_start(summed, acc_d.rearrange("(t p) d -> p t d", p=P)[:, bass.ds(i * TB, TB), :]), prev("normed"))
        for t in range(TB):
            s_ = q.op("dve", lambda i, t=t: V.bn_stats(stats[:, t, :], summed[:, t, :]), ld)
            m = q.op("dve", lambda i, t=t: V.bn_aggr(mv[:, t, :], stats[:, t, :]), s_, prev("veps"), plain=True)
        norm_batch(m, to_X)
        q.flush(B)
        q.barrier()

    with ExitStack() as ph:
        W1 = [sb("W1_%d" % b, [P, DC, F0], where=ph) for b in range(2)]
        W2 = [sb("W2_%d" % b, [P, FC0, D], where=ph) for b in range(2)]
        b1 = sb("b1", [P, E0 * FC0], where=ph)
        b2 = sb("b2", [P, E0 * D], where=ph)
        idx_all = sb("idx_all", [P, (E0 + 2) * CT0], i32, where=ph)
        tok_col = sb("tok_col", [P, E0 * CT0], where=ph)
        tok_row = sb("tok_row", [P, E0 * C0], i32, where=ph)
        lower = sb("lower", [P, P], where=ph)
        idx = [sb("idx%d" % b, [P, CT0], i32, where=ph) for b in range(2)]
        rows = [sb("rows%d" % b, [P, CT0, GW], where=ph) for b in range(2)]
        wcol = [sb("wcol%d" % b, [P, CT0], where=ph) for b in range(2)]
        GT = [sb("GT%d" % b, [P, DC, C0], where=ph) for b in range(2)]
        hT = [sb("hT%d" % b, [P, FC0, C0], where=ph) for b in range(2)]
        same = [sb("same%d" % b, [P, CT0, P], where=ph) for b in range(2)]
        junk = sb("junk", [P, P], where=ph)
        again = sb("again", [P, 2 * CT0], where=ph)
        sidx = [sb("sidx%d" % b, [P, CT0], i32, where=ph) for b in range(2)]
        wv = [sb("wv%d" % b, [P, D], where=ph) for b in range(2)]
        merged = [sb("merged%d" % b, [P, CT0, D], where=ph) for b in range(2)]
        for dst, src in ((b1, T["b1"]), (b2, bass.AP(T["b2"].tensor, 0, [[0, P], [1, E0 * D]])), (lower, T["lower"])):
            w_in = q.dma("act", "d_w0", lambda i, dst=dst, src=src: A.dma_start(dst, src))
        i_in = q.dma("pool", "d_g0", lambda i: G.dma_start(idx_all[:, 0:E0 * CT0], T["idx"]))
        padded = [i_in, q.op("pool", lambda i: G.memset(idx_all[:, E0 * CT0:], 0))]
        j_in = q.dma("pool", "d_g1", lambda i: G.dma_start(tok_row, bass.AP(T["tok"].tensor, 0, [[0, P], [1, E0 * C0]])))
        acc_in = q.dma("pool", "d_sc0", lambda i: G.dma_start(acc_d.rearrange("(t p) d -> p t d", p=P), X[:, 0:NT, :]))
        rows_in = [q.dma("pool", "d_sc1", lambda i: G.dma_start(rows_d.rearrange("(t p) d -> p t d", p=P)[:, :, 0:D], X[:, 0:NT, :])),
                   q.dma("sp", "d_rows", lambda i: SP.dma_start(rows_d[:, D:GW], T["combine"]))]
        tok_f = q.op("dve", lambda i: V.tensor_copy(tok_col, idx_all[:, 0:E0 * CT0]), i_in)
        q.flush()

        def gather0(i, b, rows_free):
            m = q.op("pool", lambda _, b=b, i=i: G.tensor_copy(idx[b], idx_all[:, i(_, b)]), padded, rows_free, q.names.get("gathered%d" % b))
            for t in range(CT0):
                q.dma("pool", "d_g%d" % b, lambda _, b=b, t=t: G.indirect_dma_start(rows[b][:, t, :], None, rows_d, bass.IndirectOffsetOnAxis(ap=idx[b][:, t:t + 1], axis=0)),
                      m, rows_in, rows_free, name="gathered%d" % b)

        for b in range(2):
            gather0(lambda _, b: slice(b * CT0, (b + 1) * CT0), b, None)
        q.flush()
        for b in range(2):
            for dst, name in ((W1[b], "W1"), (W2[b], "W2")):
                w = q.dma("sp", "d_e%d" % b, lambda i, b=b, dst=dst, name=name: SP.dma_start(dst, T[name][bass.ds(2 * i + b, 1)].rearrange("a p c f -> p (a c) f")), prev("W_read%d" % b))
            g = prev("gathered%d" % b)
            for c in range(DC):
                for t in range(CT0):
                    m = q.op("pe", lambda i, b=b, t=t, c=c: PE.transpose(bank[c][:, t * P:(t + 1) * P], rows[b][:, t, c * P:(c + 1) * P], ident),
                             g, (q.names["GT%d" % c] if b else prev("GT%d" % c)), inc=t == CT0 - 1)
                m_t = m
                if c:
                    m = q.op("act", lambda i, b=b, c=c: A.activation(GT[b][:, c, :], bank[c], ACT.Copy), m, prev("GT_read%d" % b), name="GT1")
                else:
                    m = q.op("dve", lambda i, b=b, c=c: V.tensor_copy(GT[b][:, c, :], bank[c]), m, prev("GT_read%d" % b), name="GT0")
            gt = [q.names["GT0"], q.names["GT1"]]
            wc = q.op("dve", lambda i, b=b: V.tensor_copy(wcol[b], rows[b][:, :, bass.ds(2 * i + b + D, 1)].rearrange("p t a -> p (t a)")), g, prev("wcol_read%d" % b))
            gather0(lambda i, b: bass.ds((2 * i + b + 2) * CT0, CT0), b, [m_t, wc])
            for t in range(CT0):
                a = q.op("dve", lambda i, b=b, t=t: V.tensor_scalar(same[b][:, t, :], tok_row[:, bass.ds((2 * i + b) * C0 + t * P, P)], tok_col[:, bass.ds((2 * i + b) * CT0 + t, 1)], None, ALU.is_equal),
                         tok_f, j_in, prev("same_read%d" % b))
                m = q.op("dve", lambda i, b=b, t=t: V.scalar_tensor_tensor(junk, tok_row[:, bass.ds((2 * i + b) * C0 + t * P, P)], tok_col[:, bass.ds((2 * i + b) * CT0 + t, 1)], lower,
                                                                        ALU.is_equal, ALU.mult, accum_out=again[:, t:t + 1]), w_in, q.names.get("junk") or prev("junk"), name="junk")
            m = q.op("dve", lambda i: V.tensor_scalar(again[:, CT0:2 * CT0], again[:, 0:CT0], 0.0, float(1 << 16), ALU.is_gt, ALU.mult), m)
            found = q.op("dve", lambda i, b=b: V.tensor_tensor(sidx[b], again[:, CT0:2 * CT0], tok_col[:, bass.ds((2 * i + b) * CT0, CT0)], ALU.add), m, prev("stored%d" % b))
            for f in range(FC0):
                bk = 2 + f % 2
                for c in range(DC):
                    m = q.op("pe", lambda i, b=b, f=f, c=c, bk=bk: PE.matmul(bank[bk], W1[b][:, c, f * P:(f + 1) * P], GT[b][:, c, :], start=c == 0, stop=c == DC - 1),
                             w, gt, q.names.get("hid%d" % (f % 2)) or prev("hid%d" % (f % 2)), inc=c == DC - 1, name="GT_read%d" % b)
                m = q.op("act", lambda i, b=b, f=f, bk=bk: A.activation(hT[b][:, f, :], bank[bk], ACT.Gelu_apprx_tanh, bias=b1[:, bass.ds((2 * i + b) * FC0 + f, 1)], scale=1.0),
                         m, w_in, prev("hT_read%d" % b), name="hid%d" % (f % 2))
            for t in range(CT0):
                bk = 4 + t % 2
                for f in range(FC0):
                    m2 = q.op("pe", lambda i, b=b, t=t, f=f, bk=bk: PE.matmul(bank[bk][:, 0:D], hT[b][:, f, t * P:(t + 1) * P], W2[b][:, f, :], start=f == 0, stop=f == FC0 - 1),
                              m if f == FC0 - 1 else q.names["hid%d" % (f % 2)], q.names.get("up%d" % (t % 2)) or prev("up%d" % (t % 2)), inc=f == FC0 - 1, name="hT_read%d" % b)
                q.names["W_read%d" % b] = m2
                a = q.op("dve", lambda i, b=b, t=t, bk=bk: V.tensor_tensor(wv[t % 2], bank[bk][:, 0:D], b2[:, bass.ds((2 * i + b) * D, D)], ALU.add), m2,
                         q.names.get("wv_read%d" % (t % 2)) or prev("wv_read%d" % (t % 2)), name="up%d" % (t % 2))
                a = q.op("dve", lambda i, b=b, t=t: V.tensor_scalar(wv[t % 2], wv[t % 2], wcol[b][:, t:t + 1], None, ALU.mult), a, wc, name="wcol_read%d" % b)
                bm = 6 + t % 2
                m3 = q.op("pe", lambda i, b=b, t=t, bm=bm: PE.matmul(bank[bm][:, 0:D], same[b][:, t, :], wv[t % 2], start=True, stop=True), a,
                          q.names.get("mg%d" % (t % 2)) or prev("mg%d" % (t % 2)), name="wv_read%d" % (t % 2))
                q.names["same_read%d" % b] = m3
                a = q.op("dve", lambda i, b=b, t=t, bm=bm: V.tensor_copy(merged[b][:, t, :], bank[bm][:, 0:D]), m3, prev("stored%d" % b), name="mg%d" % (t % 2))
                q.dma("pool", "d_sc%d" % b, lambda i, b=b, t=t: G.indirect_dma_start(acc_d, bass.IndirectOffsetOnAxis(ap=sidx[b][:, t:t + 1], axis=0), merged[b][:, t, :], None,
                                                                           compute_op=ALU.add, bounds_check=B * S - 1, oob_is_err=False),
                      a, found, acc_in, q.names.get("stored") or prev("stored"), name="stored")
            q.names["stored%d" % b] = q.names["stored"]
        q.flush(E0 // 2)
        q.barrier()
    norm_from_acc()
    if phases <= 3:
        return finish(q, out, X, SP)

    MAX_BANKS, ST_BANKS, OUT_BANKS, ROW_BANK, SPARE_BANK = (0, 1), (2, 3), (4, 5), 6, 7
    ROW_LAG, ST_LAG, OUT_LAG = 4, 7, 9
    ROWS = 96
    MAX_ROW = 64

    def attend_heads(buf, maxima, row, scores, values, besides, after, seconds):
        steps = TB * H1
        done = {}

        def group(bk, pairs, *after):
            for n, (lhs, rhs) in enumerate(pairs):
                m = q.op("pe", lambda i, lhs=lhs, rhs=rhs, n=n: PE.matmul(bank[bk], lhs, rhs, start=n == 0, stop=n == len(pairs) - 1),
                         *after, inc=n == len(pairs) - 1)
            return m

        for s in range(steps + OUT_LAG):
            if s < steps:
                h, j = divmod(s, TB)
                bk = MAX_BANKS[s % 2]
                pairs, ready = maxima(h, j)
                m = done["first", h] = group(bk, pairs, ready, bank_free(bk))
                m = q.op("dve", lambda i, h=h, j=j, bk=bk: V.tensor_reduce(buf.nmax[:, (h % 2) * TB + j:(h % 2) * TB + j + 1], bank[bk], AX.X, ALU.max, negate=True),
                         m, done.get(("nmax_read", h - 2)) or prev("nmax_read%d" % (h % 2)), name="bank%d" % bk)
                done["nmax", h] = m
            u = s - ST_LAG
            if 0 <= u < steps:
                h, kt = divmod(u, TB)
                bk = ST_BANKS[u % 2]
                m = q.names["second"] = group(bk, scores(h, kt), done["row", h], bank_free(bk))
                if kt == TB - 1:
                    seconds(h)
                m = q.op("act", lambda i, u=u, bk=bk: A.activation(buf.PT[u % 4], bank[bk], ACT.Exp), m, done.get(("pv", u - 4)) or prev("pv_last"), name="bank%d" % bk)
                done["exp", u] = m
            u = s - OUT_LAG
            if 0 <= u < steps:
                h, kt = divmod(u, TB)
                lhs, bk, first, last, ready = values(h, kt)
                m = q.op("pe", lambda i, lhs=lhs, bk=bk, u=u, first=first, last=last: PE.matmul(bank[bk], lhs, buf.PT[u % 4], start=first, stop=last),
                         done["exp", u], ready, bank_free(bk) if first else None, name="pv_last")
                done["pv", u] = m
                if kt == TB - 1:
                    after(h, m)
            h, j = divmod(s - ROW_LAG, TB)
            if j == 0 and 0 <= h < H1:
                for t in range(TB):
                    m = q.op("pe", lambda i, h=h, t=t: PE.transpose(bank[ROW_BANK][0:1, t * P:(t + 1) * P], buf.nmax[:, (h % 2) * TB + t:(h % 2) * TB + t + 1], ident),
                             done["nmax", h], bank_free(ROW_BANK), inc=t == TB - 1, plain=True)
                done["nmax_read", h] = m
                q.names["nmax_read%d" % (h % 2)] = m
                dst, ready = row(h)
                done["row", h] = q.op("act", lambda i, dst=dst: A.activation(dst, bank[ROW_BANK][0:1, :], ACT.Copy), m, ready, name="bank%d" % ROW_BANK)
            besides(s)
        return done

    class HeadBuffers:

        def __init__(self, where):
            self.PT = [sb("ST%d" % k, [P, S], where=where) for k in range(4)]
            self.nmax = sb("nmax1", [P, 2 * TB], where=where)

    def out_projection(attT, Wo, bo, ready, ng):
        for t in range(TB):
            bk = MAX_BANKS[t // 2]
            half = bank[bk][:, (t % 2) * D:(t % 2 + 1) * D]
            for g in range(ng):
                m = q.op("pe", lambda i, t=t, g=g, half=half: PE.matmul(half, attT[:, g, t * P:(t + 1) * P], Wo[:, g, :], start=g == 0, stop=g == ng - 1),
                         ready, bank_free(bk), inc=g == ng - 1, name="att_read")
            if t % 2:
                for v in (t - 1, t):
                    last = norm_tile(v, bank[bk][:, (v % 2) * D:(v % 2 + 1) * D], m, extra=bo, x_of=to_X)
                bank_read(bk, last[0])
        norm_batch(last[1], to_X)

    with ExitStack() as ph:
        HD, HG = D // H1, 4
        buf = HeadBuffers(ph)
        Wq, Wk, Wv = (parts("W" + n, [P, DC, D], ph) for n in "qkv")
        Wo = sb("Wo", [P, DC, D], where=ph)
        bo = sb("bo", [P, D], where=ph)
        bv = sb("bv", [P, D], where=ph)
        bqkv = sb("bqkv", [P, 3, DC], where=ph)
        cs = sb("cs", [P, 2, S], where=ph)
        full = sb("full", [P, S], where=ph)
        turned = sb("turned", [P, DC, S], where=ph)
        part = sb("part", [P, DC, S], where=ph)
        stage = [turned[:, :, 0:D], part[:, :, 0:D]]
        srcp = parts("srcp", [P, DC, S], ph)
        qk = [parts(n, [P, DC, S], ph) for n in ("qp", "kp")]
        rows_q, rows_k = (sb(n, [ROWS, H1, S], f32r, where=ph) for n in ("rows_q", "rows_k"))
        Vone = sb("Vone", [P, TB, H1, P], where=ph)
        gathered_o = [sb("gathered_o%d" % k, [P, S], where=ph) for k in range(2)]
        sums = sb("sums", [P, TB, HG], where=ph)
        att = sb("att", [P, TB, D], where=ph)
        attT = sb("attT", [P, DC, S], where=ph)
        for dst, src in ((Wo, T["Wo1"]), (bqkv, T["bqkv"]), (cs, T["cs"]), (bo, bass.AP(T["bo1"].tensor, 0, [[0, P], [1, D]])),
                         (bv, bass.AP(T["bv1"].tensor, 0, [[0, P], [1, D]]))):
            w_in = q.dma("act", "d_w0", lambda i, dst=dst, src=src: A.dma_start(dst, src))
        z = None
        for r in (rows_q, rows_k):
            z = q.op("pool", lambda i, r=r: G.memset(f32_of(r[MAX_ROW:ROWS]), 0.0), z)
        z = q.op("pool", lambda i: G.memset(f32_of(rows_k[MAX_ROW:MAX_ROW + 1]), 1.0), z)
        z = q.op("pool", lambda i: G.memset(Vone, 0.0), z)

        def head_columns(n, k):
            return [bass.AP(Vone.tensor, Vone.offset + t * H1 * P + n, [Vone.ap[0], [HG * P, H1 // HG], [P + 32, HG], [1, k]]) for t in range(TB)]

        for ap in head_columns(HD, 1):
            z = q.op("pool", lambda i, ap=ap: G.memset(ap, 1.0), z)
        w_done = []
        for k, (t, n) in enumerate(((Wq, "Wq1"), (Wk, "Wk1"), (Wv, "Wv1"))):
            w_done.append(weights_in(t, stage[k % 2], T[n], w_done[0] if k == 2 else None, k % 2))
        q.barrier()

        Vc = sb("Vc", [P, TB, D], where=ph)
        prep = {}

        def rows_of_next(i):
            return X[:, bass.ds((i + 1) * TB, TB), :] if i is not None else X[:, 0:TB, :]

        def take(i_):
            prep["xs"] = q.op("dve", lambda i: V.tensor_copy(xs, rows_of_next(i)), prev("xs_read"))

        def turn(c):
            for t in range(TB):
                m = q.op("pe", lambda i, c=c, t=t: PE.transpose(bank[SPARE_BANK][:, t * P:(t + 1) * P], xs[:, t, c * P:(c + 1) * P], ident),
                         prep["xs"], bank_free(SPARE_BANK), inc=t == TB - 1, name="xs_read")
            prep["xT", c] = q.op("act", lambda i, c=c: A.activation(xT[:, c, :], bank[SPARE_BANK], ACT.Copy), m, prev("xT_read"), name="bank%d" % SPARE_BANK)

        def rope(c):
            x_in = [prep["xT", 0], prep["xT", 1]]
            b = q.op("pool", lambda i, c=c: G.tensor_tensor(part[:, c, :], xT[:, 1, :], cs[:, 1 - c, :], ALU.mult), x_in, prev("turned%d" % c), plain=True)
            a = q.op("dve", lambda i, c=c: V.tensor_tensor(turned[:, c, :], xT[:, 0, :], cs[:, c, :], ALU.mult), x_in, prev("turned_read%d" % c))
            prep["mul", c] = a, b
            q.names["xT_read"] = [a, b] + (list(prep["mul", 0]) if c else [])

        def rope_end(c):
            m = q.op("dve", lambda i, c=c: V.tensor_tensor(turned[:, c, :], turned[:, c, :], part[:, c, :], ALU.add if c else ALU.subtract), *prep["mul", c], name="turned%d" % c)
            prep["src", c] = split(cut(srcp, slice(None), c), turned[:, c, :], m, free=[prev("src_read")], name="turned_read%d" % c)

        def to_stack(n, g):
            w, scale = ((Wq, HD ** -0.5), (Wk, 1.0))[n]
            prep["hop", n, g] = project(w, srcp, g, full, cut(qk[n], slice(None), g), bqkv[:, n, g:g + 1], scale, [prep["src", 0], prep["src", 1]], prev("hop_read"), "qk%d%d" % (n, g), bk=SPARE_BANK)

        def hop_out():
            hop = [prep["hop", n, g] for n in range(2) for g in range(DC)]
            for n in range(2):
                for p in range(2):
                    prep["hopped"] = q.dma("sp", "d_hop", lambda i, n=n, p=p: SP.dma_start(hop_d[n, p].rearrange("g r s -> r g s"), f32_of(qk[n][p])), hop, prev("rows_in1"), name="hop_read")

        def stack_in(half, after):
            hs = slice(half * H1 // 2, (half + 1) * H1 // 2)
            stream = "d_stack%d" % half
            q.dma("pool", stream, lambda i: G.dma_start(rows_q[MAX_ROW:MAX_ROW + 1, hs], T["zeros"]), after)
            for n, (dst, order) in enumerate(((rows_q, (0, 1, 0, 1)), (rows_k, (0, 0, 1, 1)))):
                for k, p in enumerate(order):
                    q.dma("pool", stream, lambda i, n=n, k=k, p=p, dst=dst: G.dma_start(dst[k * 16:(k + 1) * 16, hs], hop_d[n, p, half].rearrange("(h f) s -> f h s", f=16)),
                          prep["hopped"], after, name="rows_in%d" % half)

        def v_in(t):
            m = product(bank[SPARE_BANK][:, 0:D], [(cut(srcp, slice(None), c, slice(t * P, (t + 1) * P)), cut(Wv, slice(None), c)) for c in range(DC)],
                        prep["src", 0], prep["src", 1], bank_free(SPARE_BANK), name="src_read")
            prep["Vc"] = q.op("dve", lambda i, t=t: V.tensor_tensor(Vc[:, t, :], bank[SPARE_BANK][:, 0:D], bv, ALU.add), m, prev("Vone%d" % (H1 // HG - 1)), name="bank%d" % SPARE_BANK)

        def v_place(g, after):
            dst = bass.AP(Vone.tensor, Vone.offset + g * HG * P, [Vone.ap[0], [H1 * P, TB], [P + 32, HG], [1, HD]])
            src = Vc[:, :, g * HG * HD:(g + 1) * HG * HD].rearrange("p t (k f) -> p t k f", k=HG)
            q.op("dve", lambda i: V.tensor_copy(dst, src), prep["Vc"], after, name="Vone%d" % g)

        plan = {1: lambda: take(0), 2: lambda: turn(0), 3: lambda: turn(1), 5: lambda: rope(0), 6: lambda: rope(1), 8: lambda: rope_end(0), 9: lambda: rope_end(1),
                12: lambda: to_stack(0, 0), 14: lambda: to_stack(1, 0), 16: lambda: to_stack(0, 1), 18: lambda: to_stack(1, 1), 20: hop_out,
                **{22 + 2 * t: lambda t=t: v_in(t) for t in range(TB)}}
        for s in sorted(plan):
            plan[s]()
        for half in range(2):
            stack_in(half, None)
        for g in range(H1 // HG):
            v_place(g, None)
        q.barrier()

        def maxima_r(h, j):
            return [(rows_q[:, h, j * P:(j + 1) * P], rows_k[:, h, :])], prev("rows_in%d" % (h // 8))

        def row_r(h):
            return rows_q[MAX_ROW:MAX_ROW + 1, h, :], None

        def scores_r(h, kt):
            return [(rows_k[:, h, kt * P:(kt + 1) * P], rows_q[:, h, :])]

        def values_r(h, kt):
            g, k = divmod(h, HG)
            return Vone[:, kt, h, :], OUT_BANKS[g % 2], k == 0 and kt == 0, k == HG - 1 and kt == TB - 1, prev("Vone%d" % g)

        later = {}

        def after_r(h, m):
            g, k = divmod(h, HG)
            if k == HG - 1:
                for x in {0: (), 1: (0, 1)}.get(g, (g,)):
                    v_place(x, m)
                bk = OUT_BANKS[g % 2]
                later[h + 1] = g, q.op("act", lambda i, g=g, bk=bk: A.activation(gathered_o[g % 2], bank[bk], ACT.Copy), m, later.get(("read", g - 2)) or prev("gathered_read%d" % (g % 2)), name="bank%d" % bk)
            if h in later or h == H1 - 1:
                g, m = later[h if h in later else h + 1]
                for t in range(TB):
                    m = q.op("pe", lambda i, g=g, t=t: PE.transpose(bank[SPARE_BANK][:, t * P:(t + 1) * P], gathered_o[g % 2][:, t * P:(t + 1) * P], ident), m, bank_free(SPARE_BANK), inc=t == TB - 1)
                later["read", g] = m
                q.names["gathered_read%d" % (g % 2)] = m
                o = bank[SPARE_BANK].rearrange("p (t k x) -> p t k x", t=TB, k=HG)
                r = q.op("dve", lambda i, o=o: V.reciprocal(sums, o[:, :, :, HD]), m)
                later["att"] = q.op("dve", lambda i, o=o, g=g: V.tensor_tensor(att[:, :, g * HG * HD:(g + 1) * HG * HD].rearrange("p t (k f) -> p t k f", k=HG), o[:, :, :, 0:HD],
                                                                              bass.AP(sums.tensor, sums.offset, [*sums.ap, [0, HD]]), ALU.mult), r, prev("att_T"), name="bank%d" % SPARE_BANK)

        def besides_r(s):
            if s in plan:
                plan[s]()

        def seconds_r(h):
            if h % 8 == 7:
                stack_in(h // 8, q.names["second"])

        done = attend_heads(buf, maxima_r, row_r, scores_r, values_r, besides_r, after_r, seconds_r)
        ready = []
        for c in range(DC):
            for t in range(TB):
                m = q.op("pe", lambda i, c=c, t=t: PE.transpose(bank[ST_BANKS[c]][:, t * P:(t + 1) * P], att[:, t, c * P:(c + 1) * P], ident),
                         later["att"], bank_free(ST_BANKS[c]), inc=t == TB - 1, name="att_T")
            ready.append(q.op(("dve", "act")[c], (lambda i, c=c: V.tensor_copy(attT[:, c, :], bank[ST_BANKS[c]])) if c == 0 else
                              (lambda i, c=c: A.activation(attT[:, c, :], bank[ST_BANKS[c]], ACT.Copy)), m, prev("att_read"), name="bank%d" % ST_BANKS[c]))
        out_projection(attT, Wo, bo, ready, DC)
        q.flush(B)
        q.barrier()
    if phases <= 4:
        return finish(q, out, X, SP)

    with ExitStack() as ph:
        HD, N, NG = 64, 512, H1 // 2
        SLOTS = 4
        buf = HeadBuffers(ph)
        Wq, Wk, Wv = (parts("W" + n, [P, DC, H1 * HD], ph) for n in "qkv")
        Wo = sb("Wo", [P, NG, D], where=ph)
        bo = sb("bo", [P, D], where=ph)
        srcp = parts("srcp", [P, DC, S], ph)
        ctxp = parts("ctxp", [P, DC, S], ph)
        ctxT = xT
        qs = [sb("qs%d" % k, [P, S], f32r, where=ph) for k in range(SLOTS)]
        ks = [sb("ks%d" % k, [P, S], f32r, where=ph) for k in range(SLOTS)]
        q2 = [sb("q2_%d" % k, [ROWS, S], f32r, where=ph) for k in range(SLOTS)]
        k2 = [sb("k2_%d" % k, [ROWS, S], f32r, where=ph) for k in range(SLOTS)]
        Vone = sb("Vone", [P, TB, NG, 3 * HD], where=ph)
        attT = sb("attT", [P, NG, S], where=ph)
        rinv = sb("rinv", [P, S], where=ph)
        for dst, src in ((Wo, T["Wo2"]), (bo, bass.AP(T["bo2"].tensor, 0, [[0, P], [1, D]]))):
            w_in = q.dma("act", "d_w0", lambda i, dst=dst, src=src: A.dma_start(dst, src))
        z = None
        for k in range(SLOTS):
            for t in (q2, k2):
                z = q.op("pool", lambda i, t=t, k=k: G.memset(f32_of(t[k][MAX_ROW:ROWS]), 0.0), z)
            z = q.op("pool", lambda i, k=k: G.memset(f32_of(k2[k][MAX_ROW:MAX_ROW + 1]), 1.0), z)
        q.op("pool", lambda i: G.memset(Vone[:, :, :, HD:2 * HD], 1.0), z)
        stage = attT.rearrange("p g s -> p (g s)").rearrange("p (k c n) -> p k c n", k=2, c=DC)
        w_done = []
        for k, (t, n) in enumerate(((Wq, "Wq2"), (Wk, "Wk2"), (Wv, "Wv2"))):
            w_done.append(weights_in(t, stage[:, k % 2], T[n], w_done[0] if k == 2 else None, k % 2))
        q.barrier()

        free, prep = {}, {}

        def rows_of_next(i):
            return X[:, bass.ds((i + 1) * TB, TB), :] if i is not None else X[:, 0:TB, :]

        def ctx_of_next(i):
            return (T["ctxT"][bass.ds(i + 1, 1)] if i is not None else T["ctxT"][0:1]).rearrange("a p c s -> p (a c) s")

        def fetch():
            prep["xs"] = q.op("dve", lambda i: V.tensor_copy(xs, rows_of_next(i)), prev("xs_read"))
            prep["ctx"] = q.dma("sp", "d_ctx", lambda i: SP.dma_start(ctxT, ctx_of_next(i)), prev("ctx_read"))

        def ctx_in():
            prep["k"] = split(ctxp, ctxT, prep["ctx"], free=[q.names.get("ctxp_read")], name="ctx_read")

        def turn(c):
            for t in range(TB):
                m = q.op("pe", lambda i, c=c, t=t: PE.transpose(bank[SPARE_BANK][:, t * P:(t + 1) * P], xs[:, t, c * P:(c + 1) * P], ident),
                         prep["xs"], bank_free(SPARE_BANK), inc=t == TB - 1, name="xs_read")
            prep["q", c] = split(cut(srcp, slice(None), c), bank[SPARE_BANK], m, free=[q.names.get("srcp_read")], name="bank%d" % SPARE_BANK)

        def pair_product(g, of):
            if of == "q":
                w, src, bk, r = Wq, srcp, SPARE_BANK, [prep.get(("q", 0)), prep.get(("q", 1))]
            else:
                w, src, bk, r = Wk, ctxp, ROW_BANK, prep.get("k")
            prep[of, "ps"] = product(bank[bk], [(cut(w, slice(None), c, slice(g * P, (g + 1) * P)), cut(src, slice(None), c)) for c in range(DC)],
                                     r, bank_free(bk), name={"q": "srcp_read", "k": "ctxp_read"}[of])

        def head_in(h, of):
            z, m = h % SLOTS, prep[of, "ps"]
            ps = bank[SPARE_BANK if of == "q" else ROW_BANK][(h % 2) * HD:(h % 2 + 1) * HD]
            f = free.get((h - SLOTS) % H1)
            if of == "q":
                a = q.op("act", lambda i: A.activation(qs[z][0:HD], ps, ACT.Copy, scale=HD ** -0.5), m, f)
                b = q.op("pool", lambda i: G.tensor_copy(q2[z][0:HD], f32_of(qs[z][0:HD])), a, f, plain=True)
                c = q.op("dve", lambda i: V.scalar_tensor_tensor(qs[z][HD:2 * HD], ps, HD ** -0.5, f32_of(qs[z][0:HD]), ALU.mult, ALU.subtract), a, name="bank%d" % SPARE_BANK)
            else:
                a = q.op("act", lambda i: A.activation(ks[z][0:HD], ps, ACT.Copy), m, f)
                b = q.op("act", lambda i: A.activation(ks[z][HD:2 * HD], f32_of(ks[z][0:HD]), ACT.Copy), a)
                c = q.op("dve", lambda i: V.tensor_tensor(k2[z][0:HD], ps, f32_of(ks[z][0:HD]), ALU.subtract), a, name="bank%d" % ROW_BANK)
            q.names["%s_of%d" % (of, h)] = [a, b, c]

        def v_in(t, n, bk):
            m = product(bank[bk], [(cut(ctxp, slice(None), c, slice(t * P, (t + 1) * P)), cut(Wv, slice(None), c, slice(n * N, (n + 1) * N))) for c in range(DC)],
                        bank_free(bk), name="ctxp_read")
            dst = bass.AP(Vone.tensor, Vone.offset + (t * NG + n * NG // 2) * 3 * HD, [Vone.ap[0], [3 * HD, NG // 2], [2 * HD, 2], [1, HD]])
            src = bank[bk].rearrange("p (g k f) -> p g k f", g=NG // 2, k=2)
            q.names["V", n, t] = q.op("act", lambda i: A.activation(dst, src, ACT.Copy), m, prev("pv_last"), name="bank%d" % bk)

        plan = {0: [lambda: v_in(0, 0, SPARE_BANK), lambda: v_in(1, 0, ROW_BANK)], 2: [lambda: v_in(2, 0, SPARE_BANK), lambda: v_in(3, 0, ROW_BANK)],
                8: [lambda: v_in(0, 1, SPARE_BANK)], 9: [lambda: v_in(1, 1, SPARE_BANK)], 10: [lambda: v_in(2, 1, SPARE_BANK)], 16: [lambda: v_in(3, 1, SPARE_BANK)],
                48: [fetch], 54: [ctx_in], 56: [lambda: turn(0)], 57: [lambda: turn(1)]}
        for g in range(NG):
            nxt = (g + 1) % NG
            plan.setdefault(8 * g + 3, []).extend([lambda nxt=nxt: pair_product(nxt, "q"), lambda nxt=nxt: head_in(2 * nxt, "q")])
            plan.setdefault(8 * g + 5, []).extend([lambda nxt=nxt: pair_product(nxt, "k"), lambda nxt=nxt: head_in(2 * nxt, "k")])
            plan.setdefault(8 * g + 7, []).extend([lambda nxt=nxt, of=of: head_in(2 * nxt + 1, of) for of in "qk"])
        for s in (48, 54, 56, 57):
            plan[s][0]()
        for of in "qk":
            pair_product(0, of)
            head_in(0, of)
            head_in(1, of)
        q.barrier()
        prep.clear()

        quarters = {}

        def besides(s):
            for f in plan.get(s, []) + quarters.get(s, []):
                f()

        def operands_of(h):
            return [prev("q_of%d" % h), prev("k_of%d" % h)] if h < 2 else [q.names["q_of%d" % h], q.names["k_of%d" % h]]

        def maxima_x(h, j):
            z = h % SLOTS
            return [(qs[z][:, j * P:(j + 1) * P], ks[z])], operands_of(h)

        def row_x(h):
            return q2[h % SLOTS][MAX_ROW:MAX_ROW + 1, :], None

        def scores_x(h, kt):
            z = h % SLOTS
            return [(ks[z][:, kt * P:(kt + 1) * P], qs[z]), (k2[z][:, kt * P:(kt + 1) * P], q2[z])]

        def values_x(h, kt):
            return Vone[:, kt, h // 2, (h % 2) * HD:(h % 2) * HD + P], OUT_BANKS[h % 2], kt == 0, kt == TB - 1, q.names["V", h // 8, kt]

        def after_x(h, m):
            o, s_ = (slice(0, HD), slice(HD, P)) if h % 2 == 0 else (slice(HD, P), slice(0, HD))
            ps = bank[OUT_BANKS[h % 2]]
            def over(t):
                cols = slice(t * P, (t + 1) * P)
                r = q.op("dve", lambda i: V.reciprocal(rinv[o, cols], ps[s_, cols]), m)
                if t == TB - 1:
                    prep["att"] = q.op("dve", lambda i: V.tensor_tensor(attT[o, h // 2, :], ps[o], rinv[o], ALU.mult), r, prev("att_read"), name="bank%d" % OUT_BANKS[h % 2])

            for t in range(TB):
                if h == H1 - 1:
                    over(t)
                else:
                    quarters.setdefault(TB * (h + 1) + OUT_LAG + t - 1, []).append(lambda t=t: over(t))

        def seconds_x(h):
            free[h] = q.names["second"]

        done = attend_heads(buf, maxima_x, row_x, scores_x, values_x, besides, after_x, seconds_x)
        out_projection(attT, Wo, bo, prep["att"], NG)
        q.flush(B)
        q.barrier()
    if phases <= 5:
        return finish(q, out, X, SP)

    with ExitStack() as ph:
        gidx_all = sb("gidx_all", [P, (E1 + 2) * CT1], i32, where=ph)
        sidx_all = sb("sidx_all", [P, E1 * CT1], i32, where=ph)
        slot_w = sb("slot_w", [P, E1 * CT1], where=ph)
        with ExitStack() as route:
            TE = [P, NT, E1]
            gw = sb("gw", [P, DC, E1], where=route)
            L = sb("L", TE, where=route)
            shifted = sb("shifted", TE, where=route)
            left = sb("left", TE, where=route)
            chosen = sb("chosen", TE, where=route)
            weight = sb("weight", TE, where=route)
            top = sb("top", [P, NT, 8], where=route)
            cols = sb("cols", [P, 3, NT], where=route)
            marks16 = sb("marks16", TE, bf16, where=route)
            before16 = sb("before16", TE, bf16, where=route)
            tri = sb("tri", [P, 2, P], bf16, where=route)
            keep = sb("keep", TE, where=route)
            place = sb("place", TE, i32, where=route)
            hi_i = sb("hi_i", TE, i32, where=route)
            lo_i = sb("lo_i", TE, i32, where=route)
            hi = sb("hi", TE, where=route)
            lo = sb("lo", TE, where=route)
            ramp = sb("ramp", [P, 32], where=route)
            token1 = sb("token1", [P, NT], where=route)
            A_ = [sb("A%d" % b, [P, NT, 8, 16], where=route) for b in range(2)]
            B_ = [sb("B%d" % b, [P, NT, 8, 16], where=route) for b in range(2)]
            BV = [sb("BV%d" % b, [P, NT, 2, 128], where=route) for b in range(2)]
            diag = sb("diag", [P, 8], where=route)
            cross = sb("cross", [P, 2, 8, 16], where=route)
            slots = sb("slots", [P, 4, 2, 16], where=route)
            slot_rows = sb("slot_rows", [E1 * CT1, 2, P], where=route)
            slot_n = sb("slot_n", [P, 2, E1 * CT1], where=route)
            for dst, n in ((gw, "gw"), (tri, "tri"), (ramp, "ramp"), (token1, "token1"), (diag, "diag")):
                w_in = q.dma("act", "d_w0", lambda i, dst=dst, n=n: A.dma_start(dst, T[n]))
            acc_in = q.dma("pool", "d_sc0", lambda i: G.dma_start(acc_d.rearrange("(t p) d -> p t d", p=P), X[:, 0:NT, :]))
            rows_in = q.dma("pool", "d_sc1", lambda i: G.dma_start(rows_d.rearrange("(t p) d -> p t d", p=P)[:, :, 0:D], X[:, 0:NT, :]))
            q.flush()
            x_ready = take_batch()
            for t in range(TB):
                for c in range(DC):
                    m = q.op("pe", lambda i, t=t, c=c: PE.matmul(bank[2][:, t * E1:(t + 1) * E1], xT[:, c, t * P:(t + 1) * P], gw[:, c, :], start=c == 0, stop=c == DC - 1),
                             x_ready, w_in, prev("logits"), name="xT_read")
            q.op("dve", lambda i: V.tensor_copy(L[:, bass.ds(i * TB, TB), :].rearrange("p t e -> p (t e)"), bank[2][:, 0:TB * E1]), m, name="logits")
            q.names["summed_all"] = q.names["logits"]
            q.flush(B)
            q.barrier()

            def every(ap, n):
                return bass.AP(ap.tensor, ap.offset, [*ap.ap, [0, n]])

            m = q.op("dve", lambda i: V.tensor_reduce(cols[:, 0, :], L, AX.X, ALU.max))
            m = q.op("dve", lambda i: V.tensor_tensor(shifted, L, every(cols[:, 0, :], E1), ALU.subtract), m)
            m_exp = q.op("act", lambda i: A.activation(shifted, shifted, ACT.Exp), m)
            for t in range(NT):
                m = q.op("dve", lambda i, t=t: V.max(top[:, t, :], L[:, t, :]))
            for t in range(NT):
                m2 = q.op("dve", lambda i, t=t: V.match_replace(left[:, t, :], top[:, t, :], L[:, t, :], -3e38), m)
            m = q.op("dve", lambda i: V.tensor_tensor(chosen, left, L, ALU.not_equal), m2)
            c16 = q.op("act", lambda i: A.activation(marks16, chosen, ACT.Copy), m)
            w = q.op("dve", lambda i: V.tensor_tensor(weight, shifted, chosen, ALU.mult), m, m_exp)
            w = q.op("dve", lambda i: V.tensor_reduce(cols[:, 1, :], weight, AX.X, ALU.add), w)
            w = q.op("dve", lambda i: V.reciprocal(cols[:, 2, :], cols[:, 1, :]), w)
            w = q.op("dve", lambda i: V.tensor_tensor(weight, weight, every(cols[:, 2, :], E1), ALU.mult), w)
            r = q.op("pool", lambda i: G.memset(before16[:, 0, :], 0.0))
            for t in range(1, NT):
                r = q.op("pool", lambda i, t=t: G.tensor_tensor(before16[:, t, :], before16[:, t - 1, :], marks16[:, t - 1, :], ALU.add), r, c16)
            for t in range(NT):
                q.op("pe", lambda i, t=t: PE.matmul(bank[0][:, t * E1:(t + 1) * E1], tri[:, 0, :], marks16[:, t, :], start=True, stop=False), c16, w_in, inc=False)
                n = q.op("pe", lambda i, t=t: PE.matmul(bank[0][:, t * E1:(t + 1) * E1], tri[:, 1, :], before16[:, t, :], start=False, stop=True), r)
            upto = bank[0].rearrange("p (t e) -> p t e", e=E1)
            k = q.op("dve", lambda i: V.scalar_tensor_tensor(keep, upto, float(CAP), chosen, ALU.is_le, ALU.mult), n, m)
            n = q.op("dve", lambda i: V.tensor_scalar(place, upto, -1.0, None, ALU.add), n)
            a = q.op("dve", lambda i: V.tensor_scalar(hi_i, place, 4, None, ALU.arith_shift_right), n)
            b = q.op("dve", lambda i: V.tensor_scalar(lo_i, place, 15, None, ALU.bitwise_and), n)
            a = q.op("dve", lambda i: V.tensor_copy(hi, hi_i), a)
            b = q.op("dve", lambda i: V.tensor_copy(lo, lo_i), b)
            a = q.op("dve", lambda i: V.scalar_tensor_tensor(hi, hi, 1.0, keep, ALU.add, ALU.mult), a, k)
            read, free = {}, {}
            for g in range(4):
                e8 = slice(g * 8, g * 8 + 8)
                z = g % 2

                def along(ap):
                    return bass.AP(ap.tensor, ap.offset, [ap.ap[0], [0, NT], [0, 8], [1, 16]])

                def per_tile(ap):
                    return bass.AP(ap.tensor, ap.offset, [*ap.ap, [0, 8], [0, 16]])

                def value(v, z=z):
                    ap = BV[z][:, :, v, :]
                    return ap.rearrange("p t (e j) -> p t e j", j=16)

                qa = q.op("dve", lambda i, e8=e8, z=z: V.tensor_tensor(A_[z], every(hi[:, :, e8], 16), along(ramp[:, 0:16]), ALU.is_equal), a, read.get(g - 2), w_in)
                qb = q.op("dve", lambda i, e8=e8, z=z: V.tensor_tensor(B_[z], every(lo[:, :, e8], 16), along(ramp[:, 16:32]), ALU.is_equal), b, free.get(g - 2), w_in)
                qc = q.op("pool", lambda i, z=z, value=value: G.tensor_tensor(value(0), B_[z], per_tile(token1), ALU.mult), qb, read.get(g - 2))
                qd = q.op("dve", lambda i, e8=e8, z=z, value=value: V.tensor_tensor(value(1), B_[z], every(weight[:, :, e8], 16), ALU.mult), qb, w, read.get(g - 2))
                free[g] = [qc, qd]
                for t in range(NT):
                    n = q.op("pe", lambda i, t=t, z=z: PE.matmul(bank[1 + z][:, 0:256], A_[z][:, t, :, :].rearrange("p e j -> p (e j)"), BV[z][:, t, :, :].rearrange("p v j -> p (v j)"),
                                                               start=t == 0, stop=t == NT - 1), qa, qc, qd, free.get(("bank", z)), inc=t == NT - 1)
                read[g] = n
                ps = bank[1 + z][:, 0:256].rearrange("p (v x) -> p v x", v=2).rearrange("p v (e j) -> p v e j", j=16)
                on = bass.AP(diag.tensor, diag.offset, [diag.ap[0], [0, 2], [1, 8], [0, 16]])
                n = q.op("dve", lambda i, ps=ps, on=on: V.tensor_tensor(cross, ps, on, ALU.mult), n, free.get("cross"))
                free["bank", z] = n
                n = q.op("dve", lambda i, g=g: V.tensor_reduce(slots[:, g, :, :], cross.rearrange("p v e j -> p v j e"), AX.X, ALU.add), n)
                free["cross"] = n
                for v in range(2):
                    d = q.dma("sp", "d_slot", lambda i, g=g, v=v: SP.dma_start(slot_d[v, g * 2048:(g + 1) * 2048].rearrange("(p j) -> p j", j=16), slots[:, g, v, :]), n)
            d = q.dma("sp", "d_slot", lambda i: SP.dma_start(slot_rows, slot_d.rearrange("v (r c) -> r v c", c=P)), d)
            for v in range(2):
                n = q.op("pe", lambda i, v=v: PE.transpose(bank[3][:, v * 64:(v + 1) * 64], slot_rows[:, v, :], ident[0:64, 0:64]), d)
            n = q.op("dve", lambda i: V.tensor_copy(slot_n.rearrange("p v r -> p (v r)"), bank[3][:, 0:128]), n)
            kept = q.op("dve", lambda i: V.tensor_copy(slot_w, slot_n[:, 1, :]), n)
            q.op("dve", lambda i: V.tensor_scalar(gidx_all[:, 0:E1 * CT1], slot_n[:, 0, :], -1.0, 0.0, ALU.add, ALU.max), n)
            m = q.op("dve", lambda i: V.tensor_scalar(slot_n[:, 1, :], slot_n[:, 0, :], 0.5, float(1 << 16), ALU.is_lt, ALU.mult), kept)
            q.op("dve", lambda i: V.scalar_tensor_tensor(sidx_all, slot_n[:, 0, :], -1.0, slot_n[:, 1, :], ALU.add, ALU.add), m)
            q.op("dve", lambda i: V.memset(gidx_all[:, E1 * CT1:], 0))
            q.barrier()

        Wgu = [sb("Wgu%d" % b, [P, DC, 2 * F1], where=ph) for b in range(2)]
        Wdn = [sb("Wdn%d" % b, [FH, 2, D], where=ph) for b in range(2)]
        gidx = [sb("gidx%d" % b, [P, CT1], i32, where=ph) for b in range(2)]
        sidx1 = [sb("sidx1_%d" % b, [P, CT1], i32, where=ph) for b in range(2)]
        rows1 = [sb("rows1_%d" % b, [P, CT1, GW], where=ph) for b in range(2)]
        RT = [sb("RT%d" % b, [P, DC, CAP], where=ph) for b in range(2)]
        act1 = [sb("act1_%d" % b, [FH, 2, CAP], where=ph) for b in range(2)]
        h1 = [sb("h1_%d" % b, [FH, 2, CAP], where=ph) for b in range(2)]
        res = [sb("res%d" % b, [P, CT1, D], where=ph) for b in range(2)]

        def gather1(i, b, rows_free):
            m = q.op("pool", lambda _, b=b, i=i: G.tensor_copy(gidx[b], gidx_all[:, i(_, b)]), rows_free, q.names.get("gathered%d" % b))
            for t in range(CT1):
                q.dma("pool", "d_g%d" % b, lambda _, b=b, t=t: G.indirect_dma_start(rows1[b][:, t, :], None, rows_d, bass.IndirectOffsetOnAxis(ap=gidx[b][:, t:t + 1], axis=0)),
                      m, rows_free, name="gathered%d" % b)

        for b in range(2):
            gather1(lambda _, b: slice(b * CT1, (b + 1) * CT1), b, None)
        q.flush()
        for b in range(2):
            w = q.dma("sp", "d_e%d" % b, lambda i, b=b: SP.dma_start(Wgu[b], T["Wgu"][bass.ds(2 * i + b, 1)].rearrange("a p c f -> p (a c) f")), prev("W_read%d" % b))
            w = q.dma("sp", "d_e%d" % b, lambda i, b=b: SP.dma_start(Wdn[b], T["Wdn"][bass.ds(2 * i + b, 1)].rearrange("a p c f -> p (a c) f")), prev("W_read%d" % b))
        for b in range(2):
            g = prev("gathered%d" % b)
            w = Mark("d_e%d" % b, q.count["d_e%d" % b], q.section)
            for c in range(DC):
                for t in range(CT1):
                    m = q.op("pe", lambda i, b=b, t=t, c=c: PE.transpose(bank[b][:, c * CAP + t * P:c * CAP + (t + 1) * P], rows1[b][:, t, c * P:(c + 1) * P], ident),
                             g, prev("RT%d" % b), inc=t == CT1 - 1, name="rows_read%d" % b)
            gather1(lambda i, b: bass.ds((2 * i + b + 2) * CT1, CT1), b, m)
            rt = q.op("act", lambda i, b=b: A.activation(RT[b].rearrange("p c s -> p (c s)"), bank[b], ACT.Copy), m, prev("RT_read%d" % b), name="RT%d" % b)
            for half in range(2):
                for f in range(2):
                    for c in range(DC):
                        m = q.op("pe", lambda i, b=b, half=half, f=f, c=c: PE.matmul(bank[2 + 2 * b + half][0:FH, f * CAP:(f + 1) * CAP],
                                                                             Wgu[b][:, c, half * F1 + f * FH:half * F1 + (f + 1) * FH], RT[b][:, c, :], start=c == 0, stop=c == DC - 1),
                                 w, rt, prev("act1_%d" % b) if half == 0 else prev("h1_%d" % b), inc=c == DC - 1, name="RT_read%d" % b)
                if half == 0:
                    s_ = q.op("act", lambda i, b=b: A.activation(act1[b].rearrange("p c s -> p (c s)"), bank[2 + 2 * b][0:FH, :], ACT.Silu), m, prev("h1_%d" % b), name="act1_%d" % b)
            h = q.op("dve", lambda i, b=b: V.tensor_tensor(h1[b].rearrange("p c s -> p (c s)"), bank[3 + 2 * b][0:FH, :], act1[b].rearrange("p c s -> p (c s)"), ALU.mult), m, s_, prev("h_read%d" % b), name="h1_%d" % b)
            for t in range(CT1):
                for f in range(2):
                    m = q.op("pe", lambda i, b=b, t=t, f=f: PE.matmul(bank[6 + b][:, t * D:(t + 1) * D], h1[b][:, f, t * P:(t + 1) * P], Wdn[b][:, f, :], start=f == 0, stop=f == 1),
                             h, w, prev("res%d" % b), inc=f == 1, name="h_read%d" % b)
            q.names["W_read%d" % b] = m
            c_ = q.op("pool", lambda i, b=b: G.tensor_copy(sidx1[b], sidx_all[:, bass.ds((2 * i + b) * CT1, CT1)]), prev("stored%d" % b))
            for t in range(CT1):
                r = q.op("dve", lambda i, b=b, t=t: V.tensor_scalar(res[b][:, t, :], bank[6 + b][:, t * D:(t + 1) * D], slot_w[:, bass.ds((2 * i + b) * CT1 + t, 1)], None, ALU.mult),
                         m, prev("stored%d" % b), name="res%d" % b)
            last = q.names["stored0"] if b else prev("stored1")
            for t in range(CT1):
                q.dma("pool", "d_sc%d" % b, lambda i, b=b, t=t: G.indirect_dma_start(acc_d, bass.IndirectOffsetOnAxis(ap=sidx1[b][:, t:t + 1], axis=0), res[b][:, t, :], None,
                                                                            compute_op=ALU.add, bounds_check=B * S - 1, oob_is_err=False),
                      r, c_, last, name="stored%d" % b)
        q.flush(E1 // 2)
        q.barrier()
    norm_from_acc()
    return finish(q, out, X, SP)


def finish(q, out, X, SP):
    q.dma("sp", "d_out", lambda i: SP.dma_start(out.rearrange("(t p) d -> p t d", p=P), X[:, 0:NT, :]))
    q.barrier()


def constants():
    k = np.abs(np.fft.fftfreq(D)).astype(np.float32) + np.float32(1e-8)
    n = np.arange(D)
    rows, freq = [], []
    for j in range(D // 2 + 1):
        w = np.sqrt((1.0 if j in (0, D // 2) else 2.0) / D)
        rows.append(w * np.cos(2 * np.pi * ((j * n) % D) / D)); freq.append(j)
        if j not in (0, D // 2):
            rows.append(w * np.sin(2 * np.pi * ((j * n) % D) / D)); freq.append(j)
    basis = np.array(rows, np.float32)
    ka = k[np.array(freq)]
    kc = ka.reshape(DC, P).T
    kcols = np.concatenate([kc, kc * kc], 1)
    lx = np.log(np.array(FRACTAL, np.float64))
    den = 5 * np.sum(lx * lx) - np.sum(lx) ** 2
    weights = -(5 * lx - np.sum(lx)) / den
    sizes = np.array([s * s for s in FRACTAL])
    fmask = (np.arange(1024)[None, :] < sizes[:, None]).astype(np.float32)
    fconst = np.concatenate([np.repeat(weights[:, None], P, 1), 1.0 / sizes[:, None]], 1).astype(np.float32)
    A12 = np.array([[1, 1, 1, 0, 1, 1, 1, 0, 0, 0, 1, 1], [1, 1, 0, 1, 1, 1, 0, 0, 0, 1, 1, 0], [1, 0, 1, 1, 1, 0, 0, 0, 1, 1, 0, 1],
                    [0, 1, 1, 1, 0, 0, 0, 1, 1, 0, 1, 1], [0, 0, 0, 0, 1, 1, 1, 1, 1, 1, 1, 1], [1, 1, 1, 1, 0, 0, 0, 0, 0, 0, 0, 0],
                    [0, 0, 0, 0, 1, 1, 1, 1, 0, 0, 0, 0], [1, 1, 0, 0, 1, 1, 0, 0, 1, 1, 0, 0], [1, 0, 1, 0, 1, 0, 1, 0, 1, 0, 1, 0],
                    [0, 1, 0, 1, 0, 1, 0, 1, 0, 1, 0, 1], [1, 0, 0, 1, 1, 0, 0, 1, 1, 0, 0, 1], [0, 1, 1, 0, 0, 1, 1, 0, 0, 1, 1, 0]], np.float32)
    Hm = np.concatenate([A12.T, np.eye(12, dtype=np.float32)], axis=1)
    golay = np.zeros((24, 48), np.float32)
    golay[:, 0:12] = Hm.T
    golay[0:12, 24:48] = 1.0
    sel = np.zeros((2, 10), np.float32)
    sel[0, 0:5] = 1.0
    sel[1, 5:10] = 1.0
    lower = np.tril(np.ones((P, P), np.float32), -1)
    freq = np.exp(np.arange(0, D, 2, dtype=np.float32) * np.float32(-np.log(10000.0) / D))
    ang = (np.arange(S, dtype=np.float32)[:, None] * freq[None, :]).astype(np.float32)
    cs = np.stack([np.cos(ang).T, np.sin(ang).T], 1).astype(np.float32)
    tri = np.stack([np.triu(np.ones((P, P))), np.ones((P, P))], 1).astype(mybir.dt.np(bf16))
    ramp = np.concatenate([np.arange(1, 17), np.arange(16)]).astype(np.float32)[None].repeat(P, 0)
    token1 = (np.arange(P)[:, None] + P * np.arange(NT)[None, :] + 1).astype(np.float32)
    diag = (np.arange(P)[:, None] // 16 == np.arange(8)[None, :]).astype(np.float32)
    return {"zeros": np.zeros((1, H1 // 2, S), np.float32), "tri": tri, "ramp": ramp, "token1": token1, "diag": diag, "lower": lower, "cs": cs, "ident": np.eye(P, dtype=np.float32), "basis": basis.reshape(DC, P, D).transpose(1, 0, 2), "kcols": kcols.astype(np.float32),
            "fmask": fmask, "fconst": fconst, "golay": golay, "sel": sel}


def chunks(w):
    return w.reshape(w.shape[0] // P, P, *w.shape[1:]).swapaxes(0, 1)


def layout(x, **w):
    a = constants()
    a["x"] = x.reshape(B * S, D)
    a["W_el"] = chunks(w["L0_attn_W_el"])
    a["W_le"] = np.concatenate([w["L0_attn_W_le"], w["L0_attn_b_le"][None]], 0)
    a["b_el"] = w["L0_attn_b_el"][:, None]
    g = "L0_xattn_"
    for n in ("Wq_c", "Wk_s", "Wv_s", "Wq_s", "Wk_c", "Wv_c", "Wg"):
        a[n] = chunks(w[g + n].T)
    a["bias0"] = np.stack([w[g + n].reshape(DC, P).T for n in ("bq_c", "bk_s", "bv_s", "bq_s", "bk_c", "bv_c", "bg")], 1)
    a["ctxT"] = np.concatenate([w["ctx_1024"].reshape(B, S, DC, P).transpose(0, 3, 2, 1), np.zeros((1, P, DC, S), np.float32)], 0)
    g = "L0_ffn_"
    a["W1"] = w[g + "W1"].reshape(E0, DC, P, F0).transpose(0, 2, 1, 3)
    a["W2"] = w[g + "W2"].reshape(E0, FC0, P, D).transpose(0, 2, 1, 3)
    a["b1"] = w[g + "b1"].reshape(E0 * FC0, P).T
    a["b2"] = w[g + "b2"]
    tok = w[g + "top_idx"].T
    a["tok"] = tok
    a["idx"] = tok.reshape(E0 * CT0, P).T
    a["combine"] = w[g + "combine_weights"]
    g = "L1_attn_"
    for n in ("Wq", "Wk", "Wv", "Wo"):
        a[n + "1"] = chunks(w[g + n].T)
    a["bqkv"] = np.stack([w[g + n].reshape(DC, P).T for n in ("bq", "bk", "bv")], 1)
    a["bv1"] = w[g + "bv"][None]
    a["bo1"] = w[g + "bo"][None]
    g = "L1_xattn_"
    for n in ("Wq", "Wk", "Wv", "Wo"):
        a[n + "2"] = chunks(w[g + n])
    a["bo2"] = w[g + "bo"][None]
    g = "L1_ffn_"
    a["gw"] = chunks(w[g + "gate_weight"].T)
    a["Wgu"] = w[g + "gate_up_proj"].reshape(E1, 2 * F1, DC, P).transpose(0, 3, 2, 1)
    a["Wdn"] = w[g + "down_proj"].reshape(E1, D, 2, FH).transpose(0, 3, 2, 1)
    return {k: np.ascontiguousarray(v) for k, v in a.items()}


def kernel(**inputs):
    from concourse import bacc
    from concourse.bass_utils import run_bass_kernel_spmd

    arrays = layout(**{k: np.asarray(v) for k, v in inputs.items()})
    nc = bacc.Bacc("TRN2", target_bir_lowering=False, num_devices=1)
    T = {k: nc.dram_tensor("in_" + k, v.shape, mybir.dt.from_np(v.dtype), kind="ExternalInput").ap() for k, v in arrays.items()}
    out = nc.dram_tensor("out_0", (B * S, D), f32, kind="ExternalOutput").ap()
    program(nc, T, out)
    r = run_bass_kernel_spmd(nc, [{"in_" + k: v for k, v in arrays.items()}], core_ids=[0])
    return r.results[0]["out_0"].reshape(B, S, D)
```

```python
from contextlib import ExitStack

import numpy as np
import concourse.bass as bass
from concourse import mybir

f32, f32r, bf16, i32 = mybir.dt.float32, mybir.dt.float32r, mybir.dt.bfloat16, mybir.dt.int32
ACT = mybir.ActivationFunctionType
ALU = mybir.AluOpType
AX = mybir.AxisListType

P = 128
B, S, D = 4, 512, 256
NT = B * S // P
TB = S // P
DC = D // P
EPS = 1e-5
E0, C0, F0 = 8, 512, 1024
FC0, CT0 = F0 // P, C0 // P
H1 = 16
E1, F1, CAP, TOPK = 32, 192, 256, 8
FH = F1 // 2
CT1 = CAP // P
GW = D + E0
FRACTAL = (2, 4, 8, 16, 32)
CREDIT = 1024


class Mark:

    def __init__(self, sem, k, section):
        self.sem, self.k, self.section = sem, k, section


class prev:

    def __init__(self, name):
        self.name = name


class Queue:

    def __init__(self, nc, ctx):
        self.nc, self.ctx = nc, ctx
        self.eng = {"pe": nc.tensor, "dve": nc.vector, "act": nc.scalar, "pool": nc.gpsimd, "sp": nc.sync}
        self.sems, self.base = {}, {}
        self.fence = ctx.enter_context(nc.semaphore("s_fence"))
        for e in ("pe", "dve", "act", "pool"):
            self._sem(e)
        self.section, self.ops, self.count, self.names, self.past = 0, [], {}, {}, {}

    def _sem(self, name, credit=CREDIT):
        if name not in self.sems:
            self.sems[name] = self.ctx.enter_context(self.nc.semaphore("s_" + name))
            self.base[name] = credit
            if credit:
                self.nc.sync.sem_inc(self.sems[name], credit)

    def _add(self, e, sem, by, fn, after, name, plain=False):
        mark = None
        if sem:
            self.count[sem] = self.count.get(sem, 0) + by
            mark = Mark(sem, self.count[sem], self.section)
            if name:
                self.names[name] = mark
        flat, rest = [], list(after)
        while rest:
            a = rest.pop(0)
            if isinstance(a, (list, tuple)):
                rest += a
            else:
                flat.append(a)
        self.ops.append((e, sem, by, fn, [a for a in flat if a is not None], plain))
        return mark

    def op(self, e, fn, *after, name=None, inc=True, plain=False):
        return self._add(e, e if inc else None, 1, fn, after, name, plain)

    def dma(self, e, stream, fn, *after, name=None):
        self._sem(stream, 0 if e == "pool" else CREDIT)
        return self._add(e, stream, 16, fn, after, name, plain=e != "act")

    def _value(self, mark, n):
        base, per, times = self.past[mark.section]
        return base[mark.sem] + (times - 1) * per.get(mark.sem, 0) + mark.k

    def flush(self, n=None):
        ops, per, base = self.ops, self.count, dict(self.base)
        names, me, eng = self.names, self.section, self.eng
        outer, todo = {}, []
        for e, sem, by, fn, after, plain in ops:
            waits = []
            for a in after:
                lag = isinstance(a, prev)
                if lag and n is None:
                    continue
                a = names[a.name] if lag else a
                for mark in a if isinstance(a, list) else [a]:
                    if mark.section == me:
                        waits.append((mark.sem, mark.k - lag * per[mark.sem]))
                        assert base[mark.sem] + waits[-1][1] > 0, (mark.sem, mark.k)
                    else:
                        outer[e, mark.sem] = max(outer.get((e, mark.sem), 0), self._value(mark, n))
            todo.append((e, sem, by, fn, waits, plain))
        for (e, s), v in outer.items():
            eng[e].wait_ge(self.sems[s], v)

        def emit(i):
            at, seen = {}, {}
            for e, sem, by, fn, waits, plain in todo:
                need = {}
                for s, k in waits:
                    need[s] = max(k, need.get(s, k))
                for s in need if n is not None else ():
                    if (e, s) not in at:
                        at[e, s] = eng[e].snap(i * per[s] + base[s])
                for s, k in need.items():
                    if seen.get((e, s), -1 << 30) >= k:
                        continue
                    seen[e, s] = k
                    if n is None:
                        eng[e].wait_ge(self.sems[s], base[s] + k)
                    else:
                        eng[e].wait_ge(self.sems[s], at[e, s] + k)
                        if plain:
                            eng[e].sem_inc(self.fence, 1)
                ins = fn(i)
                if sem:
                    ins.then_inc(self.sems[sem], by)

        if n is None:
            emit(None)
        else:
            with self.nc.Fori(0, n) as i:
                emit(i)
        for s, c in per.items():
            self.base[s] += c * (n or 1)
        self.past[me] = (base, per, n or 1)
        self.section += 1
        self.ops, self.count, self.names = [], {}, {}

    def barrier(self):
        self.flush()
        for e in self.eng.values():
            for s, sem in self.sems.items():
                if self.base[s] not in (0, CREDIT):
                    e.wait_ge(sem, self.base[s])


def program(nc, T, out):
    ctx = ExitStack()
    with ctx:
        ctx.enter_context(nc.allow_non_contiguous_dma(reason="broadcasts and small tables"))
        build(nc, ctx, T, out)


def build(nc, ctx, T, out):
    q = Queue(nc, ctx)
    V, A, PE, G, SP = nc.vector, nc.scalar, nc.tensor, nc.gpsimd, nc.sync

    used = {}

    def sb(name, shape, dt=f32, where=ctx):
        used[name] = used.get(name, 0) + 1
        if used[name] > 1:
            name += "_use%d" % used[name]
        return where.enter_context(nc.sbuf_tensor(name, shape, dt))[tuple(slice(None) for _ in shape)]

    bank = [ctx.enter_context(nc.psum_tensor(f"bank{k}", [P, 512], f32))[:, :] for k in range(8)]
    rows_d = nc.dram_tensor("rows_scratch", (B * S, GW), f32, kind="Internal").ap()
    acc_d = nc.dram_tensor("acc_scratch", (B * S, D), f32, kind="Internal").ap()
    hop_d = nc.dram_tensor("hop_scratch", (2, 2, DC, P, S), f32, kind="Internal").ap()
    slot_d = nc.dram_tensor("slot_scratch", (2, E1 * CAP), f32, kind="Internal").ap()

    X_all = sb("X", [P, TB + NT + TB, D])
    X = X_all[:, TB:TB + NT, :]
    ident = sb("ident", [P, P])
    xs = sb("xs", [P, TB, D])
    xT = sb("xT", [P, DC, S])
    summed = sb("summed", [P, TB, D])
    stats = sb("stats", [P, TB, 6])
    mv = sb("mv", [P, TB, 2])
    veps = sb("veps", [P, TB])
    rstd = sb("rstd", [P, TB])
    mhalf = sb("mhalf", [P, TB])
    load = q.dma("sp", "d_x", lambda i: SP.dma_start(X, T["x"].rearrange("(t p) d -> p t d", p=P)))
    load_id = q.dma("sp", "d_id", lambda i: SP.dma_start(ident, T["ident"]))
    c_half = q.op("pool", lambda i: G.memset(mhalf, -0.5))
    pad = q.op("pool", lambda i: G.memset(X_all[:, 0:TB, :], 0.0), c_half)
    q.op("pool", lambda i: G.memset(X_all[:, TB + NT:, :], 0.0), pad)

    def bank_free(k):
        return q.names.get("bank%d" % k) or prev("bank%d" % k)

    def bank_read(k, mark):
        q.names["bank%d" % k] = mark

    def at(name):
        return q.names.get(name) or prev(name)

    def batch_rows(i):
        return X[:, bass.ds(i * TB, TB), :]

    def take_batch(pair=None, rows=batch_rows):
        got = q.op("dve", lambda i: V.tensor_copy(xs, rows(i)), prev("xs_read"))
        for c in range(DC):
            for t in range(TB):
                m = q.op("pe", lambda i, c=c, t=t: PE.transpose(bank[c][:, t * P:(t + 1) * P], xs[:, t, c * P:(c + 1) * P], ident),
                         got, bank_free(c), inc=t == TB - 1, name="xs_read")
            if pair is not None:
                last = split(cut(pair, slice(None), c), bank[c], m, free=[at("xT_read")], name="xT%d" % c)
            else:
                last = q.op("act", lambda i, c=c: A.activation(xT[:, c, :], bank[c], ACT.Copy), m, at("xT_read"), name="xT%d" % c)
            bank_read(c, last)

    def norm_tile(t, ps, *after):
        a = q.op("dve", lambda i: V.tensor_tensor(summed[:, t, :], ps, to_X(i, t), ALU.add),
                 *after, prev("normed"), name="summed%d" % t)
        s = q.op("dve", lambda i: V.bn_stats(stats[:, t, :], summed[:, t, :]), a)
        return a, q.op("dve", lambda i: V.bn_aggr(mv[:, t, :], stats[:, t, :]), s, prev("veps"), name="summed_all", plain=True)

    def norm_batch(m):
        v = q.op("pool", lambda i: G.tensor_scalar(veps, mv[:, :, 1], EPS, None, ALU.add), m, name="veps", plain=True)
        r = q.op("pool", lambda i: G.tensor_tensor(rstd, veps, mhalf, ALU.pow), v, c_half)
        for t in range(TB):
            last = q.op("dve", lambda i, t=t: V.tensor_scalar(to_X(i, t), summed[:, t, :], mv[:, t, 0:1], rstd[:, t:t + 1],
                                                             ALU.subtract, ALU.mult), r, name="normed")
        return last

    def rows_of_next(i):
        return X_all[:, bass.ds(i * TB + 2 * TB, TB), :] if i is not None else X[:, 0:TB, :]

    def rows_before(i, t):
        return X_all[:, bass.ds(i * TB + t, 1), :].rearrange("p a d -> p (a d)") if i is not None else X[:, NT - TB + t, :]

    def to_X(i, t):
        return X[:, bass.ds(i * TB + t, 1), :].rearrange("p a d -> p (a d)")

    with ExitStack() as ph:
        first = sb("first", [5, 1024], where=ph)
        fmask = sb("fmask", [5, 1024], where=ph)
        work5 = sb("work5", [5, 1024], where=ph)
        fconst = sb("fconst", [5, P + 1], where=ph)
        kcols = sb("kcols", [P, 4], where=ph)
        basis = sb("basis", [P, DC, D], where=ph)
        gbasis = sb("gbasis", [P, DC, D], where=ph)
        Cmat = sb("Cmat", [P, DC, D], where=ph)
        w_el = sb("w_el", [P, DC, 24], where=ph)
        w_le = sb("w_le", [25, D], where=ph)
        b_el = sb("b_el", [24, 1], where=ph)
        golay = sb("golay", [24, 48], where=ph)
        CW = sb("CW", [P, DC, 24], where=ph)
        mm = sb("mm", [P, 2], where=ph)
        mmT = sb("mmT", [2, 1], where=ph)
        mm1 = sb("mm1", [5, 8], where=ph)
        sel = sb("sel", [2, 10], where=ph)
        dcol = sb("dcol", [P, 8], where=ph)
        trig = sb("trig", [P, 8], where=ph)
        bits = sb("bits", [24, S], where=ph)
        syn = sb("syn", [24, S], where=ph)
        fix = sb("fix", [24, S], where=ph)
        corr = sb("corr", [32, S], where=ph)
        small = [(first, bass.AP(T["x"].tensor, 0, [[0, 5], [1, 1024]])), (fmask, T["fmask"]), (fconst, T["fconst"]), (kcols, T["kcols"]),
                 (basis, T["basis"]), (w_el, T["W_el"]), (w_le, T["W_le"]), (b_el, T["b_el"]), (golay, T["golay"]), (sel, T["sel"])]
        for dst, src in small:
            loaded = q.dma("act", "d_small", lambda i, dst=dst, src=src: A.dma_start(dst, src))
        ones = q.op("pool", lambda i: G.memset(corr, 1.0))
        m1 = q.op("dve", lambda i: V.tensor_reduce(mm[:, 0:1], X, AX.XY, ALU.max), load)
        m2 = q.op("dve", lambda i: V.tensor_reduce(mm[:, 1:2], X, AX.XY, ALU.min, negate=True), load)
        m = q.op("pe", lambda i: PE.transpose(bank[0][0:2, 0:P], mm, ident), m1, m2, load_id)
        m = q.op("dve", lambda i: V.tensor_reduce(mmT, bank[0][0:2, 0:P], AX.X, ALU.max), m)
        q.op("pe", lambda i: PE.matmul(bank[1][0:5, 0:1], sel[:, 0:5], mmT, start=True, stop=True), m, loaded, inc=False)
        m = q.op("pe", lambda i: PE.matmul(bank[1][0:5, 1:2], sel[:, 5:10], mmT, start=True, stop=True))
        m = q.op("dve", lambda i: V.tensor_copy(mm1[:, 0:2], bank[1][0:5, 0:2]), m)
        m = q.op("dve", lambda i: V.scalar_tensor_tensor(mm1[:, 2:3], mm1[:, 0:1], 1e-10, mm1[:, 1:2], ALU.add, ALU.add), m)
        m = q.op("dve", lambda i: V.reciprocal(mm1[:, 3:4], mm1[:, 2:3]), m)
        m = q.op("dve", lambda i: V.tensor_scalar(first, first, mm1[:, 1:2], mm1[:, 3:4], ALU.add, ALU.mult), m)
        m = q.op("dve", lambda i: V.scalar_tensor_tensor(work5, first, 1.0, fmask, ALU.mult, ALU.mult, accum_out=mm1[:, 4:5]), m)
        m = q.op("dve", lambda i: V.tensor_tensor(mm1[:, 5:6], mm1[:, 4:5], fconst[:, P:P + 1], ALU.mult), m)
        m = q.op("dve", lambda i: V.scalar_tensor_tensor(work5, first, mm1[:, 5:6], fmask, ALU.is_gt, ALU.mult, accum_out=mm1[:, 6:7]), m)
        m = q.op("dve", lambda i: V.tensor_scalar(mm1[:, 6:7], mm1[:, 6:7], 1.0, None, ALU.max), m)
        m = q.op("act", lambda i: A.activation(mm1[:, 7:8], mm1[:, 6:7], ACT.Ln), m)
        m = q.op("pe", lambda i: PE.matmul(bank[2][:, 0:1], fconst[:, 0:P], mm1[:, 7:8], start=True, stop=True), m)
        m = q.op("dve", lambda i: V.tensor_scalar(dcol[:, 0:1], bank[2][:, 0:1], 1.0, 2.0, ALU.max, ALU.min), m)
        m = q.op("dve", lambda i: V.tensor_scalar(dcol[:, 1:2], dcol[:, 0:1], 0.2, 1.0, ALU.mult, ALU.add), m)
        m = q.op("dve", lambda i: V.tensor_tensor(dcol[:, 2:3], dcol[:, 1:2], dcol[:, 0:1], ALU.mult), m)
        m = q.op("dve", lambda i: V.tensor_scalar(dcol[:, 3:4], dcol[:, 0:1], 0.5, 1.0, ALU.mult, ALU.add), m)
        m = q.op("dve", lambda i: V.tensor_scalar(dcol[:, 4:5], dcol[:, 0:1], 0.1, None, ALU.mult), m)
        m = q.op("dve", lambda i: V.tensor_scalar(trig[:, 0:2], kcols[:, 0:2], dcol[:, 3:4], dcol[:, 2:3], ALU.mult, ALU.add), m)
        m = q.op("dve", lambda i: V.tensor_scalar(trig[:, 2:4], kcols[:, 2:4], dcol[:, 4:5], dcol[:, 2:3], ALU.mult, ALU.add), m)
        m = q.op("dve", lambda i: V.tensor_tensor(trig[:, 2:4], trig[:, 2:4], kcols[:, 0:2], ALU.subtract), m)
        m = q.op("dve", lambda i: V.tensor_scalar(trig[:, 0:2], trig[:, 0:2], -1.0, float(np.pi), ALU.mult, ALU.add), m)
        m = q.op("dve", lambda i: V.tensor_scalar(trig[:, 2:4], trig[:, 2:4], -1.0, float(np.pi / 2), ALU.mult, ALU.add), m)
        m = q.op("act", lambda i: A.activation(trig[:, 4:8], trig[:, 0:4], ACT.Sin), m)
        m = q.op("dve", lambda i: V.tensor_tensor(trig[:, 0:2], trig[:, 4:6], trig[:, 6:8], ALU.mult), m)
        for c in range(DC):
            g = q.op("dve", lambda i, c=c: V.tensor_scalar(gbasis[:, c, :], basis[:, c, :], trig[:, c:c + 1], None, ALU.mult), m)
        for r in range(DC):
            for c in range(DC):
                m = q.op("pe", lambda i, r=r, c=c: PE.matmul(bank[3][:, r * D:(r + 1) * D], basis[:, c, r * P:(r + 1) * P], gbasis[:, c, :],
                                                             start=c == 0, stop=c == DC - 1), g)
        m = q.op("dve", lambda i: V.tensor_copy(Cmat.rearrange("p c d -> p (c d)"), bank[3]), m)
        for r in range(DC):
            for c in range(DC):
                w = q.op("pe", lambda i, r=r, c=c: PE.matmul(bank[4][:, r * 24:(r + 1) * 24], Cmat[:, c, r * P:(r + 1) * P], w_el[:, c, :],
                                                             start=c == 0, stop=c == DC - 1), m)
        m_cw = q.op("dve", lambda i: V.tensor_copy(CW.rearrange("p c d -> p (c d)"), bank[4][:, 0:48]), w)
        q.barrier()

        take_batch(rows=rows_of_next)
        q.barrier()

        x_ready = [prev("xT0"), prev("xT1")]
        for c in range(DC):
            m = q.op("pe", lambda i, c=c: PE.matmul(bank[2][0:24, :], CW[:, c, :], xT[:, c, :], start=c == 0, stop=c == DC - 1),
                     x_ready, bank_free(2))
        m = q.op("dve", lambda i: V.tensor_scalar(bits, bank[2][0:24, :], b_el, 0.0, ALU.add, ALU.is_gt), m, name="bank2")
        m = q.op("pe", lambda i: PE.matmul(bank[3][0:24, :], golay[:, 0:24], bits, start=True, stop=True), m, prev("syn"), plain=True)
        m = q.op("dve", lambda i: V.tensor_scalar(syn, bank[3][0:24, :], 0.5, None, ALU.is_gt), m, name="syn")
        m = q.op("pe", lambda i: PE.matmul(bank[4][0:24, :], golay[:, 24:48], syn, start=True, stop=True), m, prev("fixed"), plain=True)
        m = q.op("dve", lambda i: V.scalar_tensor_tensor(fix, bank[4][0:24, :], 3.5, syn, ALU.is_le, ALU.mult), m, name="fixed")
        n = q.op("dve", lambda i: V.tensor_scalar(syn, bits, -2.0, 1.0, ALU.mult, ALU.add), m)
        m = q.op("dve", lambda i: V.tensor_tensor(fix, fix, syn, ALU.mult), n)
        m = q.op("dve", lambda i: V.tensor_tensor(corr[0:24, :], bits, fix, ALU.add), m, prev("xT_read"))
        y = []
        for t in range(TB):
            bk = bank[5 + t // 2][:, (t % 2) * D:(t % 2 + 1) * D]
            for c in range(DC):
                q.op("pe", lambda i, t=t, c=c, bk=bk: PE.matmul(bk, xT[:, c, t * P:(t + 1) * P], Cmat[:, c, :], start=c == 0, stop=False),
                     x_ready, prev("summed%d" % (t | 1)), inc=False)
            y.append(q.op("pe", lambda i, t=t, bk=bk: PE.matmul(bk, corr[0:25, t * P:(t + 1) * P], w_le, start=False, stop=True), m, name="xT_read"))
        take_batch(rows=rows_of_next)
        for t in range(TB):
            last = norm_tile(t, bank[5 + t // 2][:, (t % 2) * D:(t % 2 + 1) * D], y[t | 1])
        norm_batch(last[1])
        q.flush(B)
        q.barrier()

    def parts(name, shape, where):
        return tuple(sb(name + x, shape, f32r, where=where) for x in ("_hi", "_lo"))

    def f32_of(ap):
        return ap.bitcast(f32)

    def split(pair, src, *after, free=(), e="act", name=None):
        if e == "act":
            a = q.op("act", lambda i: A.activation(pair[0], src, ACT.Copy), *after, *free)
        else:
            a = q.op("dve", lambda i: V.tensor_copy(pair[0], src), *after, *free)
        return q.op("dve", lambda i: V.tensor_tensor(pair[1], src, f32_of(pair[0]), ALU.subtract), a, *after, *free, name=name)

    def terms(lhs, rhs):
        return [(lhs[0], rhs[0]), (lhs[0], rhs[1]), (lhs[1], rhs[0])]

    def product(out, pairs, *after, name=None, first=True, last=True):
        seq = [t for p in pairs for t in terms(*p)]
        for n, (lhs, rhs) in enumerate(seq):
            m = q.op("pe", lambda i, lhs=lhs, rhs=rhs, n=n: PE.matmul(out, lhs, rhs, start=first and n == 0, stop=last and n == len(seq) - 1),
                     *after, inc=n == len(seq) - 1, name=name)
        return m

    def cut(pair, *idx):
        return tuple(p[idx] for p in pair)

    def weights_in(pair, stage, src, free, k=0):
        m = q.dma("sp", "d_stage%d" % k, lambda i: SP.dma_start(stage, src), free)
        return split(pair, stage, m, e="act")

    S_BANKS, T_BANKS, O_BANKS, M_BANK = (0, 1, 2), (3, 4), (5, 6), 7
    T_LAG, PV_LAG = 5, 6

    def attend(buf, scores, values, jobs, after):
        steps = TB * jobs
        done = {}
        for s in range(steps + PV_LAG):
            u = s - T_LAG
            if 0 <= u < steps:
                h, kt = divmod(u, TB)
                tb = T_BANKS[u % 2]
                for t in range(TB):
                    m = q.op("pe", lambda i, t=t, kt=kt, tb=tb, h=h: PE.transpose(bank[tb][:, t * P:(t + 1) * P], buf.P[h % 2][:, t, kt * P:(kt + 1) * P], ident),
                             [done["scaled", h, x] for x in range(TB)], bank_free(tb),
                             inc=t == TB - 1)
                done["transposed", h] = m
                if kt == TB - 1:
                    q.names["P_read%d" % (h % 2)] = m
                free = done.get(("pv", u - 3)) or prev("pv_any")
                a = q.op("act", lambda i, u=u, tb=tb: A.activation(buf.PT[u % 3][0], bank[tb], ACT.Copy), m, free)
                m = q.op("dve", lambda i, u=u, tb=tb: V.tensor_tensor(buf.PT[u % 3][1], bank[tb], f32_of(buf.PT[u % 3][0]), ALU.subtract), a, name="bank%d" % tb)
                done["copied", u] = m
            if s < steps:
                h, j = divmod(s, TB)
                sbk = S_BANKS[s % 3]
                pairs, ready = scores(h, j)
                for n, (lhs, rhs) in enumerate(pairs):
                    m = q.op("pe", lambda i, lhs=lhs, rhs=rhs, n=n, sbk=sbk, k=len(pairs): PE.matmul(bank[sbk], lhs, rhs, start=n == 0, stop=n == k - 1),
                             ready, bank_free(sbk), inc=n == len(pairs) - 1)
                done["scores", h] = m
                c = s % 8
                m = q.op("dve", lambda i, c=c, sbk=sbk: V.tensor_reduce(buf.nmax[:, c:c + 1], bank[sbk], AX.X, ALU.max, negate=True), m,
                         done.get(("exp", s - 8)) or prev("exp_any"))
                m = q.op("act", lambda i, c=c, sbk=sbk, h=h, j=j: A.activation(buf.P[h % 2][:, j, :], bank[sbk], ACT.Exp, bias=buf.nmax[:, c:c + 1], accum_out=buf.rsum[:, c:c + 1]),
                         m, done.get(("transposed", h - 2)) or prev("P_read%d" % (h % 2)), done.get(("scaled8", s - 8)) or prev("scaled_any"), name="bank%d" % sbk)
                q.names["exp_any"] = m
                done["exp", s] = m
                m = q.op("dve", lambda i, c=c: V.reciprocal(buf.rinv[:, c:c + 1], buf.rsum[:, c:c + 1]), m)
                m = q.op("dve", lambda i, c=c, h=h, j=j: V.tensor_scalar(buf.P[h % 2][:, j, :], buf.P[h % 2][:, j, :], buf.rinv[:, c:c + 1], None, ALU.mult), m, name="scaled_any")
                done["scaled", h, j] = done["scaled8", s] = m
            u = s - PV_LAG
            if 0 <= u < steps:
                h, kt = divmod(u, TB)
                triples, ready = values(h, kt)
                for lhs, bk, first, last in triples:
                    m = product(bank[bk], [(lhs, buf.PT[u % 3])], done["copied", u], ready, name="pv_any", first=first, last=last)
                done["pv", u] = m
                if kt == TB - 1:
                    done["head", h] = m
                    after(h, m)
        return done

    class Buffers:

        def __init__(self, where):
            self.P = [sb("P%d" % k, [P, TB, S], where=where) for k in range(2)]
            self.PT = [parts("PT%d" % k, [P, S], where) for k in range(3)]
            self.nmax = sb("nmax", [P, 8], where=where)
            self.rsum = sb("rsum", [P, 8], where=where)
            self.rinv = sb("rinv", [P, 8], where=where)

    def low_part(pair, full, name):
        q.op("dve", lambda i: V.tensor_tensor(pair[1], full, f32_of(pair[0]), ALU.subtract), q.names[name + "_hi"], name=name)
        q.names["full_read"] = q.names[name]

    def project(w, src, c, full, pair, bias, scale, ready, free, name, bk=M_BANK, low=True):
        m = product(bank[bk], [(cut(w, slice(None), k, slice(c * P, (c + 1) * P)), cut(src, slice(None), k)) for k in range(DC)],
                    ready, bank_free(bk), name=name + "_in")
        m = q.op("dve", lambda i: V.tensor_scalar(full, bank[bk], bias if bias is not None else 0.0, scale, ALU.add, ALU.mult), m,
                 q.names.get("full_read") or prev("full_read"))
        bank_read(bk, m)
        if not low:
            return q.op("act", lambda i: A.activation(pair[0], full, ACT.Copy), m, free, name=name + "_hi")
        m = split(pair, full, m, free=[free], name=name)
        q.names["full_read"] = m
        return m

    with ExitStack() as ph:
        buf = Buffers(ph)
        W6 = {n: parts("w_" + n, [P, DC, D], ph) for n in ("Wq_c", "Wk_s", "Wv_s", "Wq_s", "Wk_c", "Wv_c")}
        Wg = parts("Wg", [P, 2 * DC, D], ph)
        stage = [sb("stage%d" % k, [P, 2 * DC, D], where=ph) for k in range(2)]
        xTp = parts("xTp", [P, DC, S], ph)
        ctxp = parts("ctxp", [P, DC, S], ph)
        full = sb("full", [P, S], where=ph)
        bias0 = sb("bias0", [P, 7, DC], where=ph)
        bgh = sb("bgh", [P, DC], where=ph)
        ctxT = sb("ctxT", [P, DC, S], where=ph)
        QK = [[parts("%s%d" % (n, d), [P, DC, S], ph) for n in ("QT", "KT")] for d in range(2)]
        VV = [parts("VV%d" % d, [P, TB, D], ph) for d in range(2)]
        cTp = parts("cTp", [P, 2 * DC, S], ph)
        cT = sb("cT", [P, 2 * DC, S], where=ph)
        gate = sb("gate", [P, DC, S], where=ph)
        mix = sb("mix", [P, DC, S], where=ph)
        w_done = []
        for k, (n, t) in enumerate([*W6.items(), ("Wg", Wg)]):
            w_done.append(weights_in(t, stage[k % 2][:, 0:t[0].shape[1], :], T[n], w_done[k - 2] if k > 1 else None, k % 2))
        w_in = q.dma("act", "d_w0", lambda i: A.dma_start(bias0, T["bias0"]))
        halved = q.op("dve", lambda i: V.tensor_scalar(bgh, bias0[:, 6, :], 0.5, None, ALU.mult), w_in)
        q.flush()

        def next_batch():
            m = q.dma("sp", "d_ctx", lambda i: SP.dma_start(ctxT, (T["ctxT"][bass.ds(i + 1, 1)] if i is not None else T["ctxT"][0:1]).rearrange("a p c s -> p (a c) s")), prev("ctx_read"))
            take_batch(pair=xTp, rows=rows_of_next)
            split((ctxp[0], ctxp[1]), ctxT, m, free=[at("xT_read")], name="ctx_read")

        next_batch()
        q.barrier()

        x_ready = [prev("xT0"), prev("xT1")]
        ctx_in = prev("ctx_read")
        SC = D ** -0.5
        ready = {}
        for d, (qs, ks, qm, km, wq, wk, wv) in enumerate([(xTp, ctxp, x_ready, ctx_in, "Wq_c", "Wk_s", "Wv_s"),
                                                          (ctxp, xTp, ctx_in, x_ready, "Wq_s", "Wk_c", "Wv_c")]):
            for c in range(DC):
                a = project(W6[wq], qs, c, full, cut(QK[d][0], slice(None), c), bias0[:, 3 * d, c:c + 1], SC, [qm, x_ready], prev("scores%d" % d), "Q%d%d" % (d, c))
                b = project(W6[wk], ks, c, full, cut(QK[d][1], slice(None), c), bias0[:, 3 * d + 1, c:c + 1], 1.0, [km, x_ready], prev("scores%d" % d), "K%d%d" % (d, c), bk=T_BANKS[c])
                ready.setdefault(d, []).extend([a, b])
            for pair in range(2):
                for t in (2 * pair, 2 * pair + 1):
                    m = product(bank[O_BANKS[pair]][:, (t % 2) * D:(t % 2 + 1) * D],
                                [(cut(ks, slice(None), k, slice(t * P, (t + 1) * P)), cut(W6[wv], slice(None), k)) for k in range(DC)],
                                km, x_ready, bank_free(O_BANKS[pair]), name="xT_read")
                ready["V", d, pair] = split(tuple(v[:, 2 * pair:2 * pair + 2, :].rearrange("p t d -> p (t d)") for v in VV[d]), bank[O_BANKS[pair]], m, free=[prev("pv_any")])
                bank_read(O_BANKS[pair], ready["V", d, pair])

        def scores0(h, j):
            Q, K = QK[h]
            return [t for c in range(DC) for t in terms(cut(Q, slice(None), c, slice(j * P, (j + 1) * P)), cut(K, slice(None), c))], ready[h]

        def values0(h, kt):
            w = [ready["V", h, 0], ready["V", h, 1], ready["V", 1, 0], ready["V", 1, 1]]
            w += [bank_free(k) for k in O_BANKS] if kt == 0 else []
            return [(cut(VV[h], slice(None), kt, slice(c * P, (c + 1) * P)), O_BANKS[c], kt == 0, kt == TB - 1) for c in range(DC)], w

        def after0(h, m):
            for c in range(DC):
                r = q.op("act", lambda i, c=c: A.activation(cT[:, DC * h + c, :], bank[O_BANKS[c]], ACT.Identity, bias=bias0[:, 3 * h + 2, c:c + 1], scale=1.0),
                         m, prev("mixed"), name="bank%d" % O_BANKS[c])
                ready.setdefault(("out", h), []).append(r)
                ready.setdefault(("outp", h), []).append(split(cut(cTp, slice(None), DC * h + c), cT[:, DC * h + c, :], r, free=[prev("gate_in")]))

        done = attend(buf, scores0, values0, 2, after0)
        q.names["scores0"], q.names["scores1"] = done["scores", 0], done["scores", 1]
        next_batch()
        both = ready["out", 0] + ready["out", 1]
        for c in range(DC):
            m = product(bank[T_BANKS[c]], [(cut(Wg, slice(None), k, slice(c * P, (c + 1) * P)), cut(cTp, slice(None), k)) for k in range(2 * DC)],
                        ready["outp", 0], ready["outp", 1], bank_free(T_BANKS[c]), name="gate_in")
            m = q.op("act", lambda i, c=c: A.activation(gate[:, c, :], bank[T_BANKS[c]], ACT.Tanh, bias=bgh[:, c:c + 1], scale=0.5), m, prev("mixed"), name="bank%d" % T_BANKS[c])
            m = q.op("pool", lambda i, c=c: G.tensor_scalar(gate[:, c, :], gate[:, c, :], 0.5, 0.5, ALU.mult, ALU.add), m, plain=True)
            n = q.op("dve", lambda i, c=c: V.tensor_tensor(mix[:, c, :], cT[:, c, :], cT[:, DC + c, :], ALU.subtract), both, prev("mix_read"))
            n = q.op("dve", lambda i, c=c: V.tensor_tensor(mix[:, c, :], mix[:, c, :], gate[:, c, :], ALU.mult), n, m)
            n = q.op("dve", lambda i, c=c: V.tensor_tensor(mix[:, c, :], mix[:, c, :], cT[:, DC + c, :], ALU.add), n, name="mixed")
            ready["mix", c] = n
        for t in range(TB):
            for c in range(DC):
                m = q.op("pe", lambda i, t=t, c=c: PE.transpose(bank[O_BANKS[t // 2]][:, (t % 2) * D + c * P:(t % 2) * D + (c + 1) * P], mix[:, c, t * P:(t + 1) * P], ident),
                         ready["mix", 0], ready["mix", 1], bank_free(O_BANKS[t // 2]), name="mix_read")
            if t % 2:
                for v in (t - 1, t):
                    last = norm_tile(v, bank[O_BANKS[t // 2]][:, (v % 2) * D:(v % 2 + 1) * D], m)
                bank_read(O_BANKS[t // 2], last[0])
        norm_batch(last[1])
        q.flush(B)
        q.barrier()

    all_stats = sb("all_stats", [P, NT, 6])
    all_mv = sb("all_mv", [P, NT, 2])
    all_rstd = sb("all_rstd", [P, 2, NT])

    def norm_from_acc(result=None):
        quarter = [slice(k * TB, (k + 1) * TB) for k in range(B)]
        half_all = q.op("pool", lambda i: G.memset(all_rstd[:, 1, :], -0.5))
        for k in range(B):
            e, issuer = (("sp", SP), ("act", A))[k % 2]
            ld = q.dma(e, "d_acc%d" % k, lambda i, k=k, issuer=issuer: issuer.dma_start(X[:, quarter[k], :], acc_d.rearrange("(t p) d -> p t d", p=P)[:, quarter[k], :]))
            for t in range(NT)[quarter[k]]:
                q.op("dve", lambda i, t=t: V.bn_stats(all_stats[:, t, :], X[:, t, :]), ld, name="bn%d" % t)
            for t in range(NT)[quarter[k]]:
                m = q.op("dve", lambda i, t=t: V.bn_aggr(all_mv[:, t, :], all_stats[:, t, :]), q.names["bn%d" % t])
            m = q.op("pool", lambda i, k=k: G.tensor_scalar(all_rstd[:, 0, quarter[k]], all_mv[:, quarter[k], 1], EPS, None, ALU.add), m)
            q.op("pool", lambda i, k=k: G.tensor_tensor(all_rstd[:, 0, quarter[k]], all_rstd[:, 0, quarter[k]], all_rstd[:, 1, quarter[k]], ALU.pow), m, half_all, name="rstd%d" % k)
        for k in range(B):
            for t in range(NT)[quarter[k]]:
                m = q.op("dve", lambda i, t=t: V.tensor_scalar(X[:, t, :], X[:, t, :], all_mv[:, t, 0:1], all_rstd[:, 0, t:t + 1], ALU.subtract, ALU.mult), q.names["rstd%d" % k])
            if result is not None:
                e, issuer = (("sp", SP), ("act", A))[k % 2]
                q.dma(e, "d_out%d" % (k % 2), lambda i, k=k, issuer=issuer: issuer.dma_start(result.rearrange("(t p) d -> p t d", p=P)[:, quarter[k], :], X[:, quarter[k], :]), m)
        q.barrier()

    with ExitStack() as ph:
        W1 = [sb("W1_%d" % b, [P, DC, F0], where=ph) for b in range(2)]
        W2 = [sb("W2_%d" % b, [P, FC0, D], where=ph) for b in range(2)]
        b1 = sb("b1", [P, E0 * FC0], where=ph)
        b2 = sb("b2", [P, E0 * D], where=ph)
        idx_all = sb("idx_all", [P, (E0 + 2) * CT0], i32, where=ph)
        tok_col = sb("tok_col", [P, E0 * CT0], where=ph)
        tok_row = sb("tok_row", [P, E0 * C0], i32, where=ph)
        lower = sb("lower", [P, P], where=ph)
        idx = [sb("idx%d" % b, [P, CT0], i32, where=ph) for b in range(2)]
        rows = [sb("rows%d" % b, [P, CT0, GW], where=ph) for b in range(2)]
        wcol = [sb("wcol%d" % b, [P, CT0], where=ph) for b in range(2)]
        GT = [sb("GT%d" % b, [P, DC, C0], where=ph) for b in range(2)]
        hT = [sb("hT%d" % b, [P, FC0, C0], where=ph) for b in range(2)]
        same = [sb("same%d" % b, [P, CT0, P], where=ph) for b in range(2)]
        junk = sb("junk", [P, P], where=ph)
        again = sb("again", [P, 2 * CT0], where=ph)
        sidx = [sb("sidx%d" % b, [P, CT0], i32, where=ph) for b in range(2)]
        wv = [sb("wv%d" % b, [P, D], where=ph) for b in range(2)]
        merged = [sb("merged%d" % b, [P, CT0, D], where=ph) for b in range(2)]
        for dst, src in ((b1, T["b1"]), (b2, bass.AP(T["b2"].tensor, 0, [[0, P], [1, E0 * D]])), (lower, T["lower"])):
            w_in = q.dma("act", "d_w0", lambda i, dst=dst, src=src: A.dma_start(dst, src))
        i_in = q.dma("pool", "d_g0", lambda i: G.dma_start(idx_all[:, 0:E0 * CT0], T["idx"]))
        padded = [i_in, q.op("pool", lambda i: G.memset(idx_all[:, E0 * CT0:], 0))]
        rows_of_tiles = rows_d.rearrange("(t p) d -> p t d", p=P)[:, :, 0:D]
        rows_in = [q.dma("sp", "d_rows0", lambda i: SP.dma_start(rows_of_tiles[:, 0:NT // 2], X[:, 0:NT // 2])),
                   q.dma("act", "d_rows1", lambda i: A.dma_start(rows_of_tiles[:, NT // 2:], X[:, NT // 2:])),
                   q.dma("pool", "d_sc1", lambda i: G.dma_start(rows_d[:, D:GW], T["combine"]))]
        acc_in = q.dma("pool", "d_sc0", lambda i: G.dma_start(acc_d.rearrange("(t p) d -> p t d", p=P), X))
        j_in = q.dma("pool", "d_tok", lambda i: G.dma_start(tok_row, bass.AP(T["tok"].tensor, 0, [[0, P], [1, E0 * C0]])))
        tok_f = q.op("dve", lambda i: V.tensor_copy(tok_col, idx_all[:, 0:E0 * CT0]), i_in)
        q.flush()

        def gather0(i, b, rows_free):
            m = q.op("pool", lambda _, b=b, i=i: G.tensor_copy(idx[b], idx_all[:, i(_, b)]), padded, rows_free, q.names.get("gathered%d" % b))
            for t in range(CT0):
                q.dma("pool", "d_g%d" % b, lambda _, b=b, t=t: G.indirect_dma_start(rows[b][:, t, :], None, rows_d, bass.IndirectOffsetOnAxis(ap=idx[b][:, t:t + 1], axis=0)),
                      m, rows_in, rows_free, name="gathered%d" % b)

        for b in range(2):
            gather0(lambda _, b: slice(b * CT0, (b + 1) * CT0), b, None)
        q.flush()
        w_of, gt_of, wc_of, found_of = [], {}, {}, {}
        for b in range(2):
            for dst, name in ((W1[b], "W1"), (W2[b], "W2")):
                w = q.dma("sp", "d_e%d" % b, lambda i, b=b, dst=dst, name=name: SP.dma_start(dst, T[name][bass.ds(2 * i + b, 1)].rearrange("a p c f -> p (a c) f")), prev("W_read%d" % b))
            w_of.append(w)

        def head(b):
            g = prev("gathered%d" % b)
            for c in range(DC):
                for t in range(CT0):
                    m = q.op("pe", lambda i, b=b, t=t, c=c: PE.transpose(bank[c][:, t * P:(t + 1) * P], rows[b][:, t, c * P:(c + 1) * P], ident),
                             g, (q.names["GT%d" % c] if b else prev("GT%d" % c)), inc=t == CT0 - 1)
                m_t = m
                if c:
                    m = q.op("act", lambda i, b=b, c=c: A.activation(GT[b][:, c, :], bank[c], ACT.Copy), m, prev("GT_read%d" % b), name="GT1")
                else:
                    m = q.op("dve", lambda i, b=b, c=c: V.tensor_copy(GT[b][:, c, :], bank[c]), m, prev("GT_read%d" % b), name="GT0")
            gt_of[b] = [q.names["GT0"], q.names["GT1"]]
            wc = wc_of[b] = q.op("dve", lambda i, b=b: V.tensor_copy(wcol[b], rows[b][:, :, bass.ds(2 * i + b + D, 1)].rearrange("p t a -> p (t a)")), g, prev("wcol_read%d" % b))
            gather0(lambda i, b: bass.ds((2 * i + b + 2) * CT0, CT0), b, [m_t, wc])
            for t in range(CT0):
                a = q.op("dve", lambda i, b=b, t=t: V.tensor_scalar(same[b][:, t, :], tok_row[:, bass.ds((2 * i + b) * C0 + t * P, P)], tok_col[:, bass.ds((2 * i + b) * CT0 + t, 1)], None, ALU.is_equal),
                         tok_f, j_in, prev("same_read%d" % b))
                m = q.op("dve", lambda i, b=b, t=t: V.scalar_tensor_tensor(junk, tok_row[:, bass.ds((2 * i + b) * C0 + t * P, P)], tok_col[:, bass.ds((2 * i + b) * CT0 + t, 1)], lower,
                                                                        ALU.is_equal, ALU.mult, accum_out=again[:, t:t + 1]), w_in, q.names.get("junk") or prev("junk"), name="junk")
            m = q.op("dve", lambda i: V.tensor_scalar(again[:, CT0:2 * CT0], again[:, 0:CT0], 0.0, float(1 << 16), ALU.is_gt, ALU.mult), m)
            found_of[b] = q.op("dve", lambda i, b=b: V.tensor_tensor(sidx[b], again[:, CT0:2 * CT0], tok_col[:, bass.ds((2 * i + b) * CT0, CT0)], ALU.add), m, prev("stored%d" % b))

        def up(b):
            for f in range(FC0):
                bk = 2 + f % 2
                for c in range(DC):
                    m = q.op("pe", lambda i, b=b, f=f, c=c, bk=bk: PE.matmul(bank[bk], W1[b][:, c, f * P:(f + 1) * P], GT[b][:, c, :], start=c == 0, stop=c == DC - 1),
                             w_of[b], gt_of[b], q.names.get("hid%d" % (f % 2)) or prev("hid%d" % (f % 2)), inc=c == DC - 1, name="GT_read%d" % b)
                m = q.op("act", lambda i, b=b, f=f, bk=bk: A.activation(hT[b][:, f, :], bank[bk], ACT.Gelu_apprx_tanh, bias=b1[:, bass.ds((2 * i + b) * FC0 + f, 1)], scale=1.0),
                         m, w_in, prev("hT_read%d" % b), name="hid%d" % (f % 2))
                q.names["hid_of%d_%d" % (b, f)] = m

        def down(b):
            def merge(t):
                bm = 6 + t % 2
                m3 = q.op("pe", lambda i: PE.matmul(bank[bm][:, 0:D], same[b][:, t, :], wv[t % 2], start=True, stop=True), q.names["weighted%d" % t],
                          at("mg%d" % (t % 2)), name="wv_read%d" % (t % 2))
                q.names["same_read%d" % b] = m3
                a = q.op("dve", lambda i: V.tensor_copy(merged[b][:, t, :], bank[bm][:, 0:D]), m3, prev("stored%d" % b), name="mg%d" % (t % 2))
                q.dma("pool", "d_sc%d" % b, lambda i: G.indirect_dma_start(acc_d, bass.IndirectOffsetOnAxis(ap=sidx[b][:, t:t + 1], axis=0), merged[b][:, t, :], None,
                                                                           compute_op=ALU.add, bounds_check=B * S - 1, oob_is_err=False),
                      a, found_of[b], acc_in, at("stored"), name="stored")

            for t in range(CT0):
                bk = 4 + t % 2
                for f in range(FC0):
                    m2 = q.op("pe", lambda i, t=t, f=f, bk=bk: PE.matmul(bank[bk][:, 0:D], hT[b][:, f, t * P:(t + 1) * P], W2[b][:, f, :], start=f == 0, stop=f == FC0 - 1),
                              q.names["hid_of%d_%d" % (b, f)], w_of[b], at("up%d" % (t % 2)), inc=f == FC0 - 1, name="hT_read%d" % b)
                q.names["W_read%d" % b] = m2
                a = q.op("dve", lambda i, t=t, bk=bk: V.tensor_tensor(wv[t % 2], bank[bk][:, 0:D], b2[:, bass.ds((2 * i + b) * D, D)], ALU.add), m2,
                         at("wv_read%d" % (t % 2)), name="up%d" % (t % 2))
                q.names["weighted%d" % t] = q.op("dve", lambda i, t=t: V.tensor_scalar(wv[t % 2], wv[t % 2], wcol[b][:, t:t + 1], None, ALU.mult), a, wc_of[b], name="wcol_read%d" % b)
                if t:
                    merge(t - 1)
            merge(CT0 - 1)
            q.names["stored%d" % b] = q.names["stored"]

        for stage_of, b in ((head, 0), (up, 0), (head, 1), (down, 0), (up, 1), (down, 1)):
            stage_of(b)
        q.flush(E0 // 2)
        q.barrier()
    norm_from_acc()

    MAX_BANKS, ST_BANKS, OUT_BANKS, ROW_BANK, SPARE_BANK = (0, 1), (2, 3), (4, 5), 6, 7
    LAGS = (4, 7, 9)
    ROWS = 96
    MAX_ROW = 64

    STEPS = TB * H1
    DONE = STEPS - 1 + LAGS[2]

    def attend_heads(buf, maxima, row, scores, values, after, events, loop=True):
        ROW_LAG, ST_LAG, OUT_LAG = LAGS

        def group(bk, pairs, *after, name):
            for n, (lhs, rhs) in enumerate(pairs):
                m = q.op("pe", lambda i, lhs=lhs, rhs=rhs, n=n: PE.matmul(bank[bk], lhs, rhs, start=n == 0, stop=n == len(pairs) - 1),
                         *after, inc=n == len(pairs) - 1, name=name)
            return m

        def now(s, lag):
            u = s - lag
            return u if loop and u >= 0 else u + STEPS if u < 0 else None

        for s in range(STEPS if loop else STEPS // 2):
            if loop:
                h, j = divmod(s, TB)
                bk = MAX_BANKS[s % 2]
                pairs, ready = maxima(h, j)
                m = group(bk, pairs, ready, bank_free(bk), name="first")
                c = (h % 2) * TB + j
                q.op("dve", lambda i, c=c, bk=bk: V.tensor_reduce(buf.nmax[:, c:c + 1], bank[bk], AX.X, ALU.max, negate=True), m, at("nmax_read%d" % (h % 2)), name="bank%d" % bk)
                q.names["nmax%d" % h] = q.names["bank%d" % bk]
            u = now(s, ST_LAG)
            if u is not None:
                h, kt = divmod(u, TB)
                bk = ST_BANKS[u % 2]
                m = group(bk, scores(h, kt), at("row%d" % h), bank_free(bk), name="second%d" % h)
                n = len(buf.PTp) or len(buf.PT)
                free = at("pv%d" % ((u - n) % STEPS))
                PT = buf.PT[u % len(buf.PT)]
                if not buf.PTp:
                    m = q.op("act", lambda i, PT=PT, bk=bk: A.activation(PT, bank[bk], ACT.Exp), m, free, name="bank%d" % bk)
                    q.names["exp%d" % u] = m
                else:
                    a = q.op("act", lambda i, u=u, bk=bk: A.activation(buf.PTp[u % len(buf.PTp)][0], bank[bk], ACT.Exp), m, free, name="hi%d" % u)
                    q.op("act", lambda i, PT=PT, bk=bk: A.activation(PT, bank[bk], ACT.Exp), m, at("exp%d" % ((u - len(buf.PT)) % STEPS)), name="bank%d" % bk)
                    q.names["full%d" % u] = q.names["bank%d" % bk]
            u = now(s, ST_LAG + 1)
            if buf.PTp and u is not None:
                PT, (hi, lo) = buf.PT[u % len(buf.PT)], buf.PTp[u % len(buf.PTp)]
                q.op("dve", lambda i, PT=PT, hi=hi, lo=lo: V.tensor_tensor(lo, PT, f32_of(hi), ALU.subtract),
                     at("hi%d" % u), at("full%d" % u), at("pv%d" % ((u - len(buf.PTp)) % STEPS)), name="exp%d" % u)
            u = now(s, OUT_LAG)
            if u is not None:
                h, kt = divmod(u, TB)
                lhs, bk, first, last, ready = values(h, kt)
                rhs = buf.PTp[u % len(buf.PTp)] if buf.PTp else [buf.PT[u % len(buf.PT)]]
                for n, r in enumerate(rhs):
                    m = q.op("pe", lambda i, lhs=lhs, bk=bk, r=r, start=first and n == 0, stop=last and n == len(rhs) - 1: PE.matmul(bank[bk], lhs, r, start=start, stop=stop),
                             at("exp%d" % u), ready, bank_free(bk) if first else None, inc=n == len(rhs) - 1, name="pv%d" % u)
                if kt == TB - 1:
                    after(h, m)
            u = now(s, ROW_LAG)
            if u is not None and u % TB == 0:
                h = u // TB
                for t in range(TB):
                    m = q.op("pe", lambda i, h=h, t=t: PE.transpose(bank[ROW_BANK][0:1, t * P:(t + 1) * P], buf.nmax[:, (h % 2) * TB + t:(h % 2) * TB + t + 1], ident),
                             at("nmax%d" % h), bank_free(ROW_BANK), inc=t == TB - 1, plain=True, name="nmax_read%d" % (h % 2))
                dst = row(h)
                q.op("act", lambda i, dst=dst: A.activation(dst, bank[ROW_BANK][0:1, :], ACT.Copy), m, name="bank%d" % ROW_BANK)
                q.names["row%d" % h] = q.names["bank%d" % ROW_BANK]
            for T_, of_next, f in events:
                if (T_ % STEPS == s) if loop else (T_ - STEPS == s and not of_next):
                    f()

    class HeadBuffers:

        def __init__(self, where, n, n_parts=0):
            self.PT = [sb("ST%d" % k, [P, S], where=where) for k in range(n)]
            self.PTp = [parts("STp%d" % k, [P, S], where) for k in range(n_parts)]
            self.nmax = sb("nmax1", [P, 2 * TB], where=where)
            for ap in (*self.PT, self.nmax, *(f32_of(x) for p in self.PTp for x in p)):
                q.op("dve", lambda i, ap=ap: V.memset(ap, 1.0))

        def open_sum(self, values):
            h, kt = divmod(STEPS - LAGS[2], TB)
            lhs, bk, first, last, ready = values(h, kt)
            rhs = self.PTp[0][0] if self.PTp else self.PT[0]
            q.op("pe", lambda i: PE.matmul(bank[bk], rhs[:, 0:P], rhs, start=True, stop=False))

    def out_base(t, bo, row):
        q.op("pool", lambda i: G.tensor_tensor(summed[:, t, :], row(i, t), bo, ALU.add), at("normed%d" % t), name="summed%d" % t, plain=True)

    def out_products(attT, Wo, ready, tiles, chunks, name):
        for t in tiles:
            half = bank[SPARE_BANK][:, (t % 2) * D:(t % 2 + 1) * D]
            for g in chunks:
                q.op("pe", lambda i, t=t, g=g, half=half: PE.matmul(half, attT[:, g, t * P:(t + 1) * P], Wo[:, g, :], start=g == chunks[0], stop=g == chunks[-1]),
                     ready, bank_free(SPARE_BANK), inc=g == chunks[-1], name=name)
        for t in tiles:
            q.names["out%d" % t] = q.names[name]

    def out_sum(t):
        half = bank[SPARE_BANK][:, (t % 2) * D:(t % 2 + 1) * D]
        q.op("dve", lambda i: V.tensor_tensor(summed[:, t, :], half, summed[:, t, :], ALU.add), at("out%d" % t), at("summed%d" % t), name="bank%d" % SPARE_BANK)
        q.names["summed%d" % t] = q.names["bank%d" % SPARE_BANK]

    def out_stats(t):
        s_ = q.op("dve", lambda i: V.bn_stats(stats[:, t, :], summed[:, t, :]), at("summed%d" % t))
        q.names["to_aggregate%d" % t] = s_

    def out_mean(t):
        q.op("dve", lambda i: V.bn_aggr(mv[:, t, :], stats[:, t, :]), at("to_aggregate%d" % t), at("veps"), at("normed%d" % (TB - 1)), name="mv", plain=True)

    def out_rstd():
        v = q.op("pool", lambda i: G.tensor_scalar(veps, mv[:, :, 1], EPS, None, ALU.add), at("mv"), [at("normed%d" % t) for t in range(TB)], name="veps", plain=True)
        q.op("pool", lambda i: G.tensor_tensor(rstd, veps, mhalf, ALU.pow), v, name="rstd")

    def out_norm(t):
        q.op("dve", lambda i: V.tensor_scalar(rows_before(i, t), summed[:, t, :], mv[:, t, 0:1], rstd[:, t:t + 1], ALU.subtract, ALU.mult), at("rstd"), name="normed%d" % t)

    def norm_events(T_):
        return [*((T_ + t, lambda t=t: out_stats(t)) for t in range(TB)), *((T_ + t + 1, lambda t=t: out_mean(t)) for t in range(TB)),
                (T_ + TB + 1, out_rstd), *((T_ + TB + 3 + t, lambda t=t: out_norm(t)) for t in range(TB))]

    with ExitStack() as ph:
        HD, HG = D // H1, 2
        BLOCK, ONE, LO = P // HG, HD, 2 * HD
        buf = HeadBuffers(ph, 2, 4)
        Wq, Wk, Wv = (parts("W" + n, [P, DC, D], ph) for n in "qkv")
        Wo = sb("Wo", [P, DC, D], where=ph)
        bo = sb("bo", [P, D], where=ph)
        bv = sb("bv", [P, D], where=ph)
        bqkv = sb("bqkv", [P, 3, DC], where=ph)
        cs = sb("cs", [P, 2, S], where=ph)
        full = sb("full", [P, S], where=ph)
        turned = sb("turned", [P, DC, S], where=ph)
        part = xs.rearrange("p t d -> p (t d)").rearrange("p (c s) -> p c s", c=DC)
        stage = [turned[:, :, 0:D], part[:, :, 0:D]]
        srcp = parts("srcp", [P, DC, S], ph)
        qkp = parts("qkp", [P, DC, S], ph)
        rows_q, rows_k = (sb(n, [ROWS, H1, S], f32r, where=ph) for n in ("rows_q", "rows_k"))
        Vone = sb("Vone", [P, TB, H1, P], f32r, where=ph)
        gathered_o = [sb("gathered_o%d" % k, [P, S], where=ph) for k in range(2)]
        sums = sb("sums", [P, TB, HG], where=ph)
        att = sb("att", [P, TB, D], where=ph)
        attT = turned
        for dst, src in ((Wo, T["Wo1"]), (bqkv, T["bqkv"]), (cs, T["cs"]), (bo, bass.AP(T["bo1"].tensor, 0, [[0, P], [1, D]])),
                         (bv, bass.AP(T["bv1"].tensor, 0, [[0, P], [1, D]]))):
            w_in = q.dma("act", "d_w0", lambda i, dst=dst, src=src: A.dma_start(dst, src))
        z = None
        for r in (rows_q, rows_k):
            z = q.op("pool", lambda i, r=r: G.memset(f32_of(r[MAX_ROW:ROWS]), 0.0), z)
        z = q.op("pool", lambda i: G.memset(f32_of(rows_k[MAX_ROW:MAX_ROW + 1]), 1.0), z)
        z = q.op("dve", lambda i: V.memset(f32_of(Vone), 0.0))

        def head_columns(g, n, k):
            return bass.AP(Vone.tensor, Vone.offset + g * HG * P + n, [Vone.ap[0], [H1 * P, TB], [P + BLOCK, HG], [1, k]])

        for g in range(H1 // HG):
            z = q.op("dve", lambda i, g=g: V.memset(f32_of(head_columns(g, ONE, 1)), 1.0), z)
        w_done = []
        for ap in (*gathered_o, att):
            q.op("dve", lambda i, ap=ap: V.memset(ap, 0.0))
        for k, (t, n) in enumerate(((Wq, "Wq1"), (Wk, "Wk1"), (Wv, "Wv1"))):
            w_done.append(weights_in(t, stage[k % 2], T[n], w_done[0] if k == 2 else None, k % 2))
        q.barrier()

        Vc = sb("Vc", [P, TB, D], where=ph)
        prep = {}

        def take():
            prep["xs"] = q.op("dve", lambda i: V.tensor_copy(xs, rows_of_next(i)), prev("xs_read"), prev("turned0"), prev("turned1"))

        def turn(c):
            for t in range(TB):
                m = q.op("pe", lambda i, c=c, t=t: PE.transpose(bank[SPARE_BANK][:, t * P:(t + 1) * P], xs[:, t, c * P:(c + 1) * P], ident),
                         prep["xs"], bank_free(SPARE_BANK), inc=t == TB - 1, name="xs_read")
            prep["xT", c] = q.op("act", lambda i, c=c: A.activation(xT[:, c, :], bank[SPARE_BANK], ACT.Copy), m, prev("xT_read"), name="bank%d" % SPARE_BANK)

        def rope(c):
            x_in = [prep["xT", 0], prep["xT", 1]]
            b = q.op("pool", lambda i, c=c: G.tensor_tensor(part[:, c, :], xT[:, 1, :], cs[:, 1 - c, :], ALU.mult), x_in, q.names["xs_read"], prev("turned%d" % c), plain=True)
            a = q.op("dve", lambda i, c=c: V.tensor_tensor(turned[:, c, :], xT[:, 0, :], cs[:, c, :], ALU.mult), x_in, prev("turned_read%d" % c), at("att_read"))
            prep["mul", c] = a, b
            q.names["xT_read"] = [a, b] + (list(prep["mul", 0]) if c else [])

        def rope_end(c):
            m = q.op("dve", lambda i, c=c: V.tensor_tensor(turned[:, c, :], turned[:, c, :], part[:, c, :], ALU.add if c else ALU.subtract), *prep["mul", c], name="turned%d" % c)
            prep["src", c] = split(cut(srcp, slice(None), c), turned[:, c, :], m, free=[prev("src_read")], name="turned_read%d" % c)

        def to_stack(n, g):
            w, scale = ((Wq, HD ** -0.5), (Wk, 1.0))[n]
            project(w, srcp, g, full, cut(qkp, slice(None), g), bqkv[:, n, g:g + 1], scale, [prep["src", 0], prep["src", 1]], [at("hopped0"), at("hopped1")], "qk%d%d" % (n, g), bk=SPARE_BANK, low=False)

        def to_stack_low(n, g):
            low_part(cut(qkp, slice(None), g), full, "qk%d%d" % (n, g))

        def hop_out(n):
            for p in range(2):
                q.dma("sp", "d_hop%d" % n, lambda i, p=p: SP.dma_start(hop_d[n, p].rearrange("g r s -> r g s"), f32_of(qkp[p])),
                      q.names["qk%d0" % n], q.names["qk%d1" % n], at("rows_in0"), at("rows_in1"), name="hopped%d" % n)

        def stack_in(half):
            hs = slice(half * H1 // 2, (half + 1) * H1 // 2)
            stream = "d_stack%d" % half
            after = [at("second%d" % h) for h in range(H1)[hs]]
            q.dma("pool", stream, lambda i: G.dma_start(rows_q[MAX_ROW:MAX_ROW + 1, hs], T["zeros"]), after)
            for n, (dst, order) in enumerate(((rows_q, (0, 1, 0, 1)), (rows_k, (0, 0, 1, 1)))):
                for k, p in enumerate(order):
                    q.dma("pool", stream, lambda i, n=n, k=k, p=p, dst=dst: G.dma_start(dst[k * 16:(k + 1) * 16, hs], hop_d[n, p, half].rearrange("(h f) s -> f h s", f=16)),
                          at("hopped0"), at("hopped1"), after, name="rows_in%d" % half)

        def v_in(t):
            m = product(bank[SPARE_BANK][:, 0:D], [(cut(srcp, slice(None), c, slice(t * P, (t + 1) * P)), cut(Wv, slice(None), c)) for c in range(DC)],
                        prep["src", 0], prep["src", 1], bank_free(SPARE_BANK), name="src_read")
            q.names["Vc"] = q.op("dve", lambda i, t=t: V.tensor_tensor(Vc[:, t, :], bank[SPARE_BANK][:, 0:D], bv, ALU.add), m, [at("Vone%d" % g) for g in range(H1 // HG)], name="bank%d" % SPARE_BANK)

        def v_place(g):
            last = (g + 1) * HG * TB - 1
            hi, lo = head_columns(g, 0, HD), head_columns(g, LO, HD)
            src = Vc[:, :, g * HG * HD:(g + 1) * HG * HD].rearrange("p t (k f) -> p t k f", k=HG)
            a = q.op("dve", lambda i: V.tensor_copy(hi, src), at("Vc"), at("pv%d" % last))
            q.op("dve", lambda i: V.tensor_tensor(lo, src, f32_of(hi), ALU.subtract), a, name="Vone%d" % g)

        prepare = [(16, take), (18, lambda: turn(0)), (19, lambda: turn(1)), (21, lambda: rope(0)), (22, lambda: rope(1)), (24, lambda: rope_end(0)), (25, lambda: rope_end(1)),
                   (28, lambda: to_stack(0, 0)), (31, lambda: to_stack(0, 1)), *((T_ + 2, lambda n=n, g=g: to_stack_low(n, g)) for T_, n, g in ((28, 0, 0), (31, 0, 1), (34, 1, 0), (37, 1, 1))), (33, lambda: hop_out(0)), (34, lambda: to_stack(1, 0)), (37, lambda: to_stack(1, 1)), (39, lambda: hop_out(1)),
                   *((40 + 2 * t, lambda t=t: v_in(t)) for t in range(TB)),
                   (47, lambda: stack_in(0)), (STEPS + LAGS[1], lambda: stack_in(1)),
                   *((max(48 + g, (g + 1) * HG * TB + LAGS[2]), lambda g=g: v_place(g)) for g in range(H1 // HG))]
        for T_, f in sorted(prepare, key=lambda e: e[0]):
            f()

        def maxima_r(h, j):
            return [(rows_q[:, h, j * P:(j + 1) * P], rows_k[:, h, :])], at("rows_in%d" % (h // 8))

        def row_r(h):
            return rows_q[MAX_ROW:MAX_ROW + 1, h, :]

        def scores_r(h, kt):
            return [(rows_k[:, h, kt * P:(kt + 1) * P], rows_q[:, h, :])]

        def values_r(h, kt):
            g, k = divmod(h, HG)
            return Vone[:, kt, h, :], OUT_BANKS[g % 2], k == 0 and kt == 0, k == HG - 1 and kt == TB - 1, at("Vone%d" % g)

        def after_r(h, m):
            g, k = divmod(h, HG)
            if k == HG - 1:
                bk = OUT_BANKS[g % 2]
                q.op("act", lambda i: A.activation(gathered_o[g % 2], bank[bk], ACT.Copy), m, at("gathered_read%d" % (g % 2)), name="bank%d" % bk)
                q.names["gathered_o%d" % g] = q.names["bank%d" % bk]

        def over_sums(g):
            for t in range(TB):
                m = q.op("pe", lambda i, t=t: PE.transpose(bank[SPARE_BANK][:, t * P:(t + 1) * P], gathered_o[g % 2][:, t * P:(t + 1) * P], ident), at("gathered_o%d" % g), bank_free(SPARE_BANK), inc=t == TB - 1,
                         name="gathered_read%d" % (g % 2))
            o = bank[SPARE_BANK].rearrange("p (t k x) -> p t k x", t=TB, k=HG)
            cols = att[:, :, g * HG * HD:(g + 1) * HG * HD].rearrange("p t (k f) -> p t k f", k=HG)
            r = q.op("dve", lambda i: V.reciprocal(sums, o[:, :, :, ONE]), m, at("att"))
            m = q.op("dve", lambda i: V.tensor_copy(cols, o[:, :, :, LO:LO + HD]), m, at("att_T"))
            m = q.op("dve", lambda i: V.tensor_tensor(cols, o[:, :, :, 0:HD], cols, ALU.add), m, name="bank%d" % SPARE_BANK)
            q.op("dve", lambda i: V.tensor_tensor(cols, cols, bass.AP(sums.tensor, sums.offset, [*sums.ap, [0, HD]]), ALU.mult), r, m, name="att")

        def att_turn(c):
            for t in range(TB):
                m = q.op("pe", lambda i, c=c, t=t: PE.transpose(bank[SPARE_BANK][:, t * P:(t + 1) * P], att[:, t, c * P:(c + 1) * P], ident),
                         at("att"), bank_free(SPARE_BANK), inc=t == TB - 1, name="att_T")
            q.op("act", lambda i: A.activation(attT[:, c, :], bank[SPARE_BANK], ACT.Copy), m, at("att_read"), at("turned_read%d" % c), name="bank%d" % SPARE_BANK)
            q.names["attT%d" % c] = q.names["bank%d" % SPARE_BANK]

        def outs(tiles):
            out_products(attT, Wo, [at("attT0"), at("attT1")], tiles, range(DC), "att_read")

        finish_r = [*((((g + 1) * HG * TB + LAGS[2] + 2), lambda g=g: over_sums(g)) for g in range(H1 // HG)),
                    (DONE + 4, lambda: att_turn(0)), (DONE + 5, lambda: att_turn(1)), *((DONE + 3 + t, lambda t=t: out_base(t, bo, rows_before)) for t in range(TB)),
                    (DONE + 7, lambda: outs((0, 1))), (DONE + 8, lambda: out_sum(0)), (DONE + 8, lambda: out_sum(1)), (DONE + 8, lambda: outs((2, 3))),
                    (DONE + 9, lambda: out_sum(2)), (DONE + 9, lambda: out_sum(3)), *norm_events(DONE + 10)]
        events = [(T_, True, f) for T_, f in prepare] + [(T_, False, f) for T_, f in finish_r]
        buf.open_sum(values_r)
        q.barrier()
        attend_heads(buf, maxima_r, row_r, scores_r, values_r, after_r, events)
        q.flush(B)
        q.barrier()
        attend_heads(buf, maxima_r, row_r, scores_r, values_r, after_r, events, loop=False)
        q.flush()
        q.barrier()

    with ExitStack() as ph:
        HD, N, NG = 64, 512, H1 // 2
        SLOTS = 4

        buf = HeadBuffers(ph, 4)
        Wq, Wk, Wv = (parts("W" + n, [P, DC, H1 * HD], ph) for n in "qkv")
        Wo = sb("Wo", [P, NG, D], where=ph)
        bo = sb("bo", [P, D], where=ph)
        srcp = parts("srcp", [P, DC, S], ph)
        ctxp = parts("ctxp", [P, DC, S], ph)
        ctxT = xT
        qs = [sb("qs%d" % k, [P, S], f32r, where=ph) for k in range(SLOTS)]
        ks = [sb("ks%d" % k, [P, S], f32r, where=ph) for k in range(SLOTS)]
        q2 = [sb("q2_%d" % k, [ROWS, S], f32r, where=ph) for k in range(SLOTS)]
        k2 = [sb("k2_%d" % k, [ROWS, S], f32r, where=ph) for k in range(SLOTS)]
        Vone = sb("Vone", [P, TB, NG, 3 * HD], where=ph)
        attT = sb("attT", [P, NG, S], where=ph)
        sums, rinv = (sb(n, [P, S], where=ph) for n in ("sums", "rinv"))
        for dst, src in ((Wo, T["Wo2"]), (bo, bass.AP(T["bo2"].tensor, 0, [[0, P], [1, D]]))):
            w_in = q.dma("act", "d_w0", lambda i, dst=dst, src=src: A.dma_start(dst, src))
        z = None
        for k in range(SLOTS):
            for t in (q2, k2):
                z = q.op("pool", lambda i, t=t, k=k: G.memset(f32_of(t[k][MAX_ROW:ROWS]), 0.0), z)
            z = q.op("pool", lambda i, k=k: G.memset(f32_of(k2[k][MAX_ROW:MAX_ROW + 1]), 1.0), z)
        q.op("dve", lambda i: V.memset(Vone, 1.0))
        for k in (2, 3):
            for ap in (qs[k], ks[k], q2[k][0:MAX_ROW], k2[k][0:MAX_ROW]):
                q.op("dve", lambda i, ap=ap: V.memset(f32_of(ap), 0.0))
        stage = attT.rearrange("p g s -> p (g s)").rearrange("p (k c n) -> p k c n", k=2, c=DC)
        w_done = []
        for k, (t, n) in enumerate(((Wq, "Wq2"), (Wk, "Wk2"), (Wv, "Wv2"))):
            w_done.append(weights_in(t, stage[:, k % 2], T[n], w_done[0] if k == 2 else None, k % 2))
        q.barrier()

        prep = {}

        def ctx_of_next(i):
            return (T["ctxT"][bass.ds(i + 1, 1)] if i is not None else T["ctxT"][0:1]).rearrange("a p c s -> p (a c) s")

        def fetch():
            prep["xs"] = q.op("dve", lambda i: V.tensor_copy(xs, rows_of_next(i)), prev("xs_read"))
            prep["ctx"] = q.dma("sp", "d_ctx", lambda i: SP.dma_start(ctxT, ctx_of_next(i)), prev("ctx_read"))

        def ctx_in():
            prep["k"] = split(ctxp, ctxT, prep["ctx"], free=[q.names.get("ctxp_read")], name="ctx_read")

        def turn(c):
            for t in range(TB):
                m = q.op("pe", lambda i, c=c, t=t: PE.transpose(bank[SPARE_BANK][:, t * P:(t + 1) * P], xs[:, t, c * P:(c + 1) * P], ident),
                         prep["xs"], bank_free(SPARE_BANK), inc=t == TB - 1, name="xs_read")
            prep["q", c] = split(cut(srcp, slice(None), c), bank[SPARE_BANK], m, free=[q.names.get("srcp_read")], name="bank%d" % SPARE_BANK)

        def pair_product(g, of):
            if of == "q":
                w, src, bk, r = Wq, srcp, SPARE_BANK, [prep.get(("q", 0)), prep.get(("q", 1))]
            else:
                w, src, bk, r = Wk, ctxp, ROW_BANK, prep.get("k")
            prep[of, "ps"] = product(bank[bk], [(cut(w, slice(None), c, slice(g * P, (g + 1) * P)), cut(src, slice(None), c)) for c in range(DC)],
                                     r, bank_free(bk), name={"q": "srcp_read", "k": "ctxp_read"}[of])

        def head_in(h, of):
            z, m = h % SLOTS, prep[of, "ps"]
            ps = bank[SPARE_BANK if of == "q" else ROW_BANK][(h % 2) * HD:(h % 2 + 1) * HD]
            f = at("second%d" % ((h - SLOTS) % H1))
            if of == "q":
                a = q.op("act", lambda i: A.activation(qs[z][0:HD], ps, ACT.Copy, scale=HD ** -0.5), m, f)
                b = q.op("pool", lambda i: G.tensor_copy(q2[z][0:HD], f32_of(qs[z][0:HD])), a, f, plain=True)
                c = q.op("dve", lambda i: V.scalar_tensor_tensor(qs[z][HD:2 * HD], ps, HD ** -0.5, f32_of(qs[z][0:HD]), ALU.mult, ALU.subtract), a, name="bank%d" % SPARE_BANK)
            else:
                a = q.op("act", lambda i: A.activation(ks[z][0:HD], ps, ACT.Copy), m, f)
                b = q.op("act", lambda i: A.activation(ks[z][HD:2 * HD], f32_of(ks[z][0:HD]), ACT.Copy), a)
                c = q.op("dve", lambda i: V.tensor_tensor(k2[z][0:HD], ps, f32_of(ks[z][0:HD]), ALU.subtract), a, name="bank%d" % ROW_BANK)
            q.names["%s_of%d" % (of, h)] = [a, b, c]

        def v_in(t, n, bk=SPARE_BANK):
            m = product(bank[bk], [(cut(ctxp, slice(None), c, slice(t * P, (t + 1) * P)), cut(Wv, slice(None), c, slice(n * N, (n + 1) * N))) for c in range(DC)],
                        bank_free(bk), name="ctxp_read")
            dst = bass.AP(Vone.tensor, Vone.offset + (t * NG + n * NG // 2) * 3 * HD, [Vone.ap[0], [3 * HD, NG // 2], [2 * HD, 2], [1, HD]])
            src = bank[bk].rearrange("p (g k f) -> p g k f", g=NG // 2, k=2)
            q.op("act", lambda i: A.activation(dst, src, ACT.Copy), m, at("pv%d" % ((n + 1) * STEPS // 2 - 1)), name="bank%d" % bk)
            q.names["V%d_%d" % (n, t)] = q.names["bank%d" % bk]

        prepare = [(48, fetch), (54, ctx_in), (56, lambda: turn(0)), (57, lambda: turn(1))]
        for T_, f in prepare:
            f()
        for of in "qk":
            pair_product(0, of)
            head_in(0, of)
            head_in(1, of)
        q.barrier()
        prep.clear()
        prepare += [(0, lambda: v_in(0, 0)), (0, lambda: v_in(1, 0, ROW_BANK)), (2, lambda: v_in(2, 0)), (2, lambda: v_in(3, 0, ROW_BANK)),
                    (8, lambda: v_in(0, 1)), (9, lambda: v_in(1, 1)), (10, lambda: v_in(2, 1)), (16, lambda: v_in(3, 1))]
        for g in range(NG):
            nxt = (g + 1) % NG
            for T_, fs in ((8 * g + 3, [lambda nxt=nxt: pair_product(nxt, "q"), lambda nxt=nxt: head_in(2 * nxt, "q")]),
                           (8 * g + 5, [lambda nxt=nxt: pair_product(nxt, "k"), lambda nxt=nxt: head_in(2 * nxt, "k")]),
                           (8 * g + 7, [lambda nxt=nxt, of=of: head_in(2 * nxt + 1, of) for of in "qk"])):
                prepare += [(T_, f) for f in fs]

        def operands_of(h):
            return [at("q_of%d" % h), at("k_of%d" % h)]

        def maxima_x(h, j):
            z = h % SLOTS
            return [(qs[z][:, j * P:(j + 1) * P], ks[z])], operands_of(h)

        def row_x(h):
            return q2[h % SLOTS][MAX_ROW:MAX_ROW + 1, :]

        def scores_x(h, kt):
            z = h % SLOTS
            return [(ks[z][:, kt * P:(kt + 1) * P], qs[z]), (k2[z][:, kt * P:(kt + 1) * P], q2[z])]

        def values_x(h, kt):
            return Vone[:, kt, h // 2, (h % 2) * HD:(h % 2) * HD + P], OUT_BANKS[h % 2], kt == 0, kt == TB - 1, at("V%d_%d" % (h // 8, kt))

        def after_x(h, m):
            o, s_ = (slice(0, HD), slice(HD, P)) if h % 2 == 0 else (slice(HD, P), slice(0, HD))
            ps = bank[OUT_BANKS[h % 2]]
            q.op("act", lambda i: A.activation(sums[o], ps[s_], ACT.Copy), m, at("rinv"), name="sums%d" % h)
            q.op("act", lambda i: A.activation(attT[o, h // 2, :], ps[o], ACT.Copy), m, at("att_read%d" % (h // 8)), name="bank%d" % OUT_BANKS[h % 2])
            q.names["raw%d" % h] = q.names["bank%d" % OUT_BANKS[h % 2]]

        def invert(g, t):
            cols = slice(t * P, (t + 1) * P)
            q.op("dve", lambda i: V.reciprocal(rinv[:, cols], sums[:, cols]), at("sums%d" % (2 * g)), at("sums%d" % (2 * g + 1)), at("att%d" % ((g - 1) % NG)), name="rinv")

        def over_sums(g):
            q.op("dve", lambda i: V.tensor_tensor(attT[:, g, :], attT[:, g, :], rinv, ALU.mult), at("rinv"), at("raw%d" % (2 * g)), at("raw%d" % (2 * g + 1)), name="att%d" % g)

        def outs(tiles, n):
            out_products(attT, Wo, [at("att%d" % g) for g in range(NG // 2 * n, NG // 2 * (n + 1))], tiles, range(NG // 2 * n, NG // 2 * (n + 1)), "att_read%d" % n)

        def out_steps(T_, n):
            return [(T_, lambda: outs((0, 1), n)), (T_ + 1, lambda: out_sum(0)), (T_ + 1, lambda: out_sum(1)), (T_ + 1, lambda: outs((2, 3), n)),
                    (T_ + 2, lambda: out_sum(2)), (T_ + 2, lambda: out_sum(3))]

        finish_x = [*((2 * TB * (g + 1) - 1 + LAGS[2] + t, lambda g=g, t=t: invert(g, t)) for g in range(NG) for t in range(TB)),
                    *((2 * TB * (g + 1) - 1 + LAGS[2] + TB, lambda g=g: over_sums(g)) for g in range(NG)),
                    *((44 + t, lambda t=t: out_base(t, bo, to_X)) for t in range(TB)),
                    *out_steps(48, 0), *out_steps(DONE + 8, 1), *norm_events(DONE + 11)]
        events = [(T_, True, f) for T_, f in prepare] + [(T_, False, f) for T_, f in finish_x]
        for ap in (attT, summed):
            q.op("dve", lambda i, ap=ap: V.memset(ap, 0.0))
        for ap in (sums, rinv):
            q.op("dve", lambda i, ap=ap: V.memset(ap, 1.0))
        q.barrier()
        buf.open_sum(values_x)
        q.barrier()
        attend_heads(buf, maxima_x, row_x, scores_x, values_x, after_x, events)
        q.flush(B)
        q.barrier()
        attend_heads(buf, maxima_x, row_x, scores_x, values_x, after_x, events, loop=False)
        q.flush()
        q.barrier()

    with ExitStack() as ph:
        gidx_all = sb("gidx_all", [P, (E1 + 2) * CT1], i32, where=ph)
        sidx_all = sb("sidx_all", [P, E1 * CT1], i32, where=ph)
        slot_w = sb("slot_w", [P, E1 * CT1], where=ph)
        with ExitStack() as route:
            TE = [P, NT, E1]
            gw = sb("gw", [P, DC, E1], where=route)
            L = sb("L", TE, where=route)
            shifted = sb("shifted", TE, where=route)
            left = sb("left", TE, where=route)
            chosen = sb("chosen", TE, where=route)
            weight = sb("weight", TE, where=route)
            top = sb("top", [P, NT, 8], where=route)
            cols = sb("cols", [P, 3, NT], where=route)
            marks16 = sb("marks16", TE, bf16, where=route)
            before16 = sb("before16", TE, bf16, where=route)
            tri = sb("tri", [P, 2, P], bf16, where=route)
            keep = sb("keep", TE, where=route)
            place = sb("place", TE, i32, where=route)
            hi_i = sb("hi_i", TE, i32, where=route)
            lo_i = sb("lo_i", TE, i32, where=route)
            hi = sb("hi", TE, where=route)
            lo = sb("lo", TE, where=route)
            ramp = sb("ramp", [P, 32], where=route)
            token1 = sb("token1", [P, NT], where=route)
            A_ = [sb("A%d" % b, [P, NT, 8, 16], where=route) for b in range(2)]
            B_ = [sb("B%d" % b, [P, NT, 8, 16], where=route) for b in range(2)]
            BV = [sb("BV%d" % b, [P, NT, 2, 128], where=route) for b in range(2)]
            diag = sb("diag", [P, 8], where=route)
            cross = sb("cross", [P, 2, 8, 16], where=route)
            slots = sb("slots", [P, 4, 2, 16], where=route)
            slot_rows = sb("slot_rows", [E1 * CT1, 2, P], where=route)
            slot_n = sb("slot_n", [P, 2, E1 * CT1], where=route)
            for dst, n in ((gw, "gw"), (tri, "tri"), (ramp, "ramp"), (token1, "token1"), (diag, "diag")):
                w_in = q.dma("act", "d_w0", lambda i, dst=dst, n=n: A.dma_start(dst, T[n]))
            acc_in = q.dma("pool", "d_sc0", lambda i: G.dma_start(acc_d.rearrange("(t p) d -> p t d", p=P), X))
            rows_in = q.dma("pool", "d_sc1", lambda i: G.dma_start(rows_d.rearrange("(t p) d -> p t d", p=P)[:, :, 0:D], X))
            q.flush()
            take_batch()
            x_ready = [q.names["xT0"], q.names["xT1"]]
            for t in range(TB):
                for c in range(DC):
                    m = q.op("pe", lambda i, t=t, c=c: PE.matmul(bank[2][:, t * E1:(t + 1) * E1], xT[:, c, t * P:(t + 1) * P], gw[:, c, :], start=c == 0, stop=c == DC - 1),
                             x_ready, w_in, prev("logits"), name="xT_read")
            q.op("dve", lambda i: V.tensor_copy(L[:, bass.ds(i * TB, TB), :].rearrange("p t e -> p (t e)"), bank[2][:, 0:TB * E1]), m, name="logits")
            q.flush(B)
            q.barrier()

            def every(ap, n):
                return bass.AP(ap.tensor, ap.offset, [*ap.ap, [0, n]])

            m = q.op("dve", lambda i: V.tensor_reduce(cols[:, 0, :], L, AX.X, ALU.max))
            m = q.op("dve", lambda i: V.tensor_tensor(shifted, L, every(cols[:, 0, :], E1), ALU.subtract), m)
            m_exp = q.op("act", lambda i: A.activation(shifted, shifted, ACT.Exp), m)
            for t in range(NT):
                m = q.op("dve", lambda i, t=t: V.max(top[:, t, :], L[:, t, :]))
            for t in range(NT):
                m2 = q.op("dve", lambda i, t=t: V.match_replace(left[:, t, :], top[:, t, :], L[:, t, :], -3e38), m)
            m = q.op("dve", lambda i: V.tensor_tensor(chosen, left, L, ALU.not_equal), m2)
            c16 = q.op("act", lambda i: A.activation(marks16, chosen, ACT.Copy), m)
            w = q.op("dve", lambda i: V.tensor_tensor(weight, shifted, chosen, ALU.mult), m, m_exp)
            w = q.op("dve", lambda i: V.tensor_reduce(cols[:, 1, :], weight, AX.X, ALU.add), w)
            w = q.op("dve", lambda i: V.reciprocal(cols[:, 2, :], cols[:, 1, :]), w)
            w = q.op("dve", lambda i: V.tensor_tensor(weight, weight, every(cols[:, 2, :], E1), ALU.mult), w)
            r = q.op("pool", lambda i: G.memset(before16[:, 0, :], 0.0))
            for t in range(1, NT):
                r = q.op("pool", lambda i, t=t: G.tensor_tensor(before16[:, t, :], before16[:, t - 1, :], marks16[:, t - 1, :], ALU.add), r, c16)
            for t in range(NT):
                q.op("pe", lambda i, t=t: PE.matmul(bank[0][:, t * E1:(t + 1) * E1], tri[:, 0, :], marks16[:, t, :], start=True, stop=False), c16, w_in, inc=False)
                n = q.op("pe", lambda i, t=t: PE.matmul(bank[0][:, t * E1:(t + 1) * E1], tri[:, 1, :], before16[:, t, :], start=False, stop=True), r)
            upto = bank[0].rearrange("p (t e) -> p t e", e=E1)
            k = q.op("dve", lambda i: V.scalar_tensor_tensor(keep, upto, float(CAP), chosen, ALU.is_le, ALU.mult), n, m)
            n = q.op("dve", lambda i: V.tensor_scalar(place, upto, -1.0, None, ALU.add), n)
            a = q.op("dve", lambda i: V.tensor_scalar(hi_i, place, 4, None, ALU.arith_shift_right), n)
            b = q.op("dve", lambda i: V.tensor_scalar(lo_i, place, 15, None, ALU.bitwise_and), n)
            a = q.op("dve", lambda i: V.tensor_copy(hi, hi_i), a)
            b = q.op("dve", lambda i: V.tensor_copy(lo, lo_i), b)
            a = q.op("dve", lambda i: V.scalar_tensor_tensor(hi, hi, 1.0, keep, ALU.add, ALU.mult), a, k)
            read, free = {}, {}
            for g in range(4):
                e8 = slice(g * 8, g * 8 + 8)
                z = g % 2

                def along(ap):
                    return bass.AP(ap.tensor, ap.offset, [ap.ap[0], [0, NT], [0, 8], [1, 16]])

                def per_tile(ap):
                    return bass.AP(ap.tensor, ap.offset, [*ap.ap, [0, 8], [0, 16]])

                def value(v, z=z):
                    ap = BV[z][:, :, v, :]
                    return ap.rearrange("p t (e j) -> p t e j", j=16)

                qa = q.op("dve", lambda i, e8=e8, z=z: V.tensor_tensor(A_[z], every(hi[:, :, e8], 16), along(ramp[:, 0:16]), ALU.is_equal), a, read.get(g - 2), w_in)
                qb = q.op("dve", lambda i, e8=e8, z=z: V.tensor_tensor(B_[z], every(lo[:, :, e8], 16), along(ramp[:, 16:32]), ALU.is_equal), b, free.get(g - 2), w_in)
                qc = q.op("pool", lambda i, z=z, value=value: G.tensor_tensor(value(0), B_[z], per_tile(token1), ALU.mult), qb, read.get(g - 2))
                qd = q.op("dve", lambda i, e8=e8, z=z, value=value: V.tensor_tensor(value(1), B_[z], every(weight[:, :, e8], 16), ALU.mult), qb, w, read.get(g - 2))
                free[g] = [qc, qd]
                for t in range(NT):
                    n = q.op("pe", lambda i, t=t, z=z: PE.matmul(bank[1 + z][:, 0:256], A_[z][:, t, :, :].rearrange("p e j -> p (e j)"), BV[z][:, t, :, :].rearrange("p v j -> p (v j)"),
                                                               start=t == 0, stop=t == NT - 1), qa, qc, qd, free.get(("bank", z)), inc=t == NT - 1)
                read[g] = n

                def agree(g=g, z=z, n=n):
                    ps = bank[1 + z][:, 0:256].rearrange("p (v x) -> p v x", v=2).rearrange("p v (e j) -> p v e j", j=16)
                    on = bass.AP(diag.tensor, diag.offset, [diag.ap[0], [0, 2], [1, 8], [0, 16]])
                    n = q.op("dve", lambda i, ps=ps, on=on: V.tensor_tensor(cross, ps, on, ALU.mult), n, free.get("cross"))
                    free["bank", z] = n
                    n = q.op("dve", lambda i, g=g: V.tensor_reduce(slots[:, g, :, :], cross.rearrange("p v e j -> p v j e"), AX.X, ALU.add), n)
                    free["cross"] = n
                    for v in range(2):
                        d = q.dma("sp", "d_slot", lambda i, g=g, v=v: SP.dma_start(slot_d[v, g * 2048:(g + 1) * 2048].rearrange("(p j) -> p j", j=16), slots[:, g, v, :]), n)
                    return d

                if g:
                    waiting()
                waiting = agree
            d = waiting()
            d = q.dma("sp", "d_slot", lambda i: SP.dma_start(slot_rows, slot_d.rearrange("v (r c) -> r v c", c=P)), d)
            for v in range(2):
                n = q.op("pe", lambda i, v=v: PE.transpose(bank[3][:, v * 64:(v + 1) * 64], slot_rows[:, v, :], ident[0:64, 0:64]), d)
            n = q.op("dve", lambda i: V.tensor_copy(slot_n.rearrange("p v r -> p (v r)"), bank[3][:, 0:128]), n)
            kept = q.op("dve", lambda i: V.tensor_copy(slot_w, slot_n[:, 1, :]), n)
            q.op("dve", lambda i: V.tensor_scalar(gidx_all[:, 0:E1 * CT1], slot_n[:, 0, :], -1.0, 0.0, ALU.add, ALU.max), n)
            m = q.op("dve", lambda i: V.tensor_scalar(slot_n[:, 1, :], slot_n[:, 0, :], 0.5, float(1 << 16), ALU.is_lt, ALU.mult), kept)
            q.op("dve", lambda i: V.scalar_tensor_tensor(sidx_all, slot_n[:, 0, :], -1.0, slot_n[:, 1, :], ALU.add, ALU.add), m)
            q.op("dve", lambda i: V.memset(gidx_all[:, E1 * CT1:], 0))
            q.barrier()

        Wgu = [sb("Wgu%d" % b, [P, DC, 2 * F1], where=ph) for b in range(2)]
        Wdn = [sb("Wdn%d" % b, [FH, 2, D], where=ph) for b in range(2)]
        gidx = [sb("gidx%d" % b, [P, CT1], i32, where=ph) for b in range(2)]
        sidx1 = [sb("sidx1_%d" % b, [P, CT1], i32, where=ph) for b in range(2)]
        rows1 = [sb("rows1_%d" % b, [P, CT1, GW], where=ph) for b in range(2)]
        RT = [sb("RT%d" % b, [P, DC, CAP], where=ph) for b in range(2)]
        act1 = [sb("act1_%d" % b, [FH, 2, CAP], where=ph) for b in range(2)]
        h1 = [sb("h1_%d" % b, [FH, 2, CAP], where=ph) for b in range(2)]
        res = [sb("res%d" % b, [P, CT1, D], where=ph) for b in range(2)]

        def gather1(i, b, rows_free):
            m = q.op("pool", lambda _, b=b, i=i: G.tensor_copy(gidx[b], gidx_all[:, i(_, b)]), rows_free, q.names.get("gathered%d" % b))
            for t in range(CT1):
                q.dma("pool", "d_g%d" % b, lambda _, b=b, t=t: G.indirect_dma_start(rows1[b][:, t, :], None, rows_d, bass.IndirectOffsetOnAxis(ap=gidx[b][:, t:t + 1], axis=0)),
                      m, rows_free, name="gathered%d" % b)

        for b in range(2):
            gather1(lambda _, b: slice(b * CT1, (b + 1) * CT1), b, None)
        q.flush()
        for b in range(2):
            w = q.dma("sp", "d_e%d" % b, lambda i, b=b: SP.dma_start(Wgu[b], T["Wgu"][bass.ds(2 * i + b, 1)].rearrange("a p c f -> p (a c) f")), prev("W_read%d" % b))
            w = q.dma("sp", "d_e%d" % b, lambda i, b=b: SP.dma_start(Wdn[b], T["Wdn"][bass.ds(2 * i + b, 1)].rearrange("a p c f -> p (a c) f")), prev("W_read%d" % b))
        def turn_rows(b):
            for c in range(DC):
                for t in range(CT1):
                    m = q.op("pe", lambda i, b=b, t=t, c=c: PE.transpose(bank[b][:, c * CAP + t * P:c * CAP + (t + 1) * P], rows1[b][:, t, c * P:(c + 1) * P], ident),
                             prev("gathered%d" % b), prev("RT%d" % b), inc=t == CT1 - 1)
            gather1(lambda i, b: bass.ds((2 * i + b + 2) * CT1, CT1), b, m)
            q.op("act", lambda i: A.activation(RT[b].rearrange("p c s -> p (c s)"), bank[b], ACT.Copy), m, prev("RT_read%d" % b), name="RT%d" % b)

        def hidden(b):
            for half in range(2):
                for f in range(2):
                    for c in range(DC):
                        m = q.op("pe", lambda i, half=half, f=f, c=c: PE.matmul(bank[2 + 2 * b + half][0:FH, f * CAP:(f + 1) * CAP],
                                                                        Wgu[b][:, c, half * F1 + f * FH:half * F1 + (f + 1) * FH], RT[b][:, c, :], start=c == 0, stop=c == DC - 1),
                                 w_of[b], q.names["RT%d" % b], prev("act1_%d" % b) if half == 0 else prev("h1_%d" % b), inc=c == DC - 1, name="RT_read%d" % b)
                if half == 0:
                    s_ = q.op("act", lambda i: A.activation(act1[b].rearrange("p c s -> p (c s)"), bank[2 + 2 * b][0:FH, :], ACT.Silu), m, prev("h1_%d" % b), name="act1_%d" % b)
            q.op("dve", lambda i: V.tensor_tensor(h1[b].rearrange("p c s -> p (c s)"), bank[3 + 2 * b][0:FH, :], act1[b].rearrange("p c s -> p (c s)"), ALU.mult), m, s_, prev("h_read%d" % b), name="h1_%d" % b)

        def down(b):
            for t in range(CT1):
                for f in range(2):
                    m = q.op("pe", lambda i, t=t, f=f: PE.matmul(bank[6 + b][:, t * D:(t + 1) * D], h1[b][:, f, t * P:(t + 1) * P], Wdn[b][:, f, :], start=f == 0, stop=f == 1),
                             q.names["h1_%d" % b], w_of[b], prev("res%d" % b), inc=f == 1, name="h_read%d" % b)
            q.names["W_read%d" % b] = m
            c_ = q.op("pool", lambda i: G.tensor_copy(sidx1[b], sidx_all[:, bass.ds((2 * i + b) * CT1, CT1)]), prev("stored%d" % b))
            for t in range(CT1):
                r = q.op("dve", lambda i, t=t: V.tensor_scalar(res[b][:, t, :], bank[6 + b][:, t * D:(t + 1) * D], slot_w[:, bass.ds((2 * i + b) * CT1 + t, 1)], None, ALU.mult),
                         m, prev("stored%d" % b), name="res%d" % b)
            last = q.names["stored0"] if b else prev("stored1")
            for t in range(CT1):
                q.dma("pool", "d_sc%d" % b, lambda i, t=t: G.indirect_dma_start(acc_d, bass.IndirectOffsetOnAxis(ap=sidx1[b][:, t:t + 1], axis=0), res[b][:, t, :], None,
                                                                            compute_op=ALU.add, bounds_check=B * S - 1, oob_is_err=False),
                      r, c_, last, name="stored%d" % b)

        w_of = [Mark("d_e%d" % b, q.count["d_e%d" % b], q.section) for b in range(2)]
        for stage_of in (turn_rows, hidden, down):
            for b in range(2):
                stage_of(b)
        q.flush(E1 // 2)
        q.barrier()
    norm_from_acc(out)


def constants():
    k = np.abs(np.fft.fftfreq(D)).astype(np.float32) + np.float32(1e-8)
    n = np.arange(D)
    rows, freq = [], []
    for j in range(D // 2 + 1):
        w = np.sqrt((1.0 if j in (0, D // 2) else 2.0) / D)
        rows.append(w * np.cos(2 * np.pi * ((j * n) % D) / D)); freq.append(j)
        if j not in (0, D // 2):
            rows.append(w * np.sin(2 * np.pi * ((j * n) % D) / D)); freq.append(j)
    basis = np.array(rows, np.float32)
    ka = k[np.array(freq)]
    kc = ka.reshape(DC, P).T
    kcols = np.concatenate([kc, kc * kc], 1)
    lx = np.log(np.array(FRACTAL, np.float64))
    den = 5 * np.sum(lx * lx) - np.sum(lx) ** 2
    weights = -(5 * lx - np.sum(lx)) / den
    sizes = np.array([s * s for s in FRACTAL])
    fmask = (np.arange(1024)[None, :] < sizes[:, None]).astype(np.float32)
    fconst = np.concatenate([np.repeat(weights[:, None], P, 1), 1.0 / sizes[:, None]], 1).astype(np.float32)
    A12 = np.array([[1, 1, 1, 0, 1, 1, 1, 0, 0, 0, 1, 1], [1, 1, 0, 1, 1, 1, 0, 0, 0, 1, 1, 0], [1, 0, 1, 1, 1, 0, 0, 0, 1, 1, 0, 1],
                    [0, 1, 1, 1, 0, 0, 0, 1, 1, 0, 1, 1], [0, 0, 0, 0, 1, 1, 1, 1, 1, 1, 1, 1], [1, 1, 1, 1, 0, 0, 0, 0, 0, 0, 0, 0],
                    [0, 0, 0, 0, 1, 1, 1, 1, 0, 0, 0, 0], [1, 1, 0, 0, 1, 1, 0, 0, 1, 1, 0, 0], [1, 0, 1, 0, 1, 0, 1, 0, 1, 0, 1, 0],
                    [0, 1, 0, 1, 0, 1, 0, 1, 0, 1, 0, 1], [1, 0, 0, 1, 1, 0, 0, 1, 1, 0, 0, 1], [0, 1, 1, 0, 0, 1, 1, 0, 0, 1, 1, 0]], np.float32)
    Hm = np.concatenate([A12.T, np.eye(12, dtype=np.float32)], axis=1)
    golay = np.zeros((24, 48), np.float32)
    golay[:, 0:12] = Hm.T
    golay[0:12, 24:48] = 1.0
    sel = np.zeros((2, 10), np.float32)
    sel[0, 0:5] = 1.0
    sel[1, 5:10] = 1.0
    lower = np.tril(np.ones((P, P), np.float32), -1)
    freq = np.exp(np.arange(0, D, 2, dtype=np.float32) * np.float32(-np.log(10000.0) / D))
    ang = (np.arange(S, dtype=np.float32)[:, None] * freq[None, :]).astype(np.float32)
    cs = np.stack([np.cos(ang).T, np.sin(ang).T], 1).astype(np.float32)
    tri = np.stack([np.triu(np.ones((P, P))), np.ones((P, P))], 1).astype(mybir.dt.np(bf16))
    ramp = np.concatenate([np.arange(1, 17), np.arange(16)]).astype(np.float32)[None].repeat(P, 0)
    token1 = (np.arange(P)[:, None] + P * np.arange(NT)[None, :] + 1).astype(np.float32)
    diag = (np.arange(P)[:, None] // 16 == np.arange(8)[None, :]).astype(np.float32)
    return {"zeros": np.zeros((1, H1 // 2, S), np.float32), "tri": tri, "ramp": ramp, "token1": token1, "diag": diag, "lower": lower, "cs": cs, "ident": np.eye(P, dtype=np.float32), "basis": basis.reshape(DC, P, D).transpose(1, 0, 2), "kcols": kcols.astype(np.float32),
            "fmask": fmask, "fconst": fconst, "golay": golay, "sel": sel}


def chunks(w):
    return w.reshape(w.shape[0] // P, P, *w.shape[1:]).swapaxes(0, 1)


def layout(x, **w):
    a = constants()
    a["x"] = x.reshape(B * S, D)
    a["W_el"] = chunks(w["L0_attn_W_el"])
    a["W_le"] = np.concatenate([w["L0_attn_W_le"], w["L0_attn_b_le"][None]], 0)
    a["b_el"] = w["L0_attn_b_el"][:, None]
    g = "L0_xattn_"
    for n in ("Wq_c", "Wk_s", "Wv_s", "Wq_s", "Wk_c", "Wv_c", "Wg"):
        a[n] = chunks(w[g + n].T)
    a["bias0"] = np.stack([w[g + n].reshape(DC, P).T for n in ("bq_c", "bk_s", "bv_s", "bq_s", "bk_c", "bv_c", "bg")], 1)
    a["ctxT"] = np.concatenate([w["ctx_1024"].reshape(B, S, DC, P).transpose(0, 3, 2, 1), np.zeros((1, P, DC, S), np.float32)], 0)
    g = "L0_ffn_"
    a["W1"] = w[g + "W1"].reshape(E0, DC, P, F0).transpose(0, 2, 1, 3)
    a["W2"] = w[g + "W2"].reshape(E0, FC0, P, D).transpose(0, 2, 1, 3)
    a["b1"] = w[g + "b1"].reshape(E0 * FC0, P).T
    a["b2"] = w[g + "b2"]
    tok = w[g + "top_idx"].T
    a["tok"] = tok
    a["idx"] = tok.reshape(E0 * CT0, P).T
    a["combine"] = w[g + "combine_weights"]
    g = "L1_attn_"
    for n in ("Wq", "Wk", "Wv", "Wo"):
        a[n + "1"] = chunks(w[g + n].T)
    a["bqkv"] = np.stack([w[g + n].reshape(DC, P).T for n in ("bq", "bk", "bv")], 1)
    a["bv1"] = w[g + "bv"][None]
    a["bo1"] = w[g + "bo"][None]
    g = "L1_xattn_"
    for n in ("Wq", "Wk", "Wv", "Wo"):
        a[n + "2"] = chunks(w[g + n])
    a["bo2"] = w[g + "bo"][None]
    g = "L1_ffn_"
    a["gw"] = chunks(w[g + "gate_weight"].T)
    a["Wgu"] = w[g + "gate_up_proj"].reshape(E1, 2 * F1, DC, P).transpose(0, 3, 2, 1)
    a["Wdn"] = w[g + "down_proj"].reshape(E1, D, 2, FH).transpose(0, 3, 2, 1)
    return {k: np.ascontiguousarray(v) for k, v in a.items()}


def kernel(**inputs):
    from concourse import bacc
    from concourse.bass_utils import run_bass_kernel_spmd

    arrays = layout(**{k: np.asarray(v) for k, v in inputs.items()})
    nc = bacc.Bacc("TRN2", target_bir_lowering=False, num_devices=1)
    T = {k: nc.dram_tensor("in_" + k, v.shape, mybir.dt.from_np(v.dtype), kind="ExternalInput").ap() for k, v in arrays.items()}
    out = nc.dram_tensor("out_0", (B * S, D), f32, kind="ExternalOutput").ap()
    program(nc, T, out)
    r = run_bass_kernel_spmd(nc, [{"in_" + k: v for k, v in arrays.items()}], core_ids=[0])
    return r.results[0]["out_0"].reshape(B, S, D)
```
